# Optimizing a Trainium2 kernel written in Bass

```python
import numpy as np
import jax
import jax.numpy as jnp

def _softmax(x, axis=-1):
    return jax.nn.softmax(x, axis=axis)

def _gelu(x):
    return jax.nn.gelu(x, approximate=True)

def _silu(x):
    return jax.nn.silu(x)

def _sigmoid(x):
    return jax.nn.sigmoid(x)

def _layernorm(x, axis=-1, eps=1e-05):
    m = jnp.mean(x, axis=axis, keepdims=True)
    v = jnp.var(x, axis=axis, keepdims=True)
    return (x - m) / jnp.sqrt(v + eps)

def _scatter_add(tgt, idx, src, axis=0):
    return tgt.at[idx].add(src)

def _segment_sum(src, seg, n):
    return jax.ops.segment_sum(src, seg, n)
kernel_name = 'mk_perceiver_d1_seqx_r4_c18f9a'

def setup_inputs(seed: int=0):
    np.random.seed(seed)
    _w = jnp.asarray

    def _rec_inputs():
        import jax
        import jax.numpy as jnp
        _rk = jax.random.key(seed)
        x = -0.0002928 + 1 * jax.random.normal(jax.random.fold_in(_rk, 1), (32, 64, 256), jnp.float32)
        _lenS = 64 - jax.random.randint(jax.random.fold_in(_rk, 7), (32,), 0, max(1, 64 // 4) + 1, jnp.int32)
        _lenS2 = 1601 - jax.random.randint(jax.random.fold_in(_rk, 8), (32,), 0, max(1, 1601 // 4) + 1, jnp.int32)
        _ctx_1024P = jax.random.normal(jax.random.fold_in(_rk, 11), (32, 16, 256), jnp.float32)
        _ctx_1024c = jax.random.dirichlet(jax.random.fold_in(_rk, 511), 0.3 * jnp.ones((16,), jnp.float32), (32, 1601))
        _ctx_1024t = jnp.einsum('bsk,bkd->bsd', _ctx_1024c, _ctx_1024P)
        _ctx_1024t = _ctx_1024t * jax.lax.rsqrt(jnp.mean(jnp.square(_ctx_1024t)) + 1e-12) * 0.953939
        ctx_1024 = -1.39393e-06 + 0.999914 * (_ctx_1024t + 0.3 * jax.random.normal(jax.random.fold_in(_rk, 611), (32, 1601, 256), jnp.float32))
        return (x, ctx_1024)
    x, ctx_1024 = _rec_inputs()

    def _L0_xattn_setup():
        import jax, jax.numpy as jnp
        import numpy as np
        D_MODEL = 256
        N_HEADS = 16
        D_K = D_MODEL // N_HEADS
        key = jax.random.key(seed)
        ks = jax.random.split(key, 11)
        B, L, S = (2, 512, 512)
        scale = 1.0 / np.sqrt(D_MODEL)
        return {'x_q': jax.random.normal(ks[0], (B, L, D_MODEL), jnp.float32), 'x_k': jax.random.normal(ks[1], (B, S, D_MODEL), jnp.float32), 'x_v': jax.random.normal(ks[2], (B, S, D_MODEL), jnp.float32), 'W_Q': jax.random.normal(ks[3], (D_MODEL, D_MODEL), jnp.float32) * scale, 'b_Q': jax.random.normal(ks[4], (D_MODEL,), jnp.float32) * 0.01, 'W_K': jax.random.normal(ks[5], (D_MODEL, D_MODEL), jnp.float32) * scale, 'b_K': jax.random.normal(ks[6], (D_MODEL,), jnp.float32) * 0.01, 'W_V': jax.random.normal(ks[7], (D_MODEL, D_MODEL), jnp.float32) * scale, 'b_V': jax.random.normal(ks[8], (D_MODEL,), jnp.float32) * 0.01, 'W_O': jax.random.normal(ks[9], (D_MODEL, D_MODEL), jnp.float32) * scale, 'b_O': jax.random.normal(ks[10], (D_MODEL,), jnp.float32) * 0.01}
    _L0_xattn_all = _L0_xattn_setup()
    _L0_xattn_in = {k: v for k, v in _L0_xattn_all.items() if k in ('W_Q', 'b_Q', 'W_K', 'b_K', 'W_V', 'b_V', 'W_O', 'b_O')}
    del _L0_xattn_all

    def _L0_attn_setup():
        import jax, jax.numpy as jnp
        import numpy as np
        D_MODEL, D_STATE, EXPAND = (256, 16, 2)
        D_INNER = D_MODEL * EXPAND
        DT_RANK = int(np.ceil(D_MODEL / 16))
        BATCH, SEQ = (2, 512)

        def _ssm_scan(xs, A, Bs, Cs, delta):
            batch, _, d_inner = xs.shape
            n = A.shape[1]

            def step(h, inp):
                x_t, d_t, B_t, C_t = inp
                dA = jnp.exp(d_t[:, :, None] * A)
                h = dA * h + (d_t * x_t)[:, :, None] * B_t[:, None, :]
                y = jnp.einsum('bdn,bn->bd', h, C_t)
                return (h, y)
            h0 = jnp.zeros((batch, d_inner, n), jnp.float32)
            inps = (xs.transpose(1, 0, 2), delta.transpose(1, 0, 2), Bs.transpose(1, 0, 2), Cs.transpose(1, 0, 2))
            _, ys = jax.lax.scan(step, h0, inps)
            return ys.transpose(1, 0, 2)

        def _reference_tuple_inner(x, Win, bin, Wx, bx, Wdt, bdt, A_log, Dp, Wout, bout):
            xz = x @ Win + bin
            xs, z = jnp.split(xz, 2, axis=-1)
            xs = jax.nn.silu(xs)
            xp = xs @ Wx + bx
            dp = xp[..., :DT_RANK]
            Bs = xp[..., DT_RANK:DT_RANK + D_STATE]
            Cs = xp[..., DT_RANK + D_STATE:]
            delta = jax.nn.softplus(dp @ Wdt + bdt)
            A = -jnp.exp(A_log.astype(jnp.float32))
            hidden = _ssm_scan(xs, A, Bs, Cs, delta)
            y = (hidden + xs * Dp) * jax.nn.silu(z)
            out = y @ Wout + bout
            return (out, hidden)
        key = jax.random.key(seed)
        ks = jax.random.split(key, 12)
        s_in = 1.0 / np.sqrt(D_MODEL)
        s_x = 1.0 / np.sqrt(D_INNER)
        s_dt = 1.0 / np.sqrt(DT_RANK)
        return {'x': jax.random.normal(ks[0], (BATCH, SEQ, D_MODEL), jnp.float32), 'Win': jax.random.uniform(ks[1], (D_MODEL, 2 * D_INNER), jnp.float32, -s_in, s_in), 'bin': jax.random.uniform(ks[2], (2 * D_INNER,), jnp.float32, -s_in, s_in), 'Wx': jax.random.uniform(ks[3], (D_INNER, DT_RANK + 2 * D_STATE), jnp.float32, -s_x, s_x), 'bx': jax.random.uniform(ks[4], (DT_RANK + 2 * D_STATE,), jnp.float32, -s_x, s_x), 'Wdt': jax.random.uniform(ks[5], (DT_RANK, D_INNER), jnp.float32, -s_dt, s_dt), 'bdt': jax.random.uniform(ks[6], (D_INNER,), jnp.float32, -s_dt, s_dt), 'A_log': jax.random.normal(ks[7], (D_INNER, D_STATE), jnp.float32), 'Dp': jax.random.normal(ks[8], (D_INNER,), jnp.float32), 'Wout': jax.random.uniform(ks[9], (D_INNER, D_MODEL), jnp.float32, -s_x, s_x), 'bout': jax.random.uniform(ks[10], (D_MODEL,), jnp.float32, -s_x, s_x)}
    _L0_attn_all = _L0_attn_setup()
    _L0_attn_in = {k: v for k, v in _L0_attn_all.items() if k in ('Win', 'bin', 'Wx', 'bx', 'Wdt', 'bdt', 'A_log', 'Dp', 'Wout', 'bout')}
    del _L0_attn_all

    def _L0_ffn_setup():
        import jax, jax.numpy as jnp
        import numpy as np
        D_MODEL = 256
        FF_DIM = 4 * D_MODEL
        NUM_EXPERTS = 8
        TOP_K = 2
        B, L = (4, 512)
        key = jax.random.key(seed)
        ks = jax.random.split(key, 7)
        s_in = 1.0 / np.sqrt(D_MODEL)
        s_ff = 1.0 / np.sqrt(FF_DIM)
        return {'x': jax.random.normal(ks[0], (B, L, D_MODEL), dtype=jnp.float32), 'router_w': jax.random.uniform(ks[1], (NUM_EXPERTS, D_MODEL), jnp.float32, -s_in, s_in), 'router_b': jax.random.uniform(ks[2], (NUM_EXPERTS,), jnp.float32, -s_in, s_in), 'w1': jax.random.uniform(ks[3], (NUM_EXPERTS, FF_DIM, D_MODEL), jnp.float32, -s_in, s_in), 'b1': jax.random.uniform(ks[4], (NUM_EXPERTS, FF_DIM), jnp.float32, -s_in, s_in), 'w2': jax.random.uniform(ks[5], (NUM_EXPERTS, D_MODEL, FF_DIM), jnp.float32, -s_ff, s_ff), 'b2': jax.random.uniform(ks[6], (NUM_EXPERTS, D_MODEL), jnp.float32, -s_ff, s_ff)}
    _L0_ffn_all = _L0_ffn_setup()
    _L0_ffn_in = {k: v for k, v in _L0_ffn_all.items() if k in ('router_w', 'router_b', 'w1', 'b1', 'w2', 'b2')}
    del _L0_ffn_all
    return {'x': x, 'ctx_1024': ctx_1024, 'L0_xattn_W_Q': _L0_xattn_in['W_Q'], 'L0_xattn_b_Q': _L0_xattn_in['b_Q'], 'L0_xattn_W_K': _L0_xattn_in['W_K'], 'L0_xattn_b_K': _L0_xattn_in['b_K'], 'L0_xattn_W_V': _L0_xattn_in['W_V'], 'L0_xattn_b_V': _L0_xattn_in['b_V'], 'L0_xattn_W_O': _L0_xattn_in['W_O'], 'L0_xattn_b_O': _L0_xattn_in['b_O'], 'L0_attn_Win': _L0_attn_in['Win'], 'L0_attn_bin': _L0_attn_in['bin'], 'L0_attn_Wx': _L0_attn_in['Wx'], 'L0_attn_bx': _L0_attn_in['bx'], 'L0_attn_Wdt': _L0_attn_in['Wdt'], 'L0_attn_bdt': _L0_attn_in['bdt'], 'L0_attn_A_log': _L0_attn_in['A_log'], 'L0_attn_Dp': _L0_attn_in['Dp'], 'L0_attn_Wout': _L0_attn_in['Wout'], 'L0_attn_bout': _L0_attn_in['bout'], 'L0_ffn_router_w': _L0_ffn_in['router_w'], 'L0_ffn_router_b': _L0_ffn_in['router_b'], 'L0_ffn_w1': _L0_ffn_in['w1'], 'L0_ffn_b1': _L0_ffn_in['b1'], 'L0_ffn_w2': _L0_ffn_in['w2'], 'L0_ffn_b2': _L0_ffn_in['b2']}

def reference(x, ctx_1024, L0_xattn_W_Q, L0_xattn_b_Q, L0_xattn_W_K, L0_xattn_b_K, L0_xattn_W_V, L0_xattn_b_V, L0_xattn_W_O, L0_xattn_b_O, L0_attn_Win, L0_attn_bin, L0_attn_Wx, L0_attn_bx, L0_attn_Wdt, L0_attn_bdt, L0_attn_A_log, L0_attn_Dp, L0_attn_Wout, L0_attn_bout, L0_ffn_router_w, L0_ffn_router_b, L0_ffn_w1, L0_ffn_b1, L0_ffn_w2, L0_ffn_b2):
    import jax
    import jax.numpy as jnp

    def _L0_xattn_ref(x_q, x_k, x_v, W_Q, b_Q, W_K, b_K, W_V, b_V, W_O, b_O):
        import jax, jax.numpy as jnp
        import numpy as np
        D_MODEL = 256
        N_HEADS = 16
        D_K = D_MODEL // N_HEADS
        B, L, _ = x_q.shape
        S = x_k.shape[1]
        H, dk = (N_HEADS, D_K)
        Q = (x_q @ W_Q + b_Q).reshape(B, L, H, dk).transpose(0, 2, 1, 3)
        K = (x_k @ W_K + b_K).reshape(B, S, H, dk).transpose(0, 2, 1, 3)
        V = (x_v @ W_V + b_V).reshape(B, S, H, dk).transpose(0, 2, 1, 3)
        scores = jnp.einsum('bhld,bhsd->bhls', Q, K) / jnp.sqrt(jnp.float32(dk))
        attn = jax.nn.softmax(scores, axis=-1)
        ctx = jnp.einsum('bhls,bhsd->bhld', attn, V)
        ctx = ctx.transpose(0, 2, 1, 3).reshape(B, L, H * dk)
        out = ctx @ W_O + b_O
        return out

    def _L0_attn_ref(x, Win, bin, Wx, bx, Wdt, bdt, A_log, Dp, Wout, bout):
        import jax, jax.numpy as jnp
        import numpy as np
        D_MODEL, D_STATE, EXPAND = (256, 16, 2)
        D_INNER = D_MODEL * EXPAND
        DT_RANK = int(np.ceil(D_MODEL / 16))
        BATCH, SEQ = (2, 512)

        def _ssm_scan(xs, A, Bs, Cs, delta):
            batch, _, d_inner = xs.shape
            n = A.shape[1]

            def step(h, inp):
                x_t, d_t, B_t, C_t = inp
                dA = jnp.exp(d_t[:, :, None] * A)
                h = dA * h + (d_t * x_t)[:, :, None] * B_t[:, None, :]
                y = jnp.einsum('bdn,bn->bd', h, C_t)
                return (h, y)
            h0 = jnp.zeros((batch, d_inner, n), jnp.float32)
            inps = (xs.transpose(1, 0, 2), delta.transpose(1, 0, 2), Bs.transpose(1, 0, 2), Cs.transpose(1, 0, 2))
            _, ys = jax.lax.scan(step, h0, inps)
            return ys.transpose(1, 0, 2)

        def _reference_tuple_inner(x, Win, bin, Wx, bx, Wdt, bdt, A_log, Dp, Wout, bout):
            xz = x @ Win + bin
            xs, z = jnp.split(xz, 2, axis=-1)
            xs = jax.nn.silu(xs)
            xp = xs @ Wx + bx
            dp = xp[..., :DT_RANK]
            Bs = xp[..., DT_RANK:DT_RANK + D_STATE]
            Cs = xp[..., DT_RANK + D_STATE:]
            delta = jax.nn.softplus(dp @ Wdt + bdt)
            A = -jnp.exp(A_log.astype(jnp.float32))
            hidden = _ssm_scan(xs, A, Bs, Cs, delta)
            y = (hidden + xs * Dp) * jax.nn.silu(z)
            out = y @ Wout + bout
            return (out, hidden)
        return _reference_tuple_inner(x, Win, bin, Wx, bx, Wdt, bdt, A_log, Dp, Wout, bout)[0]

    def _L0_ffn_ref(x, router_w, router_b, w1, b1, w2, b2):
        import jax, jax.numpy as jnp
        import numpy as np
        D_MODEL = 256
        FF_DIM = 4 * D_MODEL
        NUM_EXPERTS = 8
        TOP_K = 2
        B, L = (4, 512)
        Bq, Lq, D = x.shape
        x_flat = x.reshape(-1, D)
        logits = x_flat @ router_w.T + router_b
        probs = jax.nn.softmax(logits, axis=-1)
        topk_w, topk_idx = jax.lax.top_k(probs, TOP_K)
        topk_w = topk_w / jnp.sum(topk_w, axis=-1, keepdims=True)
        onehot = jax.nn.one_hot(topk_idx, NUM_EXPERTS, dtype=x.dtype)
        coef = jnp.einsum('tk,tke->te', topk_w, onehot)
        h = jnp.einsum('td,efd->tef', x_flat, w1) + b1[None]
        h = jax.nn.gelu(h, approximate=False)
        y = jnp.einsum('tef,edf->ted', h, w2) + b2[None]
        out = jnp.einsum('ted,te->td', y, coef)
        return out.reshape(Bq, Lq, D)
    x = x + _L0_xattn_ref(_layernorm(x, axis=-1), ctx_1024, ctx_1024, L0_xattn_W_Q, L0_xattn_b_Q, L0_xattn_W_K, L0_xattn_b_K, L0_xattn_W_V, L0_xattn_b_V, L0_xattn_W_O, L0_xattn_b_O)
    x = x + _L0_attn_ref(_layernorm(x, axis=-1), L0_attn_Win, L0_attn_bin, L0_attn_Wx, L0_attn_bx, L0_attn_Wdt, L0_attn_bdt, L0_attn_A_log, L0_attn_Dp, L0_attn_Wout, L0_attn_bout)
    x = x + _L0_ffn_ref(_layernorm(x, axis=-1), L0_ffn_router_w, L0_ffn_router_b, L0_ffn_w1, L0_ffn_b1, L0_ffn_w2, L0_ffn_b2)
    return x

_drawn_inputs = setup_inputs


def setup_inputs(seed=0):
    import zlib

    import numpy as np

    out = dict(_drawn_inputs(seed))
    spreads = {}
    factors = {'L0_xattn_b_Q': 8.0,
     'L0_xattn_b_K': 64.0,
     'L0_xattn_b_V': 4.62,
     'L0_xattn_b_O': 4.797,
     'L0_attn_bin': 6.776,
     'L0_attn_Wx': 5.039,
     'L0_attn_bx': 8.0,
     'L0_attn_Wdt': 8.0,
     'L0_attn_bdt': 8.0,
     'L0_attn_A_log': 7.271,
     'L0_ffn_b1': 28.888,
     'L0_ffn_b2': 19.871,
     'L0_attn_Dp': 3.88,
     'L0_attn_bout': 8.0,
     'L0_ffn_router_b': 8.0}
    for name, (base, spread) in spreads.items():
        noise = np.random.default_rng([zlib.crc32(name.encode()), seed]).standard_normal(out[name].shape)
        drawn = base * np.exp(spread * noise) if base else spread * noise
        out[name] = jnp.asarray(drawn.astype(out[name].dtype))
    for name, factor in factors.items():
        out[name] = (out[name] * factor).astype(out[name].dtype)
    return out
```

```python
import concourse.bass as bass
from concourse import mybir
from contextlib import ExitStack

F32 = mybir.dt.float32
F32R = mybir.dt.float32r
ACT = mybir.ActivationFunctionType
ALU = mybir.AluOpType
AX = mybir.AxisListType.X

P = 128
BATCH, LATENTS, DIM = 32, 64, 256
KEYS = 1601
TOK = BATCH * LATENTS
TT = TOK // P
KD = DIM // P
HEADS, HD = 16, 16
HPM = P // HD
BANK = 512
EPS = 1e-5
INNER, STATE, RANK = 512, 16, 16
KI = INNER // P
EXPERTS, FF = 8, 1024
KF = FF // P

CHUNKS = [(0, 512), (512, 512), (1024, 512), (1536, KEYS - 1536)]
TILES = [(s, min(P, KEYS - s)) for s in range(0, KEYS, P)]
NT = len(TILES)
KEYS_EVEN = KEYS + KEYS % 2
VW = HD + 1


class Names:
    pass


def even(n):
    return n + n % 2


def column_tiles(v):
    return v.rearrange("(m p) -> p m", p=P)


def normalize_and_transpose(nc, tag, x_tok, xn_T, ident):
    with ExitStack() as ctx:
        stats = ctx.enter_context(nc.sbuf_tensor(f"{tag}_stats", [P, TT, 6], F32))
        mean_var = ctx.enter_context(nc.sbuf_tensor(f"{tag}_mean_var", [P, TT, 2], F32))
        rstd = ctx.enter_context(nc.sbuf_tensor(f"{tag}_rstd", [P, TT], F32))
        xn = ctx.enter_context(nc.sbuf_tensor(f"{tag}_xn", [P, TT, DIM], F32))
        banks = [ctx.enter_context(nc.psum_tensor(f"{tag}_T{i}", [P, BANK], F32)) for i in range(4)]
        stats_ready = ctx.enter_context(nc.semaphore(f"{tag}_stats_ready"))
        rooted = ctx.enter_context(nc.semaphore(f"{tag}_rooted"))
        normed = ctx.enter_context(nc.semaphore(f"{tag}_normed"))
        transposed = ctx.enter_context(nc.semaphore(f"{tag}_transposed"))
        copied = ctx.enter_context(nc.semaphore(f"{tag}_copied"))
        block = ctx.enter_context(nc.Block())

        @block.vector
        def _(dve):
            for t in range(TT):
                nc.vector.bn_stats(stats[:, t, :], x_tok[:, t, :]).then_inc(stats_ready, 1)
            dve.wait_ge(stats_ready, TT)
            for t in range(TT):
                nc.vector.bn_aggr(mean_var[:, t, :], stats[:, t, :]).then_inc(stats_ready, 1)
            dve.wait_ge(stats_ready, 2 * TT)
            nc.vector.tensor_scalar(rstd[:, :], mean_var[:, :, 1], EPS, None, ALU.add).then_inc(stats_ready, 1)
            dve.wait_ge(rooted, 1)
            nc.vector.reciprocal(rstd[:, :], rstd[:, :]).then_inc(stats_ready, 1)
            dve.wait_ge(stats_ready, 2 * TT + 2)
            for t in range(TT):
                nc.vector.tensor_scalar(xn[:, t, :], x_tok[:, t, :], mean_var[:, t, 0:1], rstd[:, t:t + 1],
                                        ALU.subtract, ALU.mult).then_inc(normed, 1)

        @block.tensor
        def _(pe):
            n = 0
            for group in range(TT // 4):
                pe.wait_ge(normed, 4 * group + 4)
                for k in range(KD):
                    if n >= 4:
                        pe.wait_ge(copied, n - 3)
                    for j in range(4):
                        last = nc.tensor.transpose(banks[n % 4][:, j * P:(j + 1) * P],
                                                   xn[:, 4 * group + j, k * P:(k + 1) * P], ident[:, :])
                    last.then_inc(transposed, 1)
                    n += 1

        @block.scalar
        def _(act):
            act.wait_ge(stats_ready, 2 * TT + 1)
            nc.scalar.sqrt(rstd[:, :], rstd[:, :]).then_inc(rooted, 1)
            n = 0
            for group in range(TT // 4):
                for k in range(KD):
                    act.wait_ge(transposed, n + 1)
                    nc.scalar.copy(xn_T[:, k, group * BANK:(group + 1) * BANK], banks[n % 4][:, :]) \
                        .then_inc(copied, 1)
                    n += 1


def load_constants(nc, d, s):
    with ExitStack() as ctx:
        loaded = ctx.enter_context(nc.semaphore("constants_loaded"))
        filled = ctx.enter_context(nc.semaphore("constants_filled"))
        block = ctx.enter_context(nc.Block())

        @block.sync
        def _(sp):
            sp.dma_start(s.x_tok[:, :, :], d.x.rearrange("(t p) d -> p t d", p=P)).then_inc(loaded, 16)
            sp.wait_ge(loaded, 16)

        @block.gpsimd
        def _(pool):
            nc.gpsimd.memset(s.ident[:, :], 0.0).then_inc(filled, 1)
            pool.wait_ge(filled, 1)
            nc.gpsimd.affine_select(out=s.ident[:, :], in_=s.ident[:, :], compare_op=ALU.not_equal, fill=1.0,
                                    base=0, pattern=[[-1, P]], channel_multiplier=1).then_inc(filled, 1)


def project_queries(nc, d, s, xn_T):
    with ExitStack() as ctx:
        wq = ctx.enter_context(nc.sbuf_tensor("wq", [P, KD, DIM], F32))
        wk = ctx.enter_context(nc.sbuf_tensor("wk", [P, KD, DIM], F32))
        wv = ctx.enter_context(nc.sbuf_tensor("wv", [P, KD, DIM], F32))
        bq = ctx.enter_context(nc.sbuf_tensor("bq", [P, KD], F32))
        banks = [ctx.enter_context(nc.psum_tensor(f"q_bank{i}", [P, BANK], F32)) for i in range(4)]
        loaded = ctx.enter_context(nc.semaphore("q_loaded"))
        mask_made = ctx.enter_context(nc.semaphore("mask_made"))
        hi_made = ctx.enter_context(nc.semaphore("weights_hi_made"))
        projected = ctx.enter_context(nc.semaphore("q_projected"))
        copied = ctx.enter_context(nc.semaphore("q_copied"))
        block = ctx.enter_context(nc.Block())

        @block.sync
        def _(sp):
            for dst, src in ((wq, d.W_Q), (wk, d.W_K), (wv, d.W_V)):
                sp.dma_start(dst[:, :, :], src.rearrange("(k p) n -> p k n", p=P)).then_inc(loaded, 16)
            sp.dma_start(bq[:, :], column_tiles(d.b_Q), allow_slow_non_contiguous=True).then_inc(loaded, 16)
            sp.dma_start(s.bk[:, :], column_tiles(d.b_K), allow_slow_non_contiguous=True).then_inc(loaded, 16)

        @block.gpsimd
        def _(pool):
            nc.gpsimd.memset(s.head_mask[:, :], 1.0).then_inc(mask_made, 1)
            pool.wait_ge(mask_made, 1)
            nc.gpsimd.affine_select(out=s.head_mask[:, :], in_=s.head_mask[:, :], compare_op=ALU.is_ge,
                                    fill=0.0, base=0, pattern=[[-HD, HPM]], channel_multiplier=1) \
                .then_inc(mask_made, 1)
            pool.wait_ge(mask_made, 2)
            nc.gpsimd.affine_select(out=s.head_mask[:, :], in_=s.head_mask[:, :], compare_op=ALU.is_ge,
                                    fill=0.0, base=HD - 1, pattern=[[HD, HPM]], channel_multiplier=-1) \
                .then_inc(mask_made, 1)

        @block.vector
        def _(dve):
            dve.wait_ge(loaded, 80)
            nc.vector.tensor_copy(s.wk_hi[:, :, :], wk[:, :, :]).then_inc(hi_made, 1)
            nc.vector.tensor_copy(s.wv_hi[:, :, :], wv[:, :, :]).then_inc(hi_made, 1)
            dve.wait_ge(hi_made, 2)
            for lo, whole, hi in ((s.wk_lo, wk, s.wk_hi), (s.wv_lo, wv, s.wv_hi)):
                nc.vector.tensor_tensor(lo[:, :, :], whole[:, :, :], hi[:, :, :].bitcast(F32), ALU.subtract) \
                    .then_inc(hi_made, 1)
            nc.vector.memset(s.ones_row[:, :].bitcast(F32), 1.0)
            for v in s.values:
                nc.vector.memset(v[:, :, :, HD:VW], 1.0)

        @block.tensor
        def _(pe):
            pe.wait_ge(loaded, 80)
            n = 0
            for m in range(KD):
                for c in range(TOK // BANK):
                    if n >= 4:
                        pe.wait_ge(copied, n - 3)
                    for k in range(KD):
                        last = nc.tensor.matmul(banks[n % 4][:, :], wq[:, k, m * P:(m + 1) * P],
                                                xn_T[:, k, c * BANK:(c + 1) * BANK],
                                                start=(k == 0), stop=(k == KD - 1))
                    last.then_inc(projected, 1)
                    n += 1

        @block.scalar
        def _(act):
            n = 0
            for m in range(KD):
                for c in range(TOK // BANK):
                    act.wait_ge(projected, n + 1)
                    nc.scalar.activation(s.q_T[:, m, c * BANK:(c + 1) * BANK], banks[n % 4][:, :], ACT.Identity,
                                         bias=bq[:, m:m + 1]).then_inc(copied, 1)
                    n += 1


UNITS = []
for c in range(len(CHUNKS)):
    UNITS += [("k", m, c) for m in range(KD)]
    UNITS += [("v", j) for j in (2 * c, 2 * c + 1) if 2 * j < NT]
UNITS += [("max", pair, c) for pair in range(HEADS // 2) for c in range(len(CHUNKS))]
UNITS += [("row", m) for m in range(KD)]
WORK_BANKS = 3
NU = len(UNITS)
UNITS += [None] * (-NU % WORK_BANKS)
PER_TILE = [list(range(len(UNITS)))[i * NU // (NT - 1):(i + 1) * NU // (NT - 1)] for i in range(NT - 1)] + [[]]
LAST_OF_CHUNK = [max(u for u in range(NU) if UNITS[u][0] == "v" and UNITS[u][1] // 2 == c)
                 for c in range(len(CHUNKS))]
CREDIT = 2


def attention(nc, d, s, batches=BATCH):
    with ExitStack() as ctx:
        def sb(name, shape, dt=F32):
            return ctx.enter_context(nc.sbuf_tensor(name, shape, dt))

        def sem(name):
            return ctx.enter_context(nc.semaphore(name))

        ctx_hi = [sb(f"ctx_hi{i}", [P, KD, BANK], F32R) for i in range(2)]
        ctx_lo = [sb(f"ctx_lo{i}", [P, KD, BANK], F32R) for i in range(2)]
        k_hi = [sb(f"k_hi{i}", [P, KD, KEYS_EVEN], F32R) for i in range(2)]
        k_lo = [sb(f"k_lo{i}", [P, KD, KEYS_EVEN], F32R) for i in range(2)]
        q_whole = sb("q_whole", [P, KD, HPM * LATENTS])
        q_hi = [sb(f"q_hi{i}", [P, KD, HPM * LATENTS], F32R) for i in range(2)]
        q_lo = [sb(f"q_lo{i}", [P, KD, HPM * LATENTS], F32R) for i in range(2)]
        max_part = [sb(f"max_part{i}", [P, HEADS // 2, len(CHUNKS)]) for i in range(2)]
        neg_max = [sb(f"neg_max{i}", [P, HEADS // 2]) for i in range(2)]
        max_row = [sb(f"max_row{i}", [1, KD, BANK], F32R) for i in range(2)]
        probs = [sb(f"probs{i}", [P, HEADS * LATENTS]) for i in range(2)]
        mixed = [sb(f"mixed{i}", [P, 4 * LATENTS]) for i in range(2)]
        work = [ctx.enter_context(nc.psum_tensor(f"work{i}", [P, BANK], F32)) for i in range(WORK_BANKS)]
        scores = [ctx.enter_context(nc.psum_tensor(f"scores{i}", [P, KD * BANK], F32)) for i in range(2)]
        acc = ctx.enter_context(nc.psum_tensor("acc", [P, BANK], F32))

        ctx_loaded = [sem(f"ctx_loaded{i}") for i in range(2)]
        hi_split = sem("hi_split")
        lo_split = sem("lo_split")
        unit_done = sem("unit_done")
        key_hi_done = sem("key_hi_done")
        unit_evacuated = sem("unit_evacuated")
        maxima_done = sem("maxima_done")
        q_masked = sem("q_masked")
        q_split = sem("q_split")
        scores_ready = sem("scores_ready")
        exp_done = sem("exp_done")
        probs_used = sem("probs_used")
        acc_copied = sem("acc_copied")
        mixed_stored = [sem(f"mixed_stored{i}") for i in range(2)]
        block = ctx.enter_context(nc.Block())

        NC = len(CHUNKS)
        n_v = sum(u is not None and u[0] == "v" for u in UNITS)
        pairs = (batches - 1) // 2

        def evacuated_before(b, u):
            return b * NU + u

        @block.sync
        def _(sp):
            def load(b, par, dram):
                for c, (start, size) in enumerate(CHUNKS):
                    g = b * NC + c
                    if not isinstance(b, int) or g >= 2:
                        sp.wait_ge(lo_split, g - 1)
                    sp.dma_start(s.ctx_whole[c % 2][:, :, 0:size],
                                 dram.rearrange("a (k p) s -> p (a k) s", p=P)[:, :, start:start + size]) \
                        .then_inc(ctx_loaded[c % 2], 16)

            def store(b, par, dram):
                sp.wait_ge(acc_copied, b + 1 + CREDIT)
                sp.dma_start(dram, mixed[par][:, :].rearrange("p (a n) -> p a n", a=1)) \
                    .then_inc(mixed_stored[par], 16)

            def src(b):
                return d.ctx_T[bass.ds(b, 1), :, :]

            def dst(b):
                return d.mixed[bass.ds(b, 1), :, :].rearrange("a p n -> p a n")

            load(0, 0, src(0))
            if pairs:
                with sp.Fori(0, pairs) as i:
                    load(i * 2 + 1, 1, src(i * 2 + 1))
                    store(i * 2, 0, dst(i * 2))
                    load(i * 2 + 2, 0, src(i * 2 + 2))
                    store(i * 2 + 1, 1, dst(i * 2 + 1))
            load(batches - 1, 1, src(batches - 1))
            store(batches - 2, 0, dst(batches - 2))
            store(batches - 1, 1, dst(batches - 1))
            for par in range(2):
                sp.wait_ge(mixed_stored[par], 16 * (batches // 2))

        @block.gpsimd
        def _(pool):
            def prepare(b, par, tokens):
                if not isinstance(b, int) or b >= 1:
                    pool.wait_ge(probs_used, (b - 1) * NT + CREDIT)
                    pool.wait_ge(q_split, b)
                for m in range(KD):
                    q = tokens[:, m, :].rearrange("p (a l) -> p a l", a=1).to_broadcast([P, HPM, LATENTS])
                    mask = s.head_mask[:, :].rearrange("p (h a) -> p h a", a=1).to_broadcast([P, HPM, LATENTS])
                    nc.gpsimd.tensor_tensor(q_whole[:, m, :].rearrange("p (h l) -> p h l", h=HPM), q, mask,
                                            ALU.mult).then_inc(q_masked, 1)
                    nc.gpsimd.tensor_tensor(q_hi[par][:, m, :].rearrange("p (h l) -> p h l", h=HPM), q, mask,
                                            ALU.mult).then_inc(q_masked, 1)
                pool.wait_ge(q_masked, (b + 1) * 2 * KD)
                nc.gpsimd.tensor_tensor(q_lo[par][:, :, :], q_whole[:, :, :], q_hi[par][:, :, :].bitcast(F32),
                                        ALU.subtract).then_inc(q_split, 1)
                for c, (start, size) in enumerate(CHUNKS):
                    n = even(size)
                    pool.wait_ge(hi_split, b * NC + c + 1)
                    nc.gpsimd.tensor_tensor(ctx_lo[c % 2][:, :, 0:n], s.ctx_whole[c % 2][:, :, 0:n],
                                            ctx_hi[c % 2][:, :, 0:n].bitcast(F32), ALU.subtract) \
                        .then_inc(lo_split, 1)

            def tokens(b):
                return s.q_T[:, :, bass.ds(b * LATENTS, LATENTS)]

            prepare(0, 0, tokens(0))
            if pairs:
                with pool.Fori(0, pairs) as i:
                    prepare(i * 2 + 1, 1, tokens(i * 2 + 1))
                    prepare(i * 2 + 2, 0, tokens(i * 2 + 2))
            prepare(batches - 1, 1, tokens(batches - 1))

        @block.vector
        def _(dve):
            def split(b, c):
                g = b * NC + c
                n = even(CHUNKS[c][1])
                dve.wait_ge(ctx_loaded[c % 2], (b * (NC // 2) + c // 2 + 1) * 16)
                if not isinstance(b, int) or g >= 2:
                    before = LAST_OF_CHUNK[c - 2] + (NU if c >= 2 else 0)
                    dve.wait_ge(unit_done, (b - 1) * NU + before + 1)
                nc.vector.tensor_copy(ctx_hi[c % 2][:, :, 0:n], s.ctx_whole[c % 2][:, :, 0:n]) \
                    .then_inc(hi_split, 1)

            def unit(b, par, u):
                kind = UNITS[u][0]
                dve.wait_ge(unit_done, b * NU + u + 1)
                bank = work[u % WORK_BANKS]
                if kind == "k":
                    _, m, c = UNITS[u]
                    start, size = CHUNKS[c]
                    n = even(size)
                    dve.wait_ge(key_hi_done, b * KD * NC + c * KD + m + 1)
                    nc.vector.scalar_tensor_tensor(k_lo[par][:, m, start:start + n], bank[:, 0:n], s.bk[:, m:m + 1],
                                                   k_hi[par][:, m, start:start + n].bitcast(F32),
                                                   ALU.add, ALU.subtract).then_inc(unit_evacuated, 1)
                elif kind == "v":
                    j = UNITS[u][1]
                    tiles = min(2, NT - 2 * j)
                    rows = TILES[2 * j][1]
                    nc.vector.tensor_copy(
                        s.values[par][0:rows, 2 * j:2 * j + tiles, :, 0:HD],
                        bank[0:rows, 0:tiles * DIM].rearrange("p (t h e) -> p t h e", t=tiles, h=HEADS)) \
                        .then_inc(unit_evacuated, 1)
                elif kind == "max":
                    _, pair, c = UNITS[u]
                    nc.vector.reduce_max(max_part[par][:, pair, c:c + 1], bank[:, 0:CHUNKS[c][1]], AX) \
                        .then_inc(unit_evacuated, 1)
                    if pair == HEADS // 2 - 1 and c == NC - 1:
                        dve.wait_ge(unit_evacuated, b * NU + u + 1)
                        nc.vector.tensor_reduce(neg_max[par][:, :], max_part[par][:, :, :], AX, ALU.max, negate=True) \
                            .then_inc(maxima_done, 1)
                else:
                    nc.vector.tensor_copy(max_row[par][0:1, UNITS[u][1], :], bank[0:1, :]).then_inc(unit_evacuated, 1)

            def prepare(b, par):
                split(b, 0)
                split(b, 1)
                for u in range(NU):
                    unit(b, par, u)
                    if u in LAST_OF_CHUNK[:NC - 2]:
                        split(b, LAST_OF_CHUNK.index(u) + 2)

            nc.vector.memset(acc[:, :], 0.0)
            prepare(0, 0)
            if pairs:
                with dve.Fori(0, pairs) as i:
                    prepare(i * 2 + 1, 1)
                    prepare(i * 2 + 2, 0)
            prepare(batches - 1, 1)

        @block.scalar
        def _(act):
            def key_hi(b, par, u):
                if UNITS[u] and UNITS[u][0] == "k":
                    _, m, c = UNITS[u]
                    start, size = CHUNKS[c]
                    n = even(size)
                    act.wait_ge(unit_done, b * NU + u + 1)
                    nc.scalar.activation(k_hi[par][:, m, start:start + n], work[u % WORK_BANKS][:, 0:n],
                                         ACT.Identity, bias=s.bk[:, m:m + 1]).then_inc(key_hi_done, 1)

            def attend(b, par, ahead):
                for t in range(NT):
                    n = b * NT + t
                    slot = (par * NT + t) % 2
                    rows = TILES[t][1]
                    act.wait_ge(scores_ready, n + 1)
                    act.wait_ge(probs_used, n + 1)
                    nc.scalar.activation(probs[slot][0:rows, :], scores[slot][0:rows, :], ACT.Exp,
                                         scale=1.0 / HD ** 0.5).then_inc(exp_done, 1)
                    if ahead:
                        for u in PER_TILE[t]:
                            key_hi(b + 1, 1 - par, u)
                act.wait_ge(probs_used, b * NT + NT + CREDIT)
                act.wait_ge(mixed_stored[par], (b - par) * 8)
                nc.scalar.copy(mixed[par][:, :], acc[:, par * DIM:(par + 1) * DIM]).then_inc(acc_copied, 1)

            act.sem_inc(exp_done, CREDIT)
            act.sem_inc(acc_copied, CREDIT)
            for u in range(NU):
                key_hi(0, 0, u)
            if pairs:
                with act.Fori(0, pairs) as i:
                    attend(i * 2, 0, True)
                    attend(i * 2 + 1, 1, True)
            attend(batches - 2, 0, True)
            attend(batches - 1, 1, False)

        @block.tensor
        def _(pe):
            def unit(b, par, u):
                if UNITS[u] is None:
                    return
                kind = UNITS[u][0]
                bank = work[u % WORK_BANKS]
                if not isinstance(b, int) or b * NU + u - WORK_BANKS >= 0:
                    before = u - WORK_BANKS if u >= WORK_BANKS else min(u + len(UNITS) - WORK_BANKS, NU - 1) - NU
                    pe.wait_ge(unit_evacuated, evacuated_before(b, before + 1))
                if kind == "k":
                    _, m, c = UNITS[u]
                    n = even(CHUNKS[c][1])
                    if m == 0:
                        pe.wait_ge(lo_split, b * NC + c + 1)
                    cols = slice(m * P, (m + 1) * P)
                    parts = [(w, x, k) for w, x in ((s.wk_hi, ctx_hi), (s.wk_hi, ctx_lo), (s.wk_lo, ctx_hi))
                             for k in range(KD)]
                    for i, (w, x, k) in enumerate(parts):
                        last = nc.tensor.matmul(bank[:, 0:n], w[:, k, cols], x[c % 2][:, k, 0:n],
                                                start=(i == 0), stop=(i == len(parts) - 1))
                elif kind == "v":
                    j = UNITS[u][1]
                    c = j // 2
                    for i, t in enumerate(range(2 * j, min(2 * j + 2, NT))):
                        start, rows = TILES[t]
                        at = start - CHUNKS[c][0]
                        parts = [(x, w, k) for k in range(KD)
                                 for x, w in ((ctx_hi, s.wv_hi), (ctx_hi, s.wv_lo), (ctx_lo, s.wv_hi))]
                        for n, (x, w, k) in enumerate(parts):
                            last = nc.tensor.matmul(bank[0:rows, i * DIM:(i + 1) * DIM],
                                                    x[c % 2][:, k, at:at + rows], w[:, k, :],
                                                    start=(n == 0), stop=(n == len(parts) - 1))
                elif kind == "max":
                    _, pair, c = UNITS[u]
                    start, size = CHUNKS[c]
                    if pair == 0 and c == 0:
                        pe.wait_ge(q_split, b + 1)
                        pe.wait_ge(unit_evacuated, evacuated_before(b, UNITS.index(("k", KD - 1, NC - 1)) + 1))
                    m, at = pair // 4, (pair % 4) * P
                    last = nc.tensor.matmul(bank[:, 0:even(size)], q_hi[par][:, m, at:at + P],
                                            k_hi[par][:, m, start:start + even(size)], start=True, stop=True)
                else:
                    m = UNITS[u][1]
                    pe.wait_ge(maxima_done, b + 1)
                    for j in range(4):
                        last = nc.tensor.matmul(bank[0:1, j * P:(j + 1) * P], neg_max[par][:, 4 * m + j:4 * m + j + 1],
                                                s.ident[:, :], start=True, stop=True)
                last.then_inc(unit_done, 1)

            def score(b, par, t):
                n = b * NT + t
                start, rows = TILES[t]
                bank = scores[(par * NT + t) % 2]
                pe.wait_ge(exp_done, n + 1)
                for m in range(KD):
                    cols = slice(m * BANK, (m + 1) * BANK)
                    keys = slice(start, start + rows)
                    for i, (k, q) in enumerate(((k_hi, q_hi), (k_hi, q_lo), (k_lo, q_hi))):
                        nc.tensor.matmul(bank[0:rows, cols], k[par][:, m, keys], q[par][:, m, :],
                                         start=(i == 0), stop=False)
                    last = nc.tensor.matmul(bank[0:rows, cols], s.ones_row[0:1, 0:rows], max_row[par][0:1, m, :],
                                            start=False, stop=True)
                last.then_inc(scores_ready, 1)

            def mix(b, par, t):
                n = b * NT + t
                rows = TILES[t][1]
                pe.wait_ge(exp_done, n + 1 + CREDIT)
                if t == 0:
                    pe.wait_ge(acc_copied, b + 1)
                p = probs[(par * NT + t) % 2]
                for g in range(4):
                    for j in range(4):
                        h = 4 * g + j
                        last = nc.tensor.matmul(
                            acc[32 * j:32 * j + VW, par * DIM + g * LATENTS:par * DIM + (g + 1) * LATENTS],
                            s.values[par][0:rows, t, h, :], p[0:rows, h * LATENTS:(h + 1) * LATENTS],
                            start=(t == 0 and g == 0), stop=(t == NT - 1), skip_group_check=True)
                last.then_inc(probs_used, 1)

            def attend(b, par, ahead):
                pe.wait_ge(unit_evacuated, evacuated_before(b, NU))
                score(b, par, 0)
                for t in range(NT):
                    if t + 1 < NT:
                        score(b, par, t + 1)
                    if ahead:
                        for u in PER_TILE[t]:
                            unit(b + 1, 1 - par, u)
                    mix(b, par, t)

            pe.sem_inc(probs_used, CREDIT)
            for u in range(NU):
                unit(0, 0, u)
            if pairs:
                with pe.Fori(0, pairs) as i:
                    attend(i * 2, 0, True)
                    attend(i * 2 + 1, 1, True)
            attend(batches - 2, 0, True)
            attend(batches - 1, 1, False)


def attention_memory(nc, ctx):
    def sb(name, shape, dt=F32):
        return ctx.enter_context(nc.sbuf_tensor(name, shape, dt))
    s = Names()
    s.q_T, s.head_mask, s.bk = sb("q_T", [P, KD, TOK]), sb("head_mask", [P, HPM]), sb("bk", [P, KD])
    s.wk_hi, s.wk_lo = sb("wk_hi", [P, KD, DIM], F32R), sb("wk_lo", [P, KD, DIM], F32R)
    s.wv_hi, s.wv_lo = sb("wv_hi", [P, KD, DIM], F32R), sb("wv_lo", [P, KD, DIM], F32R)
    s.ones_row = sb("ones_row", [1, P], F32R)
    s.ctx_whole = [sb(f"ctx_whole{i}", [P, KD, BANK]) for i in range(2)]
    s.values = [sb(f"values{i}", [P, NT, HEADS, VW]) for i in range(2)]
    return s


def attention_output(nc, d, s):
    with ExitStack() as ctx:
        def sb(name, shape, dt=F32):
            return ctx.enter_context(nc.sbuf_tensor(name, shape, dt))

        G = HEADS // 4
        mixed = sb("mixed_T", [P, G, TOK])
        wo = sb("wo", [P, G, DIM])
        bv = sb("bv", [P, G])
        bo = sb("bo", [P, DIM])
        pick = sb("pick", [P, 4, 32])
        inverse = [sb(f"inverse{i}", [P, BANK]) for i in range(2)]
        sums = [ctx.enter_context(nc.psum_tensor(f"o_sums{i}", [P, BANK], F32)) for i in range(4)]
        outs = [ctx.enter_context(nc.psum_tensor(f"o_outs{i}", [P, BANK], F32)) for i in range(4)]
        loaded = ctx.enter_context(nc.semaphore("o_loaded"))
        cleared = ctx.enter_context(nc.semaphore("o_cleared"))
        pick_made = ctx.enter_context(nc.semaphore("pick_made"))
        summed = ctx.enter_context(nc.semaphore("o_summed"))
        inverted = ctx.enter_context(nc.semaphore("o_inverted"))
        divided = ctx.enter_context(nc.semaphore("o_divided"))
        biased = ctx.enter_context(nc.semaphore("o_biased"))
        projected = ctx.enter_context(nc.semaphore("o_projected"))
        added = ctx.enter_context(nc.semaphore("o_added"))
        block = ctx.enter_context(nc.Block())
        NCH = TOK // BANK

        @block.sync
        def _(sp):
            for g in range(G):
                sp.dma_start(mixed[:, g, :].rearrange("p (b l) -> p b l", b=BATCH),
                             d.mixed.rearrange("b p (g l) -> g p b l", g=G)[g]).then_inc(loaded, 16)
            sp.dma_start(bo[:, :], d.b_O.rearrange("(a n) -> a n", a=1).to_broadcast([P, DIM])).then_inc(loaded, 16)
            sp.wait_ge(cleared, 2)
            for j in range(4):
                rows = slice(32 * j, 32 * j + HD)
                sp.dma_start(wo[rows, :, :], d.W_O.rearrange("(g c e) n -> c e g n", c=4, e=HD)[j]) \
                    .then_inc(loaded, 16)
                sp.dma_start(bv[rows, :], d.b_V.rearrange("(g c e) -> c e g", c=4, e=HD)[j],
                             allow_slow_non_contiguous=True).then_inc(loaded, 16)

        @block.gpsimd
        def _(pool):
            nc.gpsimd.memset(wo[:, :, :], 0.0).then_inc(cleared, 1)
            nc.gpsimd.memset(bv[:, :], 0.0).then_inc(cleared, 1)
            nc.gpsimd.memset(pick[:, :, :], 0.0).then_inc(pick_made, 1)
            pool.wait_ge(pick_made, 1)
            nc.gpsimd.affine_select(out=pick[:, :, :], in_=pick[:, :, :], compare_op=ALU.not_equal, fill=1.0,
                                    base=-HD, pattern=[[-32, 4], [0, 32]], channel_multiplier=1) \
                .then_inc(pick_made, 1)

        @block.tensor
        def _(pe):
            pe.wait_ge(loaded, 16 * (G + 1 + 8))
            pe.wait_ge(pick_made, 2)
            n = 0
            for c in range(NCH):
                for g in range(G):
                    if n >= 4:
                        pe.wait_ge(inverted, n - 3)
                    nc.tensor.matmul(sums[n % 4][:, :], pick[:, :, :].rearrange("p j i -> p (j i)"),
                                     mixed[:, g, c * BANK:(c + 1) * BANK], start=True, stop=True) \
                        .then_inc(summed, 1)
                    n += 1
            for t in range(TT):
                pe.wait_ge(biased, G * (t // 4) + G)
                if t >= 4:
                    pe.wait_ge(added, t - 3)
                for g in range(G):
                    last = nc.tensor.matmul(outs[t % 4][:, 0:DIM], mixed[:, g, t * P:(t + 1) * P], wo[:, g, :],
                                            start=(g == 0), stop=(g == G - 1))
                last.then_inc(projected, 1)

        @block.scalar
        def _(act):
            for n in range(NCH * G):
                c, g = divmod(n, G)
                act.wait_ge(divided, n + 1)
                part = mixed[:, g, c * BANK:(c + 1) * BANK]
                nc.scalar.activation(part, part, ACT.Identity, bias=bv[:, g:g + 1]).then_inc(biased, 1)

        @block.vector
        def _(dve):
            for n in range(NCH * G):
                c, g = divmod(n, G)
                dve.wait_ge(summed, n + 1)
                nc.vector.reciprocal(inverse[n % 2][:, :], sums[n % 4][:, :]).then_inc(inverted, 1)
                dve.wait_ge(inverted, n + 1)
                part = mixed[:, g, c * BANK:(c + 1) * BANK]
                nc.vector.tensor_tensor(part, part, inverse[n % 2][:, :], ALU.mult).then_inc(divided, 1)
            for t in range(TT):
                dve.wait_ge(projected, t + 1)
                nc.vector.tensor_tensor(s.x_tok[:, t, :], s.x_tok[:, t, :], outs[t % 4][:, 0:DIM], ALU.add) \
                    .then_inc(added, 1)
            dve.wait_ge(added, TT)
            for t in range(TT):
                nc.vector.tensor_tensor(s.x_tok[:, t, :], s.x_tok[:, t, :], bo[:, :], ALU.add)


HALF = 1024
BC_COLS = 96


def ssm_projections(nc, d, s, xn_T):
    with ExitStack() as ctx:
        def sb(name, shape, dt=F32):
            return ctx.enter_context(nc.sbuf_tensor(name, shape, dt))

        def sem(name):
            return ctx.enter_context(nc.semaphore(name))

        win = sb("win", [P, KD, 2 * INNER])
        bin_ = sb("bin", [P, 2 * KI])
        wx = sb("wx", [P, KI, BC_COLS])
        bx = sb("bx", [BC_COLS, 1])
        wdt = sb("wdt", [RANK, INNER])
        bdt = sb("bdt", [P, KI])
        xp = sb("xp", [BC_COLS, TOK])
        z = [sb(f"z{i}", [P, BANK]) for i in range(2)]
        raw = [sb(f"raw{i}", [P, BANK]) for i in range(2)]
        decay = [sb(f"decay{i}", [P, BANK]) for i in range(2)]
        log = [sb(f"log{i}", [P, BANK]) for i in range(2)]
        banks = [ctx.enter_context(nc.psum_tensor(f"s_bank{i}", [P, BANK], F32)) for i in range(4)]
        loaded, cleared = sem("s_loaded"), sem("s_cleared")
        projected, gated = sem("s_projected"), sem("s_gated")
        z_stored = [sem(f"z_stored{i}") for i in range(2)]
        xp_projected, xp_copied, bc_stored = sem("xp_projected"), sem("xp_copied"), sem("bc_stored")
        dt_projected, dt_raw, dt_abs, dt_exp, dt_log, dt_steps = (
            sem("dt_projected"), sem("dt_raw"), sem("dt_abs"), sem("dt_exp"), sem("dt_log"), sem("dt_steps"))
        block = ctx.enter_context(nc.Block())
        NCH = TOK // BANK

        @block.sync
        def _(sp):
            sp.dma_start(win[:, :, :], d.Win.rearrange("(k p) n -> p k n", p=P)).then_inc(loaded, 16)
            sp.dma_start(bin_[:, :], column_tiles(d.bin), allow_slow_non_contiguous=True).then_inc(loaded, 16)
            sp.dma_start(wdt[:, :], d.Wdt).then_inc(loaded, 16)
            sp.dma_start(bdt[:, :], column_tiles(d.bdt), allow_slow_non_contiguous=True).then_inc(loaded, 16)
            sp.dma_start(s.dp[:, :], column_tiles(d.Dp), allow_slow_non_contiguous=True).then_inc(loaded, 16)
            sp.dma_start(s.a[:, :, :], d.A_log.rearrange("(k p) n -> p k n", p=P)).then_inc(loaded, 16)
            sp.wait_ge(cleared, 2)
            wx_v = d.Wx.rearrange("(k p) n -> p k n", p=P)
            bx_v = d.bx.rearrange("(p a) -> p a", a=1)
            for i in range(3):
                sp.dma_start(wx[:, :, 32 * i:32 * i + STATE], wx_v[:, :, STATE * i:STATE * (i + 1)]) \
                    .then_inc(loaded, 16)
                sp.dma_start(bx[32 * i:32 * i + STATE, :], bx_v[STATE * i:STATE * (i + 1), :]).then_inc(loaded, 16)
            for n in range(KI * NCH):
                m, c = divmod(n, NCH)
                sp.wait_ge(gated, (KI + m) * NCH + c + 1)
                sp.dma_start(d.z[m, :, c * BANK:(c + 1) * BANK], z[n % 2][:, :]).then_inc(z_stored[n % 2], 16)
            sp.wait_ge(xp_copied, NCH)
            for i in range(2):
                sp.dma_start(d.bc[i, :, :], xp[32 * (i + 1):32 * (i + 1) + STATE, :]).then_inc(bc_stored, 16)
            for i in range(2):
                sp.wait_ge(z_stored[i], 16 * KI * NCH // 2)
            sp.wait_ge(bc_stored, 32)

        @block.gpsimd
        def _(pool):
            nc.gpsimd.memset(wx[:, :, :], 0.0).then_inc(cleared, 1)
            nc.gpsimd.memset(bx[:, :], 0.0).then_inc(cleared, 1)

        @block.tensor
        def _(pe):
            pe.wait_ge(loaded, 16 * 12)
            n = 0
            for m in range(2 * KI):
                for c in range(NCH):
                    if n >= 4:
                        pe.wait_ge(gated, n - 3)
                    for k in range(KD):
                        last = nc.tensor.matmul(banks[n % 4][:, :], win[:, k, m * P:(m + 1) * P],
                                                xn_T[:, k, c * BANK:(c + 1) * BANK],
                                                start=(k == 0), stop=(k == KD - 1))
                    last.then_inc(projected, 1)
                    n += 1
            for c in range(NCH):
                pe.wait_ge(gated, n - 3 + c)
                for k in range(KI):
                    last = nc.tensor.matmul(banks[c][0:BC_COLS, :], wx[:, k, :], s.xs[:, k, c * BANK:(c + 1) * BANK],
                                            start=(k == 0), stop=(k == KI - 1))
                last.then_inc(xp_projected, 1)
            pe.wait_ge(xp_copied, NCH)
            n = 0
            for m in range(KI):
                for c in range(NCH):
                    if n >= 4:
                        pe.wait_ge(dt_raw, n - 3)
                    nc.tensor.matmul(banks[n % 4][:, :], wdt[:, m * P:(m + 1) * P], xp[0:RANK, c * BANK:(c + 1) * BANK],
                                     start=True, stop=True).then_inc(dt_projected, 1)
                    n += 1

        @block.scalar
        def _(act):
            act.wait_ge(loaded, 16 * 12)
            for n in range(2 * KI * NCH):
                m, c = divmod(n, NCH)
                act.wait_ge(projected, n + 1)
                if m < KI:
                    out = s.xs[:, m, c * BANK:(c + 1) * BANK]
                else:
                    i = n - KI * NCH
                    out = z[i % 2][:, :]
                    if i >= 2:
                        act.wait_ge(z_stored[i % 2], 16 * (i // 2))
                nc.scalar.activation(out, banks[n % 4][:, :], ACT.Silu, bias=bin_[:, m:m + 1]).then_inc(gated, 1)
            for c in range(NCH):
                act.wait_ge(xp_projected, c + 1)
                nc.scalar.activation(xp[:, c * BANK:(c + 1) * BANK], banks[c][0:BC_COLS, :], ACT.Identity,
                                     bias=bx[:, 0:1]).then_inc(xp_copied, 1)
            nc.scalar.activation(s.a[:, :, :], s.a[:, :, :], ACT.Exp)
            for n in range(KI * NCH):
                act.wait_ge(dt_abs, n + 1)
                if n >= 2:
                    act.wait_ge(dt_steps, 4 * (n - 1))
                nc.scalar.activation(decay[n % 2][:, :], decay[n % 2][:, :], ACT.Exp).then_inc(dt_exp, 1)
                act.wait_ge(dt_exp, n + 1)
                nc.scalar.activation(log[n % 2][:, :], decay[n % 2][:, :], ACT.Ln, bias=1.0).then_inc(dt_log, 1)

        @block.vector
        def _(dve):
            for n in range(KI * NCH):
                m, c = divmod(n, NCH)
                cols = slice(c * BANK, (c + 1) * BANK)
                e, v, l = decay[n % 2][:, :], raw[n % 2][:, :], log[n % 2][:, :]
                dve.wait_ge(dt_projected, n + 1)
                nc.vector.tensor_scalar(v, banks[n % 4][:, :], bdt[:, m:m + 1], None, ALU.add).then_inc(dt_raw, 1)
                dve.wait_ge(dt_raw, n + 1)
                nc.vector.scalar_tensor_tensor(e, v, -1.0, v, ALU.mult, ALU.min).then_inc(dt_abs, 1)
                dve.wait_ge(dt_log, n + 1)
                delta = s.delta[:, m, cols]
                steps = 4 * n
                nc.vector.tensor_scalar(delta, e, 1.0, -1.0, ALU.add, ALU.add).then_inc(dt_steps, 1)
                dve.wait_ge(dt_steps, steps + 1)
                nc.vector.tensor_tensor(e, e, delta, ALU.subtract).then_inc(dt_steps, 1)
                nc.vector.scalar_tensor_tensor(l, v, 0.0, l, ALU.max, ALU.add).then_inc(dt_steps, 1)
                dve.wait_ge(dt_steps, steps + 3)
                nc.vector.tensor_tensor(delta, l, e, ALU.add).then_inc(dt_steps, 1)
                dve.wait_ge(dt_steps, steps + 4)
                nc.vector.tensor_tensor(s.dtx[:, m, cols], delta, s.xs[:, m, cols], ALU.mult)


def ssm_scan(nc, d, s):
    with ExitStack() as ctx:
        def sb(name, shape, dt=F32):
            return ctx.enter_context(nc.sbuf_tensor(name, shape, dt))

        def sem(name):
            return ctx.enter_context(nc.semaphore(name))

        b_all = [sb(f"b_all{i}", [P, HALF]) for i in range(2)]
        c_all = [sb(f"c_all{i}", [P, HALF]) for i in range(2)]
        da = [sb(f"da{i}", [P, HALF]) for i in range(2)]
        dbx = [sb(f"dbx{i}", [P, HALF]) for i in range(2)]
        h = [sb(f"h{i}", [P, HALF]) for i in range(2)]
        hc = [sb(f"hc{i}", [P, HALF]) for i in range(2)]
        z = [sb(f"zg{i}", [P, HALF]) for i in range(2)]
        y = [ctx.enter_context(nc.psum_tensor(f"y{k}", [P, HALF], F32)) for k in range(KI)]
        bc_loaded = [sem(f"bc_loaded{i}") for i in range(2)]
        da_done, da_cut, dbx_done, h_done, hc_done, summed = (
            sem("da_done"), sem("da_cut"), sem("dbx_done"), sem("h_done"), sem("hc_done"), sem("y_summed"))
        z_loaded = [sem(f"z_loaded{i}") for i in range(2)]
        skip_done, y_added, y_done = sem("skip_done"), sem("y_added"), sem("y_done")
        a_signed = sem("a_signed")
        block = ctx.enter_context(nc.Block())
        HALVES = TOK // HALF
        ROUNDS = HALVES * STATE * KI

        @block.sync
        def _(sp):
            zi = 0
            for r in range(HALVES * STATE):
                half, n = divmod(r, STATE)
                cols = slice(half * HALF, (half + 1) * HALF)
                if r >= 2:
                    sp.wait_ge(hc_done, KI * (r - 1))
                for i, dst in enumerate((b_all, c_all)):
                    sp.dma_start(dst[r % 2][:, :], d.bc[i, n:n + 1, cols].to_broadcast([P, HALF])) \
                        .then_inc(bc_loaded[r % 2], 16)
                if n == STATE - 1:
                    for k in range(KI):
                        if zi >= 2:
                            sp.wait_ge(y_done, zi - 1)
                        sp.dma_start(z[zi % 2][:, :], d.z[k, :, cols]).then_inc(z_loaded[zi % 2], 16)
                        zi += 1

        @block.scalar
        def _(act):
            act.wait_ge(a_signed, 1)
            for r in range(ROUNDS):
                half, n, k = r // (STATE * KI), r // KI % STATE, r % KI
                if r >= 2:
                    act.wait_ge(h_done, r - 1)
                nc.scalar.activation(da[r % 2][:, :], s.delta[:, k, half * HALF:(half + 1) * HALF], ACT.Exp,
                                     scale=s.a[:, k, n:n + 1]).then_inc(da_done, 1)

        @block.gpsimd
        def _(pool):
            for r in range(ROUNDS):
                half, n, k = r // (STATE * KI), r // KI % STATE, r % KI
                state = r // KI
                pool.wait_ge(bc_loaded[state % 2], 32 * (state // 2 + 1))
                if r >= 2:
                    pool.wait_ge(h_done, r - 1)
                nc.gpsimd.tensor_tensor(dbx[r % 2][:, :], s.dtx[:, k, half * HALF:(half + 1) * HALF],
                                        b_all[state % 2][:, :], ALU.mult).then_inc(dbx_done, 1)

        @block.vector
        def _(dve):
            nc.vector.tensor_scalar(s.a[:, :, :], s.a[:, :, :], -1.0, None, ALU.mult).then_inc(a_signed, 1)
            out = 0
            for r in range(ROUNDS):
                half, n, k = r // (STATE * KI), r // KI % STATE, r % KI
                state = r // KI
                dve.wait_ge(da_done, r + 1)
                nc.vector.memset(da[r % 2][:, :].rearrange("p (b l) -> p b l", l=LATENTS)[:, :, 0:1], 0.0) \
                    .then_inc(da_cut, 1)
                dve.wait_ge(da_cut, r + 1)
                dve.wait_ge(dbx_done, r + 1)
                nc.vector.tensor_tensor_scan(h[r % 2][:, :], da[r % 2][:, :], dbx[r % 2][:, :], 0.0,
                                             ALU.mult, ALU.add).then_inc(h_done, 1)
                dve.wait_ge(h_done, r + 1)
                dve.wait_ge(bc_loaded[state % 2], 32 * (state // 2 + 1))
                if r >= 2:
                    dve.wait_ge(summed, r - 1)
                nc.vector.tensor_tensor(hc[r % 2][:, :], h[r % 2][:, :], c_all[state % 2][:, :], ALU.mult) \
                    .then_inc(hc_done, 1)
                if n == STATE - 1 and k == KI - 1:
                    for k in range(KI):
                        cols = slice(half * HALF, (half + 1) * HALF)
                        yk = s.y[:, k, cols]
                        dve.wait_ge(summed, half * STATE * KI + (STATE - 1) * KI + k + 1)
                        nc.vector.scalar_tensor_tensor(yk, s.xs[:, k, cols], s.dp[:, k:k + 1], y[k][:, :],
                                                       ALU.mult, ALU.add).then_inc(y_added, 1)
                        dve.wait_ge(y_added, out + 1)
                        dve.wait_ge(z_loaded[out % 2], 16 * (out // 2 + 1))
                        nc.vector.tensor_tensor(yk, yk, z[out % 2][:, :], ALU.mult).then_inc(y_done, 1)
                        out += 1

        @block.tensor
        def _(pe):
            for r in range(ROUNDS):
                half, n, k = r // (STATE * KI), r // KI % STATE, r % KI
                pe.wait_ge(hc_done, r + 1)
                if n == 0 and half > 0:
                    pe.wait_ge(y_added, half * KI)
                for c in range(HALF // BANK):
                    cols = slice(c * BANK, (c + 1) * BANK)
                    last = nc.tensor.matmul(y[k][:, cols], s.ident[:, :], hc[r % 2][:, cols],
                                            start=(n == 0), stop=(n == STATE - 1))
                last.then_inc(summed, 1)


def add_projection(nc, tag, s, y_T, w_dram, b_dram, kt):
    with ExitStack() as ctx:
        w = ctx.enter_context(nc.sbuf_tensor(f"{tag}_w", [P, kt, DIM], F32))
        b = ctx.enter_context(nc.sbuf_tensor(f"{tag}_b", [P, DIM], F32))
        banks = [ctx.enter_context(nc.psum_tensor(f"{tag}_bank{i}", [P, BANK], F32)) for i in range(4)]
        loaded = ctx.enter_context(nc.semaphore(f"{tag}_loaded"))
        projected = ctx.enter_context(nc.semaphore(f"{tag}_projected"))
        added = ctx.enter_context(nc.semaphore(f"{tag}_added"))
        block = ctx.enter_context(nc.Block())

        @block.sync
        def _(sp):
            sp.dma_start(w[:, :, :], w_dram.rearrange("(k p) n -> p k n", p=P)).then_inc(loaded, 16)
            sp.dma_start(b[:, :], b_dram.rearrange("(a n) -> a n", a=1).to_broadcast([P, DIM])).then_inc(loaded, 16)

        @block.tensor
        def _(pe):
            pe.wait_ge(loaded, 32)
            for t in range(TT):
                if t >= 4:
                    pe.wait_ge(added, t - 3)
                for k in range(kt):
                    last = nc.tensor.matmul(banks[t % 4][:, 0:DIM], y_T[:, k, t * P:(t + 1) * P], w[:, k, :],
                                            start=(k == 0), stop=(k == kt - 1))
                last.then_inc(projected, 1)

        @block.vector
        def _(dve):
            dve.wait_ge(loaded, 32)
            for t in range(TT):
                dve.wait_ge(projected, t + 1)
                nc.vector.tensor_tensor(s.x_tok[:, t, :], s.x_tok[:, t, :], banks[t % 4][:, 0:DIM], ALU.add) \
                    .then_inc(added, 1)
            dve.wait_ge(added, TT)
            for t in range(TT):
                nc.vector.tensor_tensor(s.x_tok[:, t, :], s.x_tok[:, t, :], b[:, :], ALU.add)


def route(nc, d, s, xn_T):
    with ExitStack() as ctx:
        def sb(name, shape, dt=F32):
            return ctx.enter_context(nc.sbuf_tensor(name, shape, dt))

        E = EXPERTS
        rw = sb("rw", [P, KD, E])
        rb = sb("rb", [P, E])
        logits = sb("logits", [P, TT, E])
        top = sb("top", [P, TT])
        ex = sb("ex", [P, TT, E])
        before = sb("before", [P, TT, E, E])
        same = sb("same", [P, TT, E, E])
        lower = sb("lower", [P, E, E])
        rank = sb("rank", [P, TT, E])
        total = sb("total", [P, TT])
        bank = ctx.enter_context(nc.psum_tensor("r_bank", [P, TT * E], F32))
        coef_bank = [ctx.enter_context(nc.psum_tensor(f"r_coef{i}", [E, BANK], F32)) for i in range(4)]
        loaded = ctx.enter_context(nc.semaphore("r_loaded"))
        lower_made = ctx.enter_context(nc.semaphore("lower_made"))
        routed = ctx.enter_context(nc.semaphore("r_routed"))
        step = ctx.enter_context(nc.semaphore("r_step"))
        shifted = ctx.enter_context(nc.semaphore("r_shifted"))
        exped = ctx.enter_context(nc.semaphore("r_exp"))
        coef_ready = ctx.enter_context(nc.semaphore("coef_ready"))
        turned = ctx.enter_context(nc.semaphore("coef_turned"))
        block = ctx.enter_context(nc.Block())

        @block.sync
        def _(sp):
            sp.dma_start(rw[:, :, :], d.router_w_T.rearrange("(k p) e -> p k e", p=P)).then_inc(loaded, 16)
            sp.dma_start(rb[:, :], d.router_b.rearrange("(a e) -> a e", a=1).to_broadcast([P, E])).then_inc(loaded, 16)

        @block.gpsimd
        def _(pool):
            nc.gpsimd.memset(lower[:, :, :], 1.0).then_inc(lower_made, 1)
            pool.wait_ge(lower_made, 1)
            nc.gpsimd.affine_select(out=lower[:, :, :], in_=lower[:, :, :], compare_op=ALU.is_gt, fill=0.0,
                                    base=0, pattern=[[1, E], [-1, E]], channel_multiplier=0).then_inc(lower_made, 1)

        @block.tensor
        def _(pe):
            pe.wait_ge(loaded, 32)
            for t in range(TT):
                for k in range(KD):
                    last = nc.tensor.matmul(bank[:, t * E:(t + 1) * E], xn_T[:, k, t * P:(t + 1) * P], rw[:, k, :],
                                            start=(k == 0), stop=(k == KD - 1))
            last.then_inc(routed, 1)
            pe.wait_ge(coef_ready, 1)
            for t in range(TT):
                last = nc.tensor.transpose(coef_bank[t // 4][:, (t % 4) * P:(t % 4 + 1) * P], s.coef[:, t, :],
                                           s.ident[:, :])
            last.then_inc(turned, 1)

        @block.scalar
        def _(act):
            act.wait_ge(shifted, 1)
            nc.scalar.activation(ex[:, :, :], ex[:, :, :], ACT.Exp).then_inc(exped, 1)
            act.wait_ge(turned, 1)
            for i in range(4):
                nc.scalar.copy(s.coef_T[:, i * BANK:(i + 1) * BANK], coef_bank[i][:, :])

        @block.vector
        def _(dve):
            done = [0]

            def then(instruction):
                done[0] += 1
                instruction.then_inc(step, 1)
                dve.wait_ge(step, done[0])

            def over_experts(a):
                return a.rearrange("p t (e a) -> p t e a", a=1).to_broadcast([P, TT, E, E])

            def of_others(a):
                return a.rearrange("p t (a e) -> p t a e", a=1).to_broadcast([P, TT, E, E])

            per_token = top[:, :].rearrange("p (t a) -> p t a", a=1).to_broadcast([P, TT, E])
            dve.wait_ge(loaded, 32)
            dve.wait_ge(routed, 1)
            dve.wait_ge(lower_made, 2)
            then(nc.vector.tensor_tensor(logits[:, :, :], bank[:, :].rearrange("p (t e) -> p t e", e=E),
                                         rb[:, :].rearrange("p (a e) -> p a e", a=1).to_broadcast([P, TT, E]), ALU.add))
            then(nc.vector.tensor_reduce(top[:, :], logits[:, :, :], AX, ALU.max))
            nc.vector.tensor_tensor(ex[:, :, :], logits[:, :, :], per_token, ALU.subtract).then_inc(shifted, 1)
            nc.vector.tensor_tensor(before[:, :, :, :], of_others(logits[:, :, :]), over_experts(logits[:, :, :]), ALU.is_gt)
            then(nc.vector.tensor_tensor(same[:, :, :, :], of_others(logits[:, :, :]), over_experts(logits[:, :, :]),
                                         ALU.is_equal))
            then(nc.vector.tensor_tensor(same[:, :, :, :], same[:, :, :, :],
                                         lower[:, :, :].rearrange("p (a i) j -> p a i j", a=1)
                                         .to_broadcast([P, TT, E, E]), ALU.mult))
            then(nc.vector.tensor_tensor(before[:, :, :, :], before[:, :, :, :], same[:, :, :, :], ALU.add))
            then(nc.vector.tensor_reduce(rank[:, :, :], before[:, :, :, :], AX, ALU.add))
            dve.wait_ge(exped, 1)
            then(nc.vector.scalar_tensor_tensor(ex[:, :, :], rank[:, :, :], 1.5, ex[:, :, :], ALU.is_lt, ALU.mult))
            then(nc.vector.tensor_reduce(total[:, :], ex[:, :, :], AX, ALU.add))
            then(nc.vector.reciprocal(total[:, :], total[:, :]))
            nc.vector.tensor_tensor(s.coef[:, :, :], ex[:, :, :],
                                    total[:, :].rearrange("p (t a) -> p t a", a=1).to_broadcast([P, TT, E]),
                                    ALU.mult).then_inc(coef_ready, 1)


def experts(nc, d, s, xn_T):
    with ExitStack() as ctx:
        def sb(name, shape, dt=F32):
            return ctx.enter_context(nc.sbuf_tensor(name, shape, dt))

        def sem(name):
            return ctx.enter_context(nc.semaphore(name))

        NCH = TOK // BANK
        w1 = [sb(f"w1_{i}", [P, KD, FF]) for i in range(2)]
        w2 = [sb(f"w2_{i}", [P, KF, DIM]) for i in range(2)]
        b1 = sb("b1", [P, EXPERTS, KF])
        b2 = sb("b2", [EXPERTS, DIM])
        hidden = [sb(f"hidden{i}", [P, KF, BANK]) for i in range(2)]
        up = [ctx.enter_context(nc.psum_tensor(f"up{i}", [P, BANK], F32)) for i in range(4)]
        down = [ctx.enter_context(nc.psum_tensor(f"down{i}", [P, BANK], F32)) for i in range(4)]
        w_loaded = [sem(f"w_loaded{i}") for i in range(2)]
        b_loaded = sem("b_loaded")
        up_done, gelu_done, down_done, added = sem("up_done"), sem("gelu_done"), sem("down_done"), sem("e_added")
        block = ctx.enter_context(nc.Block())
        ROUNDS = EXPERTS * NCH

        @block.sync
        def _(sp):
            sp.dma_start(b1[:, :, :], d.b1.rearrange("e (k p) -> p e k", p=P), allow_slow_non_contiguous=True) \
                .then_inc(b_loaded, 16)
            sp.dma_start(b2[:, :], d.b2).then_inc(b_loaded, 16)
            for e in range(EXPERTS):
                if e >= 2:
                    sp.wait_ge(down_done, TT + 4 * NCH * (e - 1))
                sp.dma_start(w1[e % 2][:, :, :], d.w1_T[e].rearrange("(k p) f -> p k f", p=P)) \
                    .then_inc(w_loaded[e % 2], 16)
                sp.dma_start(w2[e % 2][:, :, :], d.w2_T[e].rearrange("(k p) n -> p k n", p=P)) \
                    .then_inc(w_loaded[e % 2], 16)

        @block.tensor
        def _(pe):
            pe.wait_ge(b_loaded, 32)
            n_down = 0
            for t in range(TT):
                if n_down >= 4:
                    pe.wait_ge(added, n_down - 3)
                nc.tensor.matmul(down[n_down % 4][:, 0:DIM], s.coef_T[:, t * P:(t + 1) * P], b2[:, :],
                                 start=True, stop=True).then_inc(down_done, 1)
                n_down += 1
            n_up = 0

            def finish(r):
                nonlocal n_down
                e = r // NCH
                for j in range(4):
                    pe.wait_ge(added, n_down - 3)
                    for f in range(KF):
                        if j == 0:
                            pe.wait_ge(gelu_done, r * KF + f + 1)
                        last = nc.tensor.matmul(down[n_down % 4][:, 0:DIM], hidden[r % 2][:, f, j * P:(j + 1) * P],
                                                w2[e % 2][:, f, :], start=(f == 0), stop=(f == KF - 1))
                    last.then_inc(down_done, 1)
                    n_down += 1

            for r in range(ROUNDS):
                e, c = divmod(r, NCH)
                if c == 0:
                    pe.wait_ge(w_loaded[e % 2], 32 * (e // 2 + 1))
                for f in range(KF):
                    if n_up >= 4:
                        pe.wait_ge(gelu_done, n_up - 3)
                    for k in range(KD):
                        last = nc.tensor.matmul(up[n_up % 4][:, :], w1[e % 2][:, k, f * P:(f + 1) * P],
                                                xn_T[:, k, c * BANK:(c + 1) * BANK], start=(k == 0), stop=(k == KD - 1))
                    last.then_inc(up_done, 1)
                    n_up += 1
                if r >= 1:
                    finish(r - 1)
            finish(ROUNDS - 1)

        @block.scalar
        def _(act):
            act.wait_ge(b_loaded, 32)
            for r in range(ROUNDS):
                e = r // NCH
                if r >= 2:
                    act.wait_ge(down_done, TT + 4 * (r - 1))
                for f in range(KF):
                    n = r * KF + f
                    act.wait_ge(up_done, n + 1)
                    nc.scalar.activation(hidden[r % 2][:, f, :], up[n % 4][:, :], ACT.Gelu, bias=b1[:, e, f:f + 1]) \
                        .then_inc(gelu_done, 1)

        @block.vector
        def _(dve):
            n = 0
            for t in range(TT):
                dve.wait_ge(down_done, n + 1)
                nc.vector.tensor_tensor(s.x_tok[:, t, :], s.x_tok[:, t, :], down[n % 4][:, 0:DIM], ALU.add) \
                    .then_inc(added, 1)
                n += 1
            for r in range(ROUNDS):
                e, c = divmod(r, NCH)
                for j in range(4):
                    t = 4 * c + j
                    dve.wait_ge(down_done, n + 1)
                    dve.wait_ge(added, n - TT + 1)
                    nc.vector.scalar_tensor_tensor(s.x_tok[:, t, :], down[n % 4][:, 0:DIM], s.coef[:, t, e:e + 1],
                                                   s.x_tok[:, t, :], ALU.mult, ALU.add).then_inc(added, 1)
                    n += 1


def store_result(nc, d, s):
    with ExitStack() as ctx:
        stored = ctx.enter_context(nc.semaphore("stored"))
        block = ctx.enter_context(nc.Block())

        @block.sync
        def _(sp):
            sp.dma_start(d.out.rearrange("(t p) n -> p t n", p=P), s.x_tok[:, :, :]).then_inc(stored, 16)
            sp.wait_ge(stored, 16)


def perceiver(nc, d):
    with ExitStack() as ctx:
        x_tok = ctx.enter_context(nc.sbuf_tensor("x_tok", [P, TT, DIM], F32))
        ident = ctx.enter_context(nc.sbuf_tensor("ident", [P, P], F32))
        with ExitStack() as inner:
            s = attention_memory(nc, inner)
            s.x_tok, s.ident = x_tok, ident
            load_constants(nc, d, s)
            with ExitStack() as first:
                xn_T = first.enter_context(nc.sbuf_tensor("xn_T1", [P, KD, TOK], F32))
                normalize_and_transpose(nc, "ln1", x_tok, xn_T, ident)
                project_queries(nc, d, s, xn_T)
            attention(nc, d, s)
        s = Names()
        s.x_tok, s.ident = x_tok, ident
        attention_output(nc, d, s)
        with ExitStack() as inner:
            def sb(name, shape):
                return inner.enter_context(nc.sbuf_tensor(name, shape, F32))

            s.a, s.dp = sb("a", [P, KI, STATE]), sb("dp", [P, KI])
            s.xs, s.delta, s.dtx = sb("xs", [P, KI, TOK]), sb("delta", [P, KI, TOK]), sb("dtx", [P, KI, TOK])
            with ExitStack() as first:
                xn_T = first.enter_context(nc.sbuf_tensor("xn_T2", [P, KD, TOK], F32))
                normalize_and_transpose(nc, "ln2", x_tok, xn_T, ident)
                ssm_projections(nc, d, s, xn_T)
            s.y = s.xs
            ssm_scan(nc, d, s)
            add_projection(nc, "wout", s, s.y, d.Wout, d.bout, KI)
        with ExitStack() as inner:
            xn_T = inner.enter_context(nc.sbuf_tensor("xn_T3", [P, KD, TOK], F32))
            s.coef = inner.enter_context(nc.sbuf_tensor("coef", [P, TT, EXPERTS], F32))
            s.coef_T = inner.enter_context(nc.sbuf_tensor("coef_T", [EXPERTS, TOK], F32))
            normalize_and_transpose(nc, "ln3", x_tok, xn_T, ident)
            route(nc, d, s, xn_T)
            experts(nc, d, s, xn_T)
        store_result(nc, d, s)


def laid_out(inputs):
    import numpy as np
    names = dict(W_Q="xattn_W_Q", b_Q="xattn_b_Q", W_K="xattn_W_K", b_K="xattn_b_K", W_V="xattn_W_V",
                 b_V="xattn_b_V", W_O="xattn_W_O", b_O="xattn_b_O", Win="attn_Win", bin="attn_bin", Wx="attn_Wx",
                 bx="attn_bx", Wdt="attn_Wdt", bdt="attn_bdt", A_log="attn_A_log", Dp="attn_Dp",
                 Wout="attn_Wout", bout="attn_bout", router_b="ffn_router_b", b1="ffn_b1", b2="ffn_b2")
    arrays = {k: np.asarray(inputs["L0_" + v]) for k, v in names.items()}
    arrays["x"] = np.asarray(inputs["x"]).reshape(TOK, DIM)
    arrays["ctx_T"] = np.asarray(inputs["ctx_1024"]).transpose(0, 2, 1)
    arrays["router_w_T"] = np.asarray(inputs["L0_ffn_router_w"]).T
    arrays["w1_T"] = np.asarray(inputs["L0_ffn_w1"]).transpose(0, 2, 1)
    arrays["w2_T"] = np.asarray(inputs["L0_ffn_w2"]).transpose(0, 2, 1)
    return {k: np.ascontiguousarray(v) for k, v in arrays.items()}


def build(nc, shapes):
    def array(name):
        return nc.dram_tensor(f"in_{name}", shapes[name], F32, kind="ExternalInput").ap()

    d = Names()
    d.x, d.ctx_T = array("x"), array("ctx_T")
    d.W_Q, d.b_Q, d.W_K, d.b_K = array("W_Q"), array("b_Q"), array("W_K"), array("b_K")
    d.W_V, d.b_V, d.W_O, d.b_O = array("W_V"), array("b_V"), array("W_O"), array("b_O")
    d.Win, d.bin, d.Wx, d.bx = array("Win"), array("bin"), array("Wx"), array("bx")
    d.Wdt, d.bdt, d.A_log, d.Dp = array("Wdt"), array("bdt"), array("A_log"), array("Dp")
    d.Wout, d.bout = array("Wout"), array("bout")
    d.router_w_T, d.router_b = array("router_w_T"), array("router_b")
    d.w1_T, d.b1, d.w2_T, d.b2 = array("w1_T"), array("b1"), array("w2_T"), array("b2")
    d.mixed = nc.dram_tensor("scratch_mixed", (BATCH, P, DIM), F32).ap()
    d.z = nc.dram_tensor("scratch_z", (KI, P, TOK), F32).ap()
    d.bc = nc.dram_tensor("scratch_bc", (2, STATE, TOK), F32).ap()
    d.out = nc.dram_tensor("out", (TOK, DIM), F32, kind="ExternalOutput").ap()
    perceiver(nc, d)


def kernel(**inputs):
    import concourse.bacc as bacc
    from concourse.bass_utils import run_bass_kernel_spmd

    nc = bacc.Bacc("TRN2", target_bir_lowering=False, num_devices=1)
    arrays = laid_out(inputs)
    build(nc, {k: a.shape for k, a in arrays.items()})
    r = run_bass_kernel_spmd(nc, [{f"in_{k}": a for k, a in arrays.items()}], core_ids=[0])
    return r.results[0]["out"].reshape(BATCH, LATENTS, DIM)
```

```python
import concourse.bass as bass
from concourse import mybir
from contextlib import ExitStack

F32 = mybir.dt.float32
F32R = mybir.dt.float32r
ACT = mybir.ActivationFunctionType
ALU = mybir.AluOpType
AX = mybir.AxisListType.X

P = 128
BATCH, LATENTS, DIM = 32, 64, 256
KEYS = 1601
TOK = BATCH * LATENTS
TT = TOK // P
KD = DIM // P
HEADS, HD = 16, 16
HPM = P // HD
BANK = 512
EPS = 1e-5
INNER, STATE, RANK = 512, 16, 16
KI = INNER // P
EXPERTS, FF = 8, 1024
KF = FF // P

CHUNKS = [(0, 512), (512, 512), (1024, 512), (1536, KEYS - 1536)]
TILES = [(s, min(P, KEYS - s)) for s in range(0, KEYS, P)]
NT = len(TILES)
KEYS_EVEN = KEYS + KEYS % 2
VW = HD + 1


class Names:
    pass


def even(n):
    return n + n % 2


def column_tiles(v):
    return v.rearrange("(m p) -> p m", p=P)


def normalize_and_transpose(nc, tag, x_tok, xn, xn_T, ident):
    with ExitStack() as ctx:
        stats = ctx.enter_context(nc.sbuf_tensor(f"{tag}_stats", [P, TT, 6], F32))
        mean_var = ctx.enter_context(nc.sbuf_tensor(f"{tag}_mean_var", [P, TT, 2], F32))
        rstd = ctx.enter_context(nc.sbuf_tensor(f"{tag}_rstd", [P, TT], F32))
        banks = [ctx.enter_context(nc.psum_tensor(f"{tag}_T{i}", [P, BANK], F32)) for i in range(4)]
        stats_ready = ctx.enter_context(nc.semaphore(f"{tag}_stats_ready"))
        rooted = ctx.enter_context(nc.semaphore(f"{tag}_rooted"))
        normed = ctx.enter_context(nc.semaphore(f"{tag}_normed"))
        transposed = ctx.enter_context(nc.semaphore(f"{tag}_transposed"))
        copied = ctx.enter_context(nc.semaphore(f"{tag}_copied"))
        block = ctx.enter_context(nc.Block())

        @block.vector
        def _(dve):
            for t in range(TT):
                nc.vector.bn_stats(stats[:, t, :], x_tok[:, t, :]).then_inc(stats_ready, 1)
            dve.wait_ge(stats_ready, TT)
            for t in range(TT):
                nc.vector.bn_aggr(mean_var[:, t, :], stats[:, t, :]).then_inc(stats_ready, 1)
            dve.wait_ge(stats_ready, 2 * TT)
            nc.vector.tensor_scalar(rstd[:, :], mean_var[:, :, 1], EPS, None, ALU.add).then_inc(stats_ready, 1)
            dve.wait_ge(rooted, 1)
            nc.vector.reciprocal(rstd[:, :], rstd[:, :]).then_inc(stats_ready, 1)
            dve.wait_ge(stats_ready, 2 * TT + 2)
            for t in range(TT):
                nc.vector.tensor_scalar(xn[:, t, :], x_tok[:, t, :], mean_var[:, t, 0:1], rstd[:, t:t + 1],
                                        ALU.subtract, ALU.mult).then_inc(normed, 1)

        @block.tensor
        def _(pe):
            n = 0
            for group in range(TT // 4):
                pe.wait_ge(normed, 4 * group + 4)
                for k in range(KD):
                    if n >= 4:
                        pe.wait_ge(copied, n - 3)
                    for j in range(4):
                        last = nc.tensor.transpose(banks[n % 4][:, j * P:(j + 1) * P],
                                                   xn[:, 4 * group + j, k * P:(k + 1) * P], ident[:, :])
                    last.then_inc(transposed, 1)
                    n += 1

        @block.scalar
        def _(act):
            act.wait_ge(stats_ready, 2 * TT + 1)
            nc.scalar.sqrt(rstd[:, :], rstd[:, :]).then_inc(rooted, 1)
            n = 0
            for group in range(TT // 4):
                for k in range(KD):
                    act.wait_ge(transposed, n + 1)
                    nc.scalar.copy(xn_T[:, k, group * BANK:(group + 1) * BANK], banks[n % 4][:, :]) \
                        .then_inc(copied, 1)
                    n += 1


def load_constants(nc, d, s):
    with ExitStack() as ctx:
        loaded = ctx.enter_context(nc.semaphore("constants_loaded"))
        filled = ctx.enter_context(nc.semaphore("constants_filled"))
        block = ctx.enter_context(nc.Block())

        @block.sync
        def _(sp):
            sp.dma_start(s.x_tok[:, :, :], d.x.rearrange("(t p) d -> p t d", p=P)).then_inc(loaded, 16)
            sp.wait_ge(loaded, 16)

        @block.gpsimd
        def _(pool):
            nc.gpsimd.memset(s.ident[:, :], 0.0).then_inc(filled, 1)
            pool.wait_ge(filled, 1)
            nc.gpsimd.affine_select(out=s.ident[:, :], in_=s.ident[:, :], compare_op=ALU.not_equal, fill=1.0,
                                    base=0, pattern=[[-1, P]], channel_multiplier=1).then_inc(filled, 1)


def project_queries(nc, d, s, xn_T):
    with ExitStack() as ctx:
        wq = ctx.enter_context(nc.sbuf_tensor("wq", [P, KD, DIM], F32))
        wk = ctx.enter_context(nc.sbuf_tensor("wk", [P, KD, DIM], F32))
        wv = ctx.enter_context(nc.sbuf_tensor("wv", [P, KD, DIM], F32))
        bq = ctx.enter_context(nc.sbuf_tensor("bq", [P, KD], F32))
        banks = [ctx.enter_context(nc.psum_tensor(f"q_bank{i}", [P, BANK], F32)) for i in range(4)]
        loaded = ctx.enter_context(nc.semaphore("q_loaded"))
        mask_made = ctx.enter_context(nc.semaphore("mask_made"))
        hi_made = ctx.enter_context(nc.semaphore("weights_hi_made"))
        projected = ctx.enter_context(nc.semaphore("q_projected"))
        copied = ctx.enter_context(nc.semaphore("q_copied"))
        block = ctx.enter_context(nc.Block())

        @block.sync
        def _(sp):
            for dst, src in ((wq, d.W_Q), (wk, d.W_K), (wv, d.W_V)):
                sp.dma_start(dst[:, :, :], src.rearrange("(k p) n -> p k n", p=P)).then_inc(loaded, 16)
            sp.dma_start(bq[:, :], column_tiles(d.b_Q), allow_slow_non_contiguous=True).then_inc(loaded, 16)
            sp.dma_start(s.bk[:, :], column_tiles(d.b_K), allow_slow_non_contiguous=True).then_inc(loaded, 16)

        @block.gpsimd
        def _(pool):
            nc.gpsimd.memset(s.head_mask[:, :], 1.0).then_inc(mask_made, 1)
            pool.wait_ge(mask_made, 1)
            nc.gpsimd.affine_select(out=s.head_mask[:, :], in_=s.head_mask[:, :], compare_op=ALU.is_ge,
                                    fill=0.0, base=0, pattern=[[-HD, HPM]], channel_multiplier=1) \
                .then_inc(mask_made, 1)
            pool.wait_ge(mask_made, 2)
            nc.gpsimd.affine_select(out=s.head_mask[:, :], in_=s.head_mask[:, :], compare_op=ALU.is_ge,
                                    fill=0.0, base=HD - 1, pattern=[[HD, HPM]], channel_multiplier=-1) \
                .then_inc(mask_made, 1)

        @block.vector
        def _(dve):
            dve.wait_ge(loaded, 80)
            nc.vector.tensor_copy(s.wk_hi[:, :, :], wk[:, :, :]).then_inc(hi_made, 1)
            nc.vector.tensor_copy(s.wv_hi[:, :, :], wv[:, :, :]).then_inc(hi_made, 1)
            dve.wait_ge(hi_made, 2)
            for lo, whole, hi in ((s.wk_lo, wk, s.wk_hi), (s.wv_lo, wv, s.wv_hi)):
                nc.vector.tensor_tensor(lo[:, :, :], whole[:, :, :], hi[:, :, :].bitcast(F32), ALU.subtract) \
                    .then_inc(hi_made, 1)
            for v in s.values:
                nc.vector.memset(v[:, :, :, HD:VW], 1.0)

        @block.tensor
        def _(pe):
            pe.wait_ge(loaded, 80)
            n = 0
            for m in range(KD):
                for c in range(TOK // BANK):
                    if n >= 4:
                        pe.wait_ge(copied, n - 3)
                    for k in range(KD):
                        last = nc.tensor.matmul(banks[n % 4][:, :], wq[:, k, m * P:(m + 1) * P],
                                                xn_T[:, k, c * BANK:(c + 1) * BANK],
                                                start=(k == 0), stop=(k == KD - 1))
                    last.then_inc(projected, 1)
                    n += 1

        @block.scalar
        def _(act):
            n = 0
            for m in range(KD):
                for c in range(TOK // BANK):
                    act.wait_ge(projected, n + 1)
                    nc.scalar.activation(s.q_T[:, m, c * BANK:(c + 1) * BANK], banks[n % 4][:, :], ACT.Identity,
                                         bias=bq[:, m:m + 1]).then_inc(copied, 1)
                    n += 1


UNITS = []
waiting = []
for c in range(len(CHUNKS)):
    for unit in [("k", m, c) for m in range(KD)] + [("v", j) for j in (2 * c, 2 * c + 1) if 2 * j < NT]:
        UNITS += [unit] + waiting[:2]
        waiting = waiting[2:]
    UNITS += waiting
    waiting = [("max", pair, c) for pair in range(HEADS // 2)]
UNITS += waiting
UNITS += [("row", m) for m in range(KD)]
WORK_BANKS = 3
NU = len(UNITS)
UNITS += [None] * (-NU % WORK_BANKS)
PLACES = 4
SPREAD = NU - KD
BESIDE = [[[u for u in range(SPREAD) if u * PLACES * (NT - 1) // SPREAD == t * PLACES + i] for i in range(PLACES)]
          for t in range(NT)]
BESIDE[-1][-1] = list(range(SPREAD, NU))
LAST_OF_CHUNK = [max(u for u in range(NU) if UNITS[u][0] == "v" and UNITS[u][1] // 2 == c)
                 for c in range(len(CHUNKS))]
CREDIT = 2


def attention(nc, d, s, batches=BATCH):
    with ExitStack() as ctx:
        def sb(name, shape, dt=F32):
            return ctx.enter_context(nc.sbuf_tensor(name, shape, dt))

        def sem(name):
            return ctx.enter_context(nc.semaphore(name))

        ctx_hi = [sb(f"ctx_hi{i}", [P, KD, BANK], F32R) for i in range(2)]
        ctx_lo = [sb(f"ctx_lo{i}", [P, KD, BANK], F32R) for i in range(2)]
        k_hi = [sb(f"k_hi{i}", [P, KD, KEYS_EVEN], F32R) for i in range(2)]
        k_lo = [sb(f"k_lo{i}", [P, KD, KEYS_EVEN], F32R) for i in range(2)]
        q_whole = sb("q_whole", [P, KD, HPM * LATENTS])
        q_hi = [sb(f"q_hi{i}", [P, KD, HPM * LATENTS], F32R) for i in range(2)]
        q_lo = [sb(f"q_lo{i}", [P, KD, HPM * LATENTS], F32R) for i in range(2)]
        max_part = [sb(f"max_part{i}", [P, HEADS // 2, len(CHUNKS)]) for i in range(2)]
        neg_max = [sb(f"neg_max{i}", [P, HEADS // 2]) for i in range(2)]
        max_all = [sb(f"max_all{i}", [P, KD, BANK]) for i in range(2)]
        probs = [sb(f"probs{i}", [P, HEADS * LATENTS]) for i in range(2)]
        mixed = [sb(f"mixed{i}", [P, 4 * LATENTS]) for i in range(2)]
        work = [ctx.enter_context(nc.psum_tensor(f"work{i}", [P, BANK], F32)) for i in range(WORK_BANKS)]
        scores = [ctx.enter_context(nc.psum_tensor(f"scores{i}", [P, KD * BANK], F32)) for i in range(2)]
        acc = ctx.enter_context(nc.psum_tensor("acc", [P, BANK], F32))

        ctx_loaded = [sem(f"ctx_loaded{i}") for i in range(2)]
        hi_split = sem("hi_split")
        lo_split = sem("lo_split")
        unit_done = sem("unit_done")
        key_hi_done = sem("key_hi_done")
        unit_evacuated = sem("unit_evacuated")
        values_copied = sem("values_copied")
        maxima_done = sem("maxima_done")
        q_masked = sem("q_masked")
        q_split = sem("q_split")
        scores_ready = sem("scores_ready")
        scores_shifted = sem("scores_shifted")
        exp_done = sem("exp_done")
        probs_used = sem("probs_used")
        acc_copied = sem("acc_copied")
        mixed_stored = [sem(f"mixed_stored{i}") for i in range(2)]
        block = ctx.enter_context(nc.Block())

        NC = len(CHUNKS)
        n_v = sum(u is not None and u[0] == "v" for u in UNITS)
        pairs = (batches - 1) // 2

        def wait_evacuated(engine, b, u):
            of_engine = [i for i in range(NU) if (UNITS[i][0] == "v") == (UNITS[u][0] == "v")]
            engine.wait_ge(values_copied if UNITS[u][0] == "v" else unit_evacuated,
                           b * len(of_engine) + of_engine.index(u) + 1)

        @block.sync
        def _(sp):
            def load(b):
                for c, (start, size) in enumerate(CHUNKS):
                    g = b * NC + c
                    if not isinstance(b, int) or g >= 2:
                        sp.wait_ge(lo_split, g - 1)
                    sp.dma_start(s.ctx_whole[c % 2][:, :, 0:size],
                                 d.ctx_T[bass.ds(b, 1), :, start:start + size]
                                 .rearrange("a (k p) s -> p (a k) s", p=P)).then_inc(ctx_loaded[c % 2], 16)

            load(0)
            with sp.Fori(1, batches) as b:
                load(b)

        @block.gpsimd
        def _(pool):
            def mask_queries(b, par, tokens):
                if not isinstance(b, int) or b >= 1:
                    pool.wait_ge(probs_used, (b - 1) * NT + CREDIT)
                    pool.wait_ge(q_split, b)
                for m in range(KD):
                    q = tokens[:, m, :].rearrange("p (a l) -> p a l", a=1).to_broadcast([P, HPM, LATENTS])
                    mask = s.head_mask[:, :].rearrange("p (h a) -> p h a", a=1).to_broadcast([P, HPM, LATENTS])
                    nc.gpsimd.tensor_tensor(q_whole[:, m, :].rearrange("p (h l) -> p h l", h=HPM), q, mask,
                                            ALU.mult).then_inc(q_masked, 1)
                    nc.gpsimd.tensor_tensor(q_hi[par][:, m, :].rearrange("p (h l) -> p h l", h=HPM), q, mask,
                                            ALU.mult).then_inc(q_masked, 1)
                pool.wait_ge(q_masked, (b + 1) * 2 * KD)
                nc.gpsimd.tensor_tensor(q_lo[par][:, :, :], q_whole[:, :, :], q_hi[par][:, :, :].bitcast(F32),
                                        ALU.subtract).then_inc(q_split, 1)

            def split(b, c):
                n = even(CHUNKS[c][1])
                pool.wait_ge(hi_split, b * NC + c + 1)
                nc.gpsimd.tensor_tensor(ctx_lo[c % 2][:, :, 0:n], s.ctx_whole[c % 2][:, :, 0:n],
                                        ctx_hi[c % 2][:, :, 0:n].bitcast(F32), ALU.subtract).then_inc(lo_split, 1)

            def prepare(b, par, more=True):
                mask_queries(b, par, s.q_T[:, :, bass.ds(b * LATENTS, LATENTS)])
                for c in range(2, NC):
                    split(b, c)
                if more:
                    for c in range(2):
                        split(b + 1, c)

            split(0, 0)
            split(0, 1)
            prepare(0, 0)
            if pairs:
                with pool.Fori(0, pairs) as i:
                    prepare(i * 2 + 1, 1)
                    prepare(i * 2 + 2, 0)
            prepare(batches - 1, 1, more=False)

        @block.vector
        def _(dve):
            def split(b, c):
                g = b * NC + c
                n = even(CHUNKS[c][1])
                dve.wait_ge(ctx_loaded[c % 2], (b * (NC // 2) + c // 2 + 1) * 16)
                if not isinstance(b, int) or g >= 2:
                    before = LAST_OF_CHUNK[c - 2] + (NU if c >= 2 else 0)
                    dve.wait_ge(unit_done, (b - 1) * NU + before + 1)
                nc.vector.tensor_copy(ctx_hi[c % 2][:, :, 0:n], s.ctx_whole[c % 2][:, :, 0:n]) \
                    .then_inc(hi_split, 1)

            def unit(b, par, u):
                kind = UNITS[u][0]
                dve.wait_ge(unit_done, b * NU + u + 1)
                bank = work[u % WORK_BANKS]
                if kind == "k":
                    _, m, c = UNITS[u]
                    start, size = CHUNKS[c]
                    n = even(size)
                    dve.wait_ge(key_hi_done, b * KD * NC + c * KD + m + 1)
                    nc.vector.scalar_tensor_tensor(k_lo[par][:, m, start:start + n], bank[:, 0:n], s.bk[:, m:m + 1],
                                                   k_hi[par][:, m, start:start + n].bitcast(F32),
                                                   ALU.add, ALU.subtract).then_inc(unit_evacuated, 1)
                elif kind == "max":
                    _, pair, c = UNITS[u]
                    nc.vector.reduce_max(max_part[par][:, pair, c:c + 1], bank[:, 0:CHUNKS[c][1]], AX) \
                        .then_inc(unit_evacuated, 1)
                    if u == SPREAD - 1:
                        wait_evacuated(dve, b, u)
                        nc.vector.tensor_reduce(neg_max[par][:, :], max_part[par][:, :, :], AX, ALU.max, negate=True) \
                            .then_inc(maxima_done, 1)
                else:
                    nc.vector.tensor_copy(max_all[par][:, UNITS[u][1], :], bank[:, :]).then_inc(unit_evacuated, 1)

            def prepare(b, par, units, more):
                for u in units:
                    if UNITS[u][0] != "v":
                        unit(b, par, u)
                    if u in LAST_OF_CHUNK:
                        c = LAST_OF_CHUNK.index(u) + 2
                        if c < NC:
                            split(b, c)
                        elif more:
                            split(b + 1, c - NC)

            def shift(b, par, t):
                n = b * NT + t
                rows = TILES[t][1]
                bank = scores[(par * NT + t) % 2][0:rows, :]
                dve.wait_ge(scores_ready, n + 1)
                nc.vector.tensor_tensor(bank, bank, max_all[par][0:rows, :, :].rearrange("p m n -> p (m n)"),
                                        ALU.add).then_inc(scores_shifted, 1)

            def attend(b, par, ahead, more=True):
                wait_evacuated(dve, b, NU - 1)
                shift(b, par, 0)
                for t in range(NT):
                    for place in range(PLACES):
                        if place == 1 and t + 1 < NT:
                            shift(b, par, t + 1)
                        if ahead:
                            prepare(b + 1, 1 - par, BESIDE[t][place], more)

            nc.vector.memset(acc[:, :], 0.0)
            split(0, 0)
            split(0, 1)
            prepare(0, 0, range(NU), True)
            if pairs:
                with dve.Fori(0, pairs) as i:
                    attend(i * 2, 0, True)
                    attend(i * 2 + 1, 1, True)
            attend(batches - 2, 0, True, more=False)
            attend(batches - 1, 1, False)

        @block.scalar
        def _(act):
            def unit(b, par, u):
                if UNITS[u][0] == "k":
                    _, m, c = UNITS[u]
                    start, size = CHUNKS[c]
                    n = even(size)
                    act.wait_ge(unit_done, b * NU + u + 1)
                    nc.scalar.activation(k_hi[par][:, m, start:start + n], work[u % WORK_BANKS][:, 0:n],
                                         ACT.Identity, bias=s.bk[:, m:m + 1]).then_inc(key_hi_done, 1)
                elif UNITS[u][0] == "v":
                    j = UNITS[u][1]
                    tiles = min(2, NT - 2 * j)
                    rows = TILES[2 * j][1]
                    act.wait_ge(unit_done, b * NU + u + 1)
                    nc.scalar.copy(
                        s.values[par][0:rows, 2 * j:2 * j + tiles, :, 0:HD],
                        work[u % WORK_BANKS][0:rows, 0:tiles * DIM].rearrange("p (t h e) -> p t h e", t=tiles, h=HEADS)) \
                        .then_inc(values_copied, 1)

            def attend(b, par, ahead):
                for t in range(NT):
                    n = b * NT + t
                    slot = (par * NT + t) % 2
                    rows = TILES[t][1]
                    act.wait_ge(scores_shifted, n + 1)
                    act.wait_ge(probs_used, n + 1)
                    nc.scalar.activation(probs[slot][0:rows, :], scores[slot][0:rows, :], ACT.Exp,
                                         scale=1.0 / HD ** 0.5).then_inc(exp_done, 1)
                    if ahead:
                        for units in BESIDE[t]:
                            for u in units:
                                unit(b + 1, 1 - par, u)
                act.wait_ge(probs_used, b * NT + NT + CREDIT)
                act.wait_ge(mixed_stored[par], (b - par) * 8)
                nc.scalar.copy(mixed[par][:, :], acc[:, par * DIM:(par + 1) * DIM]).then_inc(acc_copied, 1)
                act.wait_ge(acc_copied, b + 1 + CREDIT)
                act.dma_start(d.mixed[bass.ds(b, 1), :, :].rearrange("a p n -> p a n"),
                              mixed[par][:, :].rearrange("p (a n) -> p a n", a=1)).then_inc(mixed_stored[par], 16)

            act.sem_inc(exp_done, CREDIT)
            act.sem_inc(acc_copied, CREDIT)
            for u in range(NU):
                unit(0, 0, u)
            if pairs:
                with act.Fori(0, pairs) as i:
                    attend(i * 2, 0, True)
                    attend(i * 2 + 1, 1, True)
            attend(batches - 2, 0, True)
            attend(batches - 1, 1, False)
            for par in range(2):
                act.wait_ge(mixed_stored[par], 16 * (batches // 2))

        @block.tensor
        def _(pe):
            def unit(b, par, u):
                if UNITS[u] is None:
                    return
                kind = UNITS[u][0]
                bank = work[u % WORK_BANKS]
                if not isinstance(b, int) or b * NU + u - WORK_BANKS >= 0:
                    if u >= WORK_BANKS:
                        wait_evacuated(pe, b, u - WORK_BANKS)
                    else:
                        wait_evacuated(pe, b - 1, min(u + len(UNITS) - WORK_BANKS, NU - 1))
                if kind == "k":
                    _, m, c = UNITS[u]
                    n = even(CHUNKS[c][1])
                    if m == 0:
                        pe.wait_ge(lo_split, b * NC + c + 1)
                    cols = slice(m * P, (m + 1) * P)
                    parts = [(w, x, k) for w, x in ((s.wk_hi, ctx_hi), (s.wk_hi, ctx_lo), (s.wk_lo, ctx_hi))
                             for k in range(KD)]
                    for i, (w, x, k) in enumerate(parts):
                        last = nc.tensor.matmul(bank[:, 0:n], w[:, k, cols], x[c % 2][:, k, 0:n],
                                                start=(i == 0), stop=(i == len(parts) - 1))
                elif kind == "v":
                    j = UNITS[u][1]
                    c = j // 2
                    for i, t in enumerate(range(2 * j, min(2 * j + 2, NT))):
                        start, rows = TILES[t]
                        at = start - CHUNKS[c][0]
                        parts = [(x, w, k) for k in range(KD)
                                 for x, w in ((ctx_hi, s.wv_hi), (ctx_hi, s.wv_lo), (ctx_lo, s.wv_hi))]
                        for n, (x, w, k) in enumerate(parts):
                            last = nc.tensor.matmul(bank[0:rows, i * DIM:(i + 1) * DIM],
                                                    x[c % 2][:, k, at:at + rows], w[:, k, :],
                                                    start=(n == 0), stop=(n == len(parts) - 1))
                elif kind == "max":
                    _, pair, c = UNITS[u]
                    start, size = CHUNKS[c]
                    if pair == 0:
                        pe.wait_ge(q_split, b + 1)
                        wait_evacuated(pe, b, UNITS.index(("k", KD - 1, c)))
                    m, at = pair // 4, (pair % 4) * P
                    last = nc.tensor.matmul(bank[:, 0:even(size)], q_hi[par][:, m, at:at + P],
                                            k_hi[par][:, m, start:start + even(size)], start=True, stop=True)
                else:
                    m = UNITS[u][1]
                    pe.wait_ge(maxima_done, b + 1)
                    for j in range(4):
                        last = nc.tensor.matmul(bank[:, j * P:(j + 1) * P],
                                                neg_max[par][:, 4 * m + j:4 * m + j + 1].to_broadcast([P, P]),
                                                s.ident[:, :], start=True, stop=True)
                last.then_inc(unit_done, 1)

            def score(b, par, t, m):
                start, rows = TILES[t]
                bank = scores[(par * NT + t) % 2]
                if m == 0:
                    pe.wait_ge(exp_done, b * NT + t + 1)
                    if t == 0:
                        wait_evacuated(pe, b, UNITS.index(("k", KD - 1, NC - 1)))
                cols = slice(m * BANK, (m + 1) * BANK)
                keys = slice(start, start + rows)
                for i, (k, q) in enumerate(((k_hi, q_hi), (k_hi, q_lo), (k_lo, q_hi))):
                    last = nc.tensor.matmul(bank[0:rows, cols], k[par][:, m, keys], q[par][:, m, :],
                                            start=(i == 0), stop=(i == 2))
                if m == KD - 1:
                    last.then_inc(scores_ready, 1)

            def mix(b, par, t, half):
                rows = TILES[t][1]
                if half == 0:
                    pe.wait_ge(exp_done, b * NT + t + 1 + CREDIT)
                if half == 0 and t == 0:
                    pe.wait_ge(acc_copied, b + 1)
                    wait_evacuated(pe, b, max(u for u in range(NU) if UNITS[u][0] == "v"))
                p = probs[(par * NT + t) % 2]
                for g in range(2 * half, 2 * half + 2):
                    for j in range(4):
                        h = 4 * g + j
                        last = nc.tensor.matmul(
                            acc[32 * j:32 * j + VW, par * DIM + g * LATENTS:par * DIM + (g + 1) * LATENTS],
                            s.values[par][0:rows, t, h, :], p[0:rows, h * LATENTS:(h + 1) * LATENTS],
                            start=(t == 0 and g == 0), stop=(t == NT - 1), skip_group_check=True)
                if half == 1:
                    last.then_inc(probs_used, 1)

            def attend(b, par, ahead):
                for t in range(NT):
                    for place in range(PLACES):
                        if place < 2:
                            if t + 1 < NT:
                                score(b, par, t + 1, place)
                            elif ahead:
                                score(b + 1, 1 - par, 0, place)
                        else:
                            mix(b, par, t, place - 2)
                        if ahead:
                            for u in BESIDE[t][place]:
                                unit(b + 1, 1 - par, u)

            pe.sem_inc(probs_used, CREDIT)
            for u in range(NU):
                unit(0, 0, u)
            score(0, 0, 0, 0)
            score(0, 0, 0, 1)
            if pairs:
                with pe.Fori(0, pairs) as i:
                    attend(i * 2, 0, True)
                    attend(i * 2 + 1, 1, True)
            attend(batches - 2, 0, True)
            attend(batches - 1, 1, False)


def attention_memory(nc, ctx):
    def sb(name, shape, dt=F32):
        return ctx.enter_context(nc.sbuf_tensor(name, shape, dt))
    s = Names()
    s.q_T, s.head_mask, s.bk = sb("q_T", [P, KD, TOK]), sb("head_mask", [P, HPM]), sb("bk", [P, KD])
    s.wk_hi, s.wk_lo = sb("wk_hi", [P, KD, DIM], F32R), sb("wk_lo", [P, KD, DIM], F32R)
    s.wv_hi, s.wv_lo = sb("wv_hi", [P, KD, DIM], F32R), sb("wv_lo", [P, KD, DIM], F32R)
    s.ctx_whole = [sb(f"ctx_whole{i}", [P, KD, BANK]) for i in range(2)]
    s.values = [sb(f"values{i}", [P, NT, HEADS, VW]) for i in range(2)]
    return s


def attention_output(nc, d, s):
    with ExitStack() as ctx:
        def sb(name, shape, dt=F32):
            return ctx.enter_context(nc.sbuf_tensor(name, shape, dt))

        G = HEADS // 4
        mixed = sb("mixed_T", [P, G, TOK])
        wo = sb("wo", [P, G, DIM])
        bv = sb("bv", [P, G])
        bo = sb("bo", [P, DIM])
        pick = sb("pick", [P, 4, 32])
        inverse = [sb(f"inverse{i}", [P, BANK]) for i in range(2)]
        sums = [ctx.enter_context(nc.psum_tensor(f"o_sums{i}", [P, BANK], F32)) for i in range(4)]
        outs = [ctx.enter_context(nc.psum_tensor(f"o_outs{i}", [P, BANK], F32)) for i in range(4)]
        loaded = ctx.enter_context(nc.semaphore("o_loaded"))
        cleared = ctx.enter_context(nc.semaphore("o_cleared"))
        pick_made = ctx.enter_context(nc.semaphore("pick_made"))
        summed = ctx.enter_context(nc.semaphore("o_summed"))
        inverted = ctx.enter_context(nc.semaphore("o_inverted"))
        divided = ctx.enter_context(nc.semaphore("o_divided"))
        biased = ctx.enter_context(nc.semaphore("o_biased"))
        projected = ctx.enter_context(nc.semaphore("o_projected"))
        added = ctx.enter_context(nc.semaphore("o_added"))
        block = ctx.enter_context(nc.Block())
        NCH = TOK // BANK

        @block.sync
        def _(sp):
            for g in range(G):
                sp.dma_start(mixed[:, g, :].rearrange("p (b l) -> p b l", b=BATCH),
                             d.mixed.rearrange("b p (g l) -> g p b l", g=G)[g]).then_inc(loaded, 16)
            sp.dma_start(bo[:, :], d.b_O.rearrange("(a n) -> a n", a=1).to_broadcast([P, DIM])).then_inc(loaded, 16)
            sp.wait_ge(cleared, 2)
            for j in range(4):
                rows = slice(32 * j, 32 * j + HD)
                sp.dma_start(wo[rows, :, :], d.W_O.rearrange("(g c e) n -> c e g n", c=4, e=HD)[j]) \
                    .then_inc(loaded, 16)
                sp.dma_start(bv[rows, :], d.b_V.rearrange("(g c e) -> c e g", c=4, e=HD)[j],
                             allow_slow_non_contiguous=True).then_inc(loaded, 16)

        @block.gpsimd
        def _(pool):
            nc.gpsimd.memset(wo[:, :, :], 0.0).then_inc(cleared, 1)
            nc.gpsimd.memset(bv[:, :], 0.0).then_inc(cleared, 1)
            nc.gpsimd.memset(pick[:, :, :], 0.0).then_inc(pick_made, 1)
            pool.wait_ge(pick_made, 1)
            nc.gpsimd.affine_select(out=pick[:, :, :], in_=pick[:, :, :], compare_op=ALU.not_equal, fill=1.0,
                                    base=-HD, pattern=[[-32, 4], [0, 32]], channel_multiplier=1) \
                .then_inc(pick_made, 1)

        @block.tensor
        def _(pe):
            pe.wait_ge(loaded, 16 * (G + 1 + 8))
            pe.wait_ge(pick_made, 2)
            n = 0
            for c in range(NCH):
                for g in range(G):
                    if n >= 4:
                        pe.wait_ge(inverted, n - 3)
                    nc.tensor.matmul(sums[n % 4][:, :], pick[:, :, :].rearrange("p j i -> p (j i)"),
                                     mixed[:, g, c * BANK:(c + 1) * BANK], start=True, stop=True) \
                        .then_inc(summed, 1)
                    n += 1
            for t in range(TT):
                pe.wait_ge(biased, G * (t // 4) + G)
                if t >= 4:
                    pe.wait_ge(added, t - 3)
                for g in range(G):
                    last = nc.tensor.matmul(outs[t % 4][:, 0:DIM], mixed[:, g, t * P:(t + 1) * P], wo[:, g, :],
                                            start=(g == 0), stop=(g == G - 1))
                last.then_inc(projected, 1)

        @block.scalar
        def _(act):
            for n in range(NCH * G):
                c, g = divmod(n, G)
                act.wait_ge(divided, n + 1)
                part = mixed[:, g, c * BANK:(c + 1) * BANK]
                nc.scalar.activation(part, part, ACT.Identity, bias=bv[:, g:g + 1]).then_inc(biased, 1)

        @block.vector
        def _(dve):
            for n in range(NCH * G):
                c, g = divmod(n, G)
                dve.wait_ge(summed, n + 1)
                nc.vector.reciprocal(inverse[n % 2][:, :], sums[n % 4][:, :]).then_inc(inverted, 1)
                dve.wait_ge(inverted, n + 1)
                part = mixed[:, g, c * BANK:(c + 1) * BANK]
                nc.vector.tensor_tensor(part, part, inverse[n % 2][:, :], ALU.mult).then_inc(divided, 1)
            for t in range(TT):
                dve.wait_ge(projected, t + 1)
                nc.vector.tensor_tensor(s.x_tok[:, t, :], s.x_tok[:, t, :], outs[t % 4][:, 0:DIM], ALU.add) \
                    .then_inc(added, 1)
            dve.wait_ge(added, TT)
            for t in range(TT):
                nc.vector.tensor_tensor(s.x_tok[:, t, :], s.x_tok[:, t, :], bo[:, :], ALU.add)


HALF = 1024
BC_COLS = 96


def ssm_projections(nc, d, s, xn_T):
    with ExitStack() as ctx:
        def sb(name, shape, dt=F32):
            return ctx.enter_context(nc.sbuf_tensor(name, shape, dt))

        def sem(name):
            return ctx.enter_context(nc.semaphore(name))

        win = sb("win", [P, KD, 2 * INNER])
        bin_ = sb("bin", [P, 2 * KI])
        wx = sb("wx", [P, KI, BC_COLS])
        bx = sb("bx", [BC_COLS, 1])
        wdt = sb("wdt", [RANK, INNER])
        bdt = sb("bdt", [P, KI])
        xp = sb("xp", [BC_COLS, TOK])
        z = [sb(f"z{i}", [P, BANK]) for i in range(2)]
        raw = [sb(f"raw{i}", [P, BANK]) for i in range(2)]
        decay = [sb(f"decay{i}", [P, BANK]) for i in range(2)]
        log = [sb(f"log{i}", [P, BANK]) for i in range(2)]
        banks = [ctx.enter_context(nc.psum_tensor(f"s_bank{i}", [P, BANK], F32)) for i in range(4)]
        loaded, cleared = sem("s_loaded"), sem("s_cleared")
        projected, gated = sem("s_projected"), sem("s_gated")
        z_stored = [sem(f"z_stored{i}") for i in range(2)]
        xp_projected, xp_copied, bc_stored = sem("xp_projected"), sem("xp_copied"), sem("bc_stored")
        dt_projected, dt_raw, dt_abs, dt_exp, dt_log, dt_steps = (
            sem("dt_projected"), sem("dt_raw"), sem("dt_abs"), sem("dt_exp"), sem("dt_log"), sem("dt_steps"))
        block = ctx.enter_context(nc.Block())
        NCH = TOK // BANK

        @block.sync
        def _(sp):
            sp.dma_start(win[:, :, :], d.Win.rearrange("(k p) n -> p k n", p=P)).then_inc(loaded, 16)
            sp.dma_start(bin_[:, :], column_tiles(d.bin), allow_slow_non_contiguous=True).then_inc(loaded, 16)
            sp.dma_start(wdt[:, :], d.Wdt).then_inc(loaded, 16)
            sp.dma_start(bdt[:, :], column_tiles(d.bdt), allow_slow_non_contiguous=True).then_inc(loaded, 16)
            sp.dma_start(s.dp[:, :], column_tiles(d.Dp), allow_slow_non_contiguous=True).then_inc(loaded, 16)
            sp.dma_start(s.a[:, :, :], d.A_log.rearrange("(k p) n -> p k n", p=P)).then_inc(loaded, 16)
            sp.wait_ge(cleared, 2)
            wx_v = d.Wx.rearrange("(k p) n -> p k n", p=P)
            bx_v = d.bx.rearrange("(p a) -> p a", a=1)
            for i in range(3):
                sp.dma_start(wx[:, :, 32 * i:32 * i + STATE], wx_v[:, :, STATE * i:STATE * (i + 1)]) \
                    .then_inc(loaded, 16)
                sp.dma_start(bx[32 * i:32 * i + STATE, :], bx_v[STATE * i:STATE * (i + 1), :]).then_inc(loaded, 16)
            for n in range(KI * NCH):
                m, c = divmod(n, NCH)
                sp.wait_ge(gated, (KI + m) * NCH + c + 1)
                sp.dma_start(d.z[m, :, c * BANK:(c + 1) * BANK], z[n % 2][:, :]).then_inc(z_stored[n % 2], 16)
            sp.wait_ge(xp_copied, NCH)
            for i in range(2):
                sp.dma_start(d.bc[i, :, :], xp[32 * (i + 1):32 * (i + 1) + STATE, :]).then_inc(bc_stored, 16)
            for i in range(2):
                sp.wait_ge(z_stored[i], 16 * KI * NCH // 2)
            sp.wait_ge(bc_stored, 32)

        @block.gpsimd
        def _(pool):
            nc.gpsimd.memset(wx[:, :, :], 0.0).then_inc(cleared, 1)
            nc.gpsimd.memset(bx[:, :], 0.0).then_inc(cleared, 1)

        @block.tensor
        def _(pe):
            pe.wait_ge(loaded, 16 * 12)
            n = 0
            for m in range(2 * KI):
                for c in range(NCH):
                    if n >= 4:
                        pe.wait_ge(gated, n - 3)
                    for k in range(KD):
                        last = nc.tensor.matmul(banks[n % 4][:, :], win[:, k, m * P:(m + 1) * P],
                                                xn_T[:, k, c * BANK:(c + 1) * BANK],
                                                start=(k == 0), stop=(k == KD - 1))
                    last.then_inc(projected, 1)
                    n += 1
            for c in range(NCH):
                pe.wait_ge(gated, n - 3 + c)
                for k in range(KI):
                    last = nc.tensor.matmul(banks[c][0:BC_COLS, :], wx[:, k, :], s.xs[:, k, c * BANK:(c + 1) * BANK],
                                            start=(k == 0), stop=(k == KI - 1))
                last.then_inc(xp_projected, 1)
            pe.wait_ge(xp_copied, NCH)
            n = 0
            for m in range(KI):
                for c in range(NCH):
                    if n >= 4:
                        pe.wait_ge(dt_raw, n - 3)
                    nc.tensor.matmul(banks[n % 4][:, :], wdt[:, m * P:(m + 1) * P], xp[0:RANK, c * BANK:(c + 1) * BANK],
                                     start=True, stop=True).then_inc(dt_projected, 1)
                    n += 1

        @block.scalar
        def _(act):
            act.wait_ge(loaded, 16 * 12)
            for n in range(2 * KI * NCH):
                m, c = divmod(n, NCH)
                act.wait_ge(projected, n + 1)
                if m < KI:
                    out = s.xs[:, m, c * BANK:(c + 1) * BANK]
                else:
                    i = n - KI * NCH
                    out = z[i % 2][:, :]
                    if i >= 2:
                        act.wait_ge(z_stored[i % 2], 16 * (i // 2))
                nc.scalar.activation(out, banks[n % 4][:, :], ACT.Silu, bias=bin_[:, m:m + 1]).then_inc(gated, 1)
            for c in range(NCH):
                act.wait_ge(xp_projected, c + 1)
                nc.scalar.activation(xp[:, c * BANK:(c + 1) * BANK], banks[c][0:BC_COLS, :], ACT.Identity,
                                     bias=bx[:, 0:1]).then_inc(xp_copied, 1)
            nc.scalar.activation(s.a[:, :, :], s.a[:, :, :], ACT.Exp)
            for n in range(KI * NCH):
                act.wait_ge(dt_abs, n + 1)
                if n >= 2:
                    act.wait_ge(dt_steps, 4 * (n - 1))
                nc.scalar.activation(decay[n % 2][:, :], decay[n % 2][:, :], ACT.Exp).then_inc(dt_exp, 1)
                act.wait_ge(dt_exp, n + 1)
                nc.scalar.activation(log[n % 2][:, :], decay[n % 2][:, :], ACT.Ln, bias=1.0).then_inc(dt_log, 1)

        @block.vector
        def _(dve):
            for n in range(KI * NCH):
                m, c = divmod(n, NCH)
                cols = slice(c * BANK, (c + 1) * BANK)
                e, v, l = decay[n % 2][:, :], raw[n % 2][:, :], log[n % 2][:, :]
                dve.wait_ge(dt_projected, n + 1)
                nc.vector.tensor_scalar(v, banks[n % 4][:, :], bdt[:, m:m + 1], None, ALU.add).then_inc(dt_raw, 1)
                dve.wait_ge(dt_raw, n + 1)
                nc.vector.scalar_tensor_tensor(e, v, -1.0, v, ALU.mult, ALU.min).then_inc(dt_abs, 1)
                dve.wait_ge(dt_log, n + 1)
                delta = s.delta[:, m, cols]
                steps = 4 * n
                nc.vector.tensor_scalar(delta, e, 1.0, -1.0, ALU.add, ALU.add).then_inc(dt_steps, 1)
                dve.wait_ge(dt_steps, steps + 1)
                nc.vector.tensor_tensor(e, e, delta, ALU.subtract).then_inc(dt_steps, 1)
                nc.vector.scalar_tensor_tensor(l, v, 0.0, l, ALU.max, ALU.add).then_inc(dt_steps, 1)
                dve.wait_ge(dt_steps, steps + 3)
                nc.vector.tensor_tensor(delta, l, e, ALU.add).then_inc(dt_steps, 1)
                dve.wait_ge(dt_steps, steps + 4)
                nc.vector.tensor_tensor(s.dtx[:, m, cols], delta, s.xs[:, m, cols], ALU.mult)


def ssm_scan(nc, d, s):
    with ExitStack() as ctx:
        def sb(name, shape, dt=F32):
            return ctx.enter_context(nc.sbuf_tensor(name, shape, dt))

        def sem(name):
            return ctx.enter_context(nc.semaphore(name))

        b_all = [sb(f"b_all{i}", [P, HALF]) for i in range(2)]
        c_all = [sb(f"c_all{i}", [P, HALF]) for i in range(2)]
        da = [sb(f"da{i}", [P, HALF]) for i in range(2)]
        dbx = [sb(f"dbx{i}", [P, HALF]) for i in range(2)]
        h = [sb(f"h{i}", [P, HALF]) for i in range(2)]
        hc = [sb(f"hc{i}", [P, HALF]) for i in range(2)]
        z = [sb(f"zg{i}", [P, HALF]) for i in range(2)]
        y = [ctx.enter_context(nc.psum_tensor(f"y{k}", [P, HALF], F32)) for k in range(KI)]
        bc_loaded = [sem(f"bc_loaded{i}") for i in range(2)]
        da_done, da_cut, dbx_done, h_done, hc_done, summed = (
            sem("da_done"), sem("da_cut"), sem("dbx_done"), sem("h_done"), sem("hc_done"), sem("y_summed"))
        z_loaded = [sem(f"z_loaded{i}") for i in range(2)]
        skip_done, y_added, y_done = sem("skip_done"), sem("y_added"), sem("y_done")
        a_signed = sem("a_signed")
        block = ctx.enter_context(nc.Block())
        HALVES = TOK // HALF
        ROUNDS = HALVES * STATE * KI

        @block.sync
        def _(sp):
            zi = 0
            for r in range(HALVES * STATE):
                half, n = divmod(r, STATE)
                cols = slice(half * HALF, (half + 1) * HALF)
                if r >= 2:
                    sp.wait_ge(hc_done, KI * (r - 1))
                for i, dst in enumerate((b_all, c_all)):
                    sp.dma_start(dst[r % 2][:, :], d.bc[i, n:n + 1, cols].to_broadcast([P, HALF])) \
                        .then_inc(bc_loaded[r % 2], 16)
                if n == STATE - 1:
                    for k in range(KI):
                        if zi >= 2:
                            sp.wait_ge(y_done, zi - 1)
                        sp.dma_start(z[zi % 2][:, :], d.z[k, :, cols]).then_inc(z_loaded[zi % 2], 16)
                        zi += 1

        @block.scalar
        def _(act):
            act.wait_ge(a_signed, 1)
            for r in range(ROUNDS):
                half, n, k = r // (STATE * KI), r // KI % STATE, r % KI
                if r >= 2:
                    act.wait_ge(h_done, r - 1)
                nc.scalar.activation(da[r % 2][:, :], s.delta[:, k, half * HALF:(half + 1) * HALF], ACT.Exp,
                                     scale=s.a[:, k, n:n + 1]).then_inc(da_done, 1)

        @block.gpsimd
        def _(pool):
            for r in range(ROUNDS):
                half, n, k = r // (STATE * KI), r // KI % STATE, r % KI
                state = r // KI
                pool.wait_ge(bc_loaded[state % 2], 32 * (state // 2 + 1))
                if r >= 2:
                    pool.wait_ge(h_done, r - 1)
                nc.gpsimd.tensor_tensor(dbx[r % 2][:, :], s.dtx[:, k, half * HALF:(half + 1) * HALF],
                                        b_all[state % 2][:, :], ALU.mult).then_inc(dbx_done, 1)

        @block.vector
        def _(dve):
            nc.vector.tensor_scalar(s.a[:, :, :], s.a[:, :, :], -1.0, None, ALU.mult).then_inc(a_signed, 1)
            out = 0
            for r in range(ROUNDS):
                half, n, k = r // (STATE * KI), r // KI % STATE, r % KI
                state = r // KI
                dve.wait_ge(da_done, r + 1)
                nc.vector.memset(da[r % 2][:, :].rearrange("p (b l) -> p b l", l=LATENTS)[:, :, 0:1], 0.0) \
                    .then_inc(da_cut, 1)
                dve.wait_ge(da_cut, r + 1)
                dve.wait_ge(dbx_done, r + 1)
                nc.vector.tensor_tensor_scan(h[r % 2][:, :], da[r % 2][:, :], dbx[r % 2][:, :], 0.0,
                                             ALU.mult, ALU.add).then_inc(h_done, 1)
                dve.wait_ge(h_done, r + 1)
                dve.wait_ge(bc_loaded[state % 2], 32 * (state // 2 + 1))
                if r >= 2:
                    dve.wait_ge(summed, r - 1)
                nc.vector.tensor_tensor(hc[r % 2][:, :], h[r % 2][:, :], c_all[state % 2][:, :], ALU.mult) \
                    .then_inc(hc_done, 1)
                if n == STATE - 1 and k == KI - 1:
                    for k in range(KI):
                        cols = slice(half * HALF, (half + 1) * HALF)
                        yk = s.y[:, k, cols]
                        dve.wait_ge(summed, half * STATE * KI + (STATE - 1) * KI + k + 1)
                        nc.vector.scalar_tensor_tensor(yk, s.xs[:, k, cols], s.dp[:, k:k + 1], y[k][:, :],
                                                       ALU.mult, ALU.add).then_inc(y_added, 1)
                        dve.wait_ge(y_added, out + 1)
                        dve.wait_ge(z_loaded[out % 2], 16 * (out // 2 + 1))
                        nc.vector.tensor_tensor(yk, yk, z[out % 2][:, :], ALU.mult).then_inc(y_done, 1)
                        out += 1

        @block.tensor
        def _(pe):
            for r in range(ROUNDS):
                half, n, k = r // (STATE * KI), r // KI % STATE, r % KI
                pe.wait_ge(hc_done, r + 1)
                if n == 0 and half > 0:
                    pe.wait_ge(y_added, half * KI)
                for c in range(HALF // BANK):
                    cols = slice(c * BANK, (c + 1) * BANK)
                    last = nc.tensor.matmul(y[k][:, cols], s.ident[:, :], hc[r % 2][:, cols],
                                            start=(n == 0), stop=(n == STATE - 1))
                last.then_inc(summed, 1)


def add_projection(nc, tag, s, y_T, w_dram, b_dram, kt):
    with ExitStack() as ctx:
        w = ctx.enter_context(nc.sbuf_tensor(f"{tag}_w", [P, kt, DIM], F32))
        b = ctx.enter_context(nc.sbuf_tensor(f"{tag}_b", [P, DIM], F32))
        banks = [ctx.enter_context(nc.psum_tensor(f"{tag}_bank{i}", [P, BANK], F32)) for i in range(4)]
        loaded = ctx.enter_context(nc.semaphore(f"{tag}_loaded"))
        projected = ctx.enter_context(nc.semaphore(f"{tag}_projected"))
        added = ctx.enter_context(nc.semaphore(f"{tag}_added"))
        block = ctx.enter_context(nc.Block())

        @block.sync
        def _(sp):
            sp.dma_start(w[:, :, :], w_dram.rearrange("(k p) n -> p k n", p=P)).then_inc(loaded, 16)
            sp.dma_start(b[:, :], b_dram.rearrange("(a n) -> a n", a=1).to_broadcast([P, DIM])).then_inc(loaded, 16)

        @block.tensor
        def _(pe):
            pe.wait_ge(loaded, 32)
            for t in range(TT):
                if t >= 4:
                    pe.wait_ge(added, t - 3)
                for k in range(kt):
                    last = nc.tensor.matmul(banks[t % 4][:, 0:DIM], y_T[:, k, t * P:(t + 1) * P], w[:, k, :],
                                            start=(k == 0), stop=(k == kt - 1))
                last.then_inc(projected, 1)

        @block.vector
        def _(dve):
            dve.wait_ge(loaded, 32)
            for t in range(TT):
                dve.wait_ge(projected, t + 1)
                nc.vector.tensor_tensor(s.x_tok[:, t, :], s.x_tok[:, t, :], banks[t % 4][:, 0:DIM], ALU.add) \
                    .then_inc(added, 1)
            dve.wait_ge(added, TT)
            for t in range(TT):
                nc.vector.tensor_tensor(s.x_tok[:, t, :], s.x_tok[:, t, :], b[:, :], ALU.add)


SLOTS = 256
BLOCKS = (2 * TOK + EXPERTS * (SLOTS - 1)) // SLOTS
ST = SLOTS // P
MAX_NB = TOK // SLOTS
U32 = mybir.dt.uint32


def route(nc, d, s, xn, xn_T):
    with ExitStack() as ctx:
        def sb(name, shape, dt=F32):
            return ctx.enter_context(nc.sbuf_tensor(name, shape, dt))

        def sem(name):
            return ctx.enter_context(nc.semaphore(name))

        E = EXPERTS
        zeros = sb("zeros", [P, DIM])
        rw = sb("rw", [P, KD, E])
        rb = sb("rb", [P, E])
        earlier = sb("earlier", [P, P])
        ones = sb("ones", [P, P])
        lower = sb("lower", [P, E, E])
        fill_levels = sb("fill_levels", [P, MAX_NB])
        block_index = sb("block_index", [P, BLOCKS])
        logits = sb("logits", [P, TT, E])
        top = sb("top", [P, TT])
        coef = sb("coef", [P, TT, E])
        before = sb("before", [P, TT, E, E])
        same = sb("same", [P, TT, E, E])
        chosen = sb("chosen", [P, TT, E])
        total = sb("total", [P, TT])
        counts = sb("counts", [P, TT + 1, E])
        filled = sb("filled", [P, E, MAX_NB])
        n_blocks = sb("n_blocks", [P, E])
        starts = sb("starts", [P, E, E])
        start = sb("start", [P, E])
        ends = sb("ends", [P, E])
        passed = sb("passed", [P, BLOCKS, E])
        block_f = sb("block_f", [P, BLOCKS])
        place = sb("place", [P, TT, E])
        masked = sb("masked", [P, TT, E])
        hit = sb("hit", [P, TT, E])
        row_f = sb("row_f", [P, TT])
        bank = ctx.enter_context(nc.psum_tensor("r_bank", [P, TT * E], F32))
        prefix_bank = ctx.enter_context(nc.psum_tensor("r_prefix", [P, TT * E], F32))
        total_bank = ctx.enter_context(nc.psum_tensor("r_total", [P, TT * E], F32))
        loaded = sem("r_loaded")
        made = sem("r_made")
        zeros_made = sem("r_zeros_made")
        cleared = sem("rows_cleared")
        routed = sem("r_routed")
        step = sem("r_step")
        shifted = sem("r_shifted")
        exped = sem("r_exp")
        chosen_ready = sem("chosen_ready")
        counted = sem("r_counted")
        rows_ready = sem("rows_ready")
        scattered = sem("scattered")
        block = ctx.enter_context(nc.Block())

        @block.sync
        def _(sp):
            sp.dma_start(rw[:, :, :], d.router_w_T.rearrange("(k p) e -> p k e", p=P)).then_inc(loaded, 16)
            sp.dma_start(rb[:, :], d.router_b.rearrange("(a e) -> a e", a=1).to_broadcast([P, E])).then_inc(loaded, 16)
            sp.wait_ge(zeros_made, 1)
            sp.dma_start(d.rows.rearrange("(s p) n -> p s n", p=P),
                         zeros[:, :].rearrange("p (a n) -> p a n", a=1).to_broadcast([P, BLOCKS * ST, DIM])) \
                .then_inc(cleared, 16)

        @block.gpsimd
        def _(pool):
            nc.gpsimd.memset(zeros[:, :], 0.0).then_inc(zeros_made, 1)
            nc.gpsimd.memset(earlier[:, :], 1.0).then_inc(made, 1)
            nc.gpsimd.memset(lower[:, :, :], 1.0).then_inc(made, 1)
            nc.gpsimd.memset(ones[:, :], 1.0).then_inc(made, 1)
            pool.wait_ge(made, 3)
            nc.gpsimd.affine_select(out=earlier[:, :], in_=earlier[:, :], compare_op=ALU.is_gt, fill=0.0,
                                    base=0, pattern=[[1, P]], channel_multiplier=-1).then_inc(made, 1)
            nc.gpsimd.affine_select(out=lower[:, :, :], in_=lower[:, :, :], compare_op=ALU.is_gt, fill=0.0,
                                    base=0, pattern=[[1, E], [-1, E]], channel_multiplier=0).then_inc(made, 1)
            nc.gpsimd.iota(fill_levels[:, :], pattern=[[SLOTS, MAX_NB]], base=0, channel_multiplier=0,
                           allow_small_or_imprecise_dtypes=True).then_inc(made, 1)
            nc.gpsimd.iota(block_index[:, :], pattern=[[1, BLOCKS]], base=0, channel_multiplier=0,
                           allow_small_or_imprecise_dtypes=True).then_inc(made, 1)
            pool.wait_ge(cleared, 16)
            pool.wait_ge(rows_ready, 2)
            for t in range(TT):
                for i in range(2):
                    nc.gpsimd.indirect_dma_start(d.rows, bass.IndirectOffsetOnAxis(s.row[:, i, t:t + 1], 0),
                                                 xn[:, t, :], None).then_inc(scattered, 16)
            pool.wait_ge(scattered, 16 * 2 * TT)

        @block.tensor
        def _(pe):
            pe.wait_ge(loaded, 32)
            for t in range(TT):
                for k in range(KD):
                    last = nc.tensor.matmul(bank[:, t * E:(t + 1) * E], xn_T[:, k, t * P:(t + 1) * P], rw[:, k, :],
                                            start=(k == 0), stop=(k == KD - 1))
            last.then_inc(routed, 1)
            pe.wait_ge(made, 7)
            pe.wait_ge(chosen_ready, 1)
            flat = chosen[:, :, :].rearrange("p t e -> p (t e)")
            nc.tensor.matmul(prefix_bank[:, :], earlier[:, :], flat, start=True, stop=True)
            nc.tensor.matmul(total_bank[:, :], ones[:, :], flat, start=True, stop=True).then_inc(counted, 1)

        @block.scalar
        def _(act):
            act.wait_ge(shifted, 1)
            nc.scalar.activation(coef[:, :, :], coef[:, :, :], ACT.Exp).then_inc(exped, 1)

        @block.vector
        def _(dve):
            done = [0]

            def then(instruction):
                done[0] += 1
                instruction.then_inc(step, 1)
                dve.wait_ge(step, done[0])

            def over(a, shape):
                axes = "p t e" if len(a.shape) == 3 else "p t"
                return a.rearrange(f"{axes[:-1]}({axes[-1]} a) -> {axes} a", a=1).to_broadcast(shape)

            def across(a, shape):
                if len(a.shape) == 3:
                    return a.rearrange("p t (a e) -> p t a e", a=1).to_broadcast(shape)
                return a.rearrange("p (a e) -> p a e", a=1).to_broadcast(shape)

            tee, te = [P, TT, E, E], [P, TT, E]
            dve.wait_ge(loaded, 32)
            dve.wait_ge(routed, 1)
            dve.wait_ge(made, 7)
            L = logits[:, :, :]
            then(nc.vector.tensor_tensor(L, bank[:, :].rearrange("p (t e) -> p t e", e=E), across(rb[:, :], te), ALU.add))
            then(nc.vector.tensor_reduce(top[:, :], L, AX, ALU.max))
            nc.vector.tensor_tensor(coef[:, :, :], L, over(top[:, :], te), ALU.subtract).then_inc(shifted, 1)
            nc.vector.tensor_tensor(before[:, :, :, :], across(L, tee), over(L, tee), ALU.is_gt)
            then(nc.vector.tensor_tensor(same[:, :, :, :], across(L, tee), over(L, tee), ALU.is_equal))
            then(nc.vector.tensor_tensor(same[:, :, :, :], same[:, :, :, :],
                                         lower[:, :, :].rearrange("p (a i) j -> p a i j", a=1).to_broadcast(tee), ALU.mult))
            then(nc.vector.tensor_tensor(before[:, :, :, :], before[:, :, :, :], same[:, :, :, :], ALU.add))
            then(nc.vector.tensor_reduce(place[:, :, :], before[:, :, :, :], AX, ALU.add))
            nc.vector.tensor_scalar(chosen[:, :, :], place[:, :, :], 1.5, None, ALU.is_lt).then_inc(chosen_ready, 1)
            dve.wait_ge(chosen_ready, 1)
            dve.wait_ge(exped, 1)
            then(nc.vector.tensor_tensor(coef[:, :, :], coef[:, :, :], chosen[:, :, :], ALU.mult))
            then(nc.vector.tensor_reduce(total[:, :], coef[:, :, :], AX, ALU.add))
            then(nc.vector.reciprocal(total[:, :], total[:, :]))
            then(nc.vector.tensor_tensor(coef[:, :, :], coef[:, :, :], over(total[:, :], te), ALU.mult))

            dve.wait_ge(counted, 1)
            then(nc.vector.memset(counts[:, 0, :], 0.0))
            for t in range(TT):
                then(nc.vector.tensor_tensor(counts[:, t + 1, :], counts[:, t, :], total_bank[:, t * E:(t + 1) * E],
                                             ALU.add))
            ee = [P, E, MAX_NB]
            then(nc.vector.tensor_tensor(filled[:, :, :], over(counts[:, TT, :], ee), across(fill_levels[:, :], ee),
                                         ALU.is_gt))
            then(nc.vector.tensor_reduce(n_blocks[:, :], filled[:, :, :], AX, ALU.add))
            then(nc.vector.tensor_tensor(starts[:, :, :], lower[:, :, :], across(n_blocks[:, :], [P, E, E]), ALU.mult))
            then(nc.vector.tensor_reduce(start[:, :], starts[:, :, :], AX, ALU.add))
            then(nc.vector.tensor_tensor(ends[:, :], start[:, :], n_blocks[:, :], ALU.add))
            be = [P, BLOCKS, E]
            then(nc.vector.tensor_tensor(passed[:, :, :], over(block_index[:, :], be), across(ends[:, :], be), ALU.is_ge))
            then(nc.vector.tensor_reduce(block_f[:, :], passed[:, :, :], AX, ALU.add))
            nc.vector.tensor_scalar(s.block_expert[:, :], block_f[:, :], float(E - 1), None, ALU.min)

            then(nc.vector.tensor_scalar(start[:, :], start[:, :], float(SLOTS), None, ALU.mult))
            then(nc.vector.tensor_tensor(place[:, :, :], counts[:, 0:TT, :], across(start[:, :], te), ALU.add))
            then(nc.vector.tensor_tensor(place[:, :, :], place[:, :, :],
                                         prefix_bank[:, :].rearrange("p (t e) -> p t e", e=E), ALU.add))
            FAR = float(BLOCKS * SLOTS)
            for i, (away, pick) in enumerate(((FAR, ALU.min), (-FAR, ALU.max))):
                then(nc.vector.tensor_scalar(masked[:, :, :], chosen[:, :, :], -away, away, ALU.mult, ALU.add))
                then(nc.vector.tensor_tensor(masked[:, :, :], masked[:, :, :], place[:, :, :], ALU.add))
                then(nc.vector.tensor_reduce(row_f[:, :], masked[:, :, :], AX, pick))
                nc.vector.tensor_copy(s.row[:, i, :], row_f[:, :]).then_inc(rows_ready, 1)
                then(nc.vector.tensor_tensor(hit[:, :, :], masked[:, :, :], over(row_f[:, :], te), ALU.is_equal))
                then(nc.vector.tensor_tensor(hit[:, :, :], hit[:, :, :], coef[:, :, :], ALU.mult))
                then(nc.vector.tensor_reduce(s.weight[:, i, :], hit[:, :, :], AX, ALU.add))


def at_least(engine, semaphore, value):
    if not isinstance(value, int) or value > 0:
        engine.wait_ge(semaphore, value)


def experts(nc, d, s):
    with ExitStack() as ctx:
        def sb(name, shape, dt=F32):
            return ctx.enter_context(nc.sbuf_tensor(name, shape, dt))

        def sem(name):
            return ctx.enter_context(nc.semaphore(name))

        QUARTERS = 4
        FQ = KF // QUARTERS
        b1_all = sb("b1_all", [P, EXPERTS, KF])
        b2_all = sb("b2_all", [P, EXPERTS, DIM])
        w1 = [sb(f"w1_{i}", [P, KD, FF]) for i in range(2)]
        w1_hi = [sb(f"w1_hi{i}", [P, KD, FF], F32R) for i in range(2)]
        w1_lo = [sb(f"w1_lo{i}", [P, KD, FF], F32R) for i in range(2)]
        w2 = [sb(f"w2_{i}", [P, KF, DIM]) for i in range(2)]
        w2_hi = [sb(f"w2_hi{i}", [P, KF, DIM], F32R) for i in range(2)]
        w2_lo = [sb(f"w2_lo{i}", [P, KF, DIM], F32R) for i in range(2)]
        b1 = [sb(f"b1_{i}", [P, KF]) for i in range(2)]
        rows = [sb(f"rows{i}", [P, ST, DIM]) for i in range(2)]
        x_hi = [sb(f"x_hi{i}", [P, KD, SLOTS], F32R) for i in range(2)]
        x_lo = [sb(f"x_lo{i}", [P, KD, SLOTS], F32R) for i in range(2)]
        hidden = sb("hidden", [P, KF, SLOTS])
        h_hi = sb("h_hi", [P, KF, SLOTS], F32R)
        h_lo = sb("h_lo", [P, KF, SLOTS], F32R)
        y = [sb(f"y_out{i}", [P, ST, DIM]) for i in range(2)]
        up = [ctx.enter_context(nc.psum_tensor(f"up{i}", [P, BANK], F32)) for i in range(QUARTERS)]
        turned = ctx.enter_context(nc.psum_tensor("turned", [P, BANK], F32))
        down = [ctx.enter_context(nc.psum_tensor(f"down{i}", [P, BANK], F32)) for i in range(ST)]
        biases_loaded = sem("biases_loaded")
        w_loaded = [sem(f"w_loaded{i}") for i in range(2)]
        rows_loaded = [sem(f"rows_loaded{i}") for i in range(2)]
        y_stored = [sem(f"y_stored{i}") for i in range(2)]
        w1_hi_done, w1_split, w2_hi_done, w2_split = (
            sem("w1_hi_done"), sem("w1_split"), sem("w2_hi_done"), sem("w2_split"))
        b1_chosen = sem("b1_chosen")
        rows_turned, x_hi_done, x_split = sem("rows_turned"), sem("x_hi_done"), sem("x_split")
        up_done, gelu_done, h_hi_done, h_split = sem("up_done"), sem("gelu_done"), sem("h_hi_done"), sem("h_split")
        down_done, y_done = sem("down_done"), sem("y_done2")
        block = ctx.enter_context(nc.Block())

        def each_block(engine, body):
            pairs = (BLOCKS - 2) // 2
            body(0, 0, True)
            with engine.Fori(0, pairs) as i:
                body(i * 2 + 1, 1, True)
                body(i * 2 + 2, 0, True)
            for j in range(2 * pairs + 1, BLOCKS):
                body(j, j % 2, j + 1 < BLOCKS)

        @block.sync
        def _(sp):
            def load(j, par, more):
                e = sp.value_load(s.block_expert[0:1, bass.ds(j, 1)], min_val=0, max_val=EXPERTS - 1)
                at_least(sp, w1_split, j - 1)
                at_least(sp, w2_split, j - 1)
                sp.dma_start(w1[par][:, :, :], d.w1_T[bass.ds(e, 1), :, :].rearrange("a (k p) f -> p (a k) f", p=P)) \
                    .then_inc(w_loaded[par], 16)
                sp.dma_start(w2[par][:, :, :], d.w2_T[bass.ds(e, 1), :, :].rearrange("a (k p) n -> p (a k) n", p=P)) \
                    .then_inc(w_loaded[par], 16)
                at_least(sp, rows_turned, j - 1)
                sp.dma_start(rows[par][:, :, :], d.rows[bass.ds(j * SLOTS, SLOTS), :]
                             .rearrange("(t p) n -> p t n", p=P)).then_inc(rows_loaded[par], 16)

            sp.dma_start(b1_all[:, :, :], d.b1_T.rearrange("e p k -> p e k")).then_inc(biases_loaded, 16)
            sp.dma_start(b2_all[:, :, :], d.b2.rearrange("(a e) n -> a e n", a=1).to_broadcast([P, EXPERTS, DIM])) \
                .then_inc(biases_loaded, 16)
            each_block(sp, load)

        @block.gpsimd
        def _(pool):
            def split(j, par, more):
                pool.wait_ge(w1_hi_done, j + 1)
                nc.gpsimd.tensor_tensor(w1_lo[par][:, :, :], w1[par][:, :, :], w1_hi[par][:, :, :].bitcast(F32),
                                        ALU.subtract).then_inc(w1_split, 1)

            each_block(pool, split)

        @block.vector
        def _(dve):
            def prepare(j, par, part):
                if part == 0:
                    dve.wait_ge(w_loaded[par], (j - par) * 16 + 32)
                    at_least(dve, down_done, (j - 1) * ST)
                    nc.vector.tensor_copy(w1_hi[par][:, :, :], w1[par][:, :, :]).then_inc(w1_hi_done, 1)
                elif part == 1:
                    nc.vector.tensor_copy(w2_hi[par][:, :, :], w2[par][:, :, :]).then_inc(w2_hi_done, 1)
                    e = dve.value_load(s.block_expert[0:1, bass.ds(j, 1)], min_val=0, max_val=EXPERTS - 1)
                    nc.vector.tensor_copy(b1[par][:, :], b1_all[:, bass.ds(e, 1), :].rearrange("p a k -> p (a k)")) \
                        .then_inc(b1_chosen, 1)
                elif part == 2:
                    dve.wait_ge(w2_hi_done, j + 1)
                    nc.vector.tensor_tensor(w2_lo[par][:, :, :], w2[par][:, :, :], w2_hi[par][:, :, :].bitcast(F32),
                                            ALU.subtract).then_inc(w2_split, 1)
                else:
                    dve.wait_ge(x_hi_done, j + 1)
                    nc.vector.tensor_tensor(x_lo[par][:, :, :], turned[:, :].rearrange("p (k n) -> p k n", k=KD),
                                            x_hi[par][:, :, :].bitcast(F32), ALU.subtract).then_inc(x_split, 1)

            def compute(j, par, more):
                for q in range(QUARTERS):
                    dve.wait_ge(gelu_done, (j * QUARTERS + q + 1) * FQ)
                    part = slice(q * FQ, (q + 1) * FQ)
                    nc.vector.tensor_copy(h_hi[:, part, :], hidden[:, part, :]).then_inc(h_hi_done, 1)
                    dve.wait_ge(h_hi_done, j * QUARTERS + q + 1)
                    nc.vector.tensor_tensor(h_lo[:, part, :], hidden[:, part, :], h_hi[:, part, :].bitcast(F32),
                                            ALU.subtract).then_inc(h_split, 1)
                    if more:
                        prepare(j + 1, 1 - par, q)
                e = dve.value_load(s.block_expert[0:1, bass.ds(j, 1)], min_val=0, max_val=EXPERTS - 1)
                at_least(dve, y_stored[par], (j - par) * 8)
                for t in range(ST):
                    dve.wait_ge(down_done, j * ST + t + 1)
                    nc.vector.tensor_tensor(y[par][:, t:t + 1, :], down[t][:, 0:DIM].rearrange("p (a n) -> p a n", a=1),
                                            b2_all[:, bass.ds(e, 1), :], ALU.add).then_inc(y_done, 1)

            dve.wait_ge(biases_loaded, 32)
            for part in range(4):
                prepare(0, 0, part)
            each_block(dve, compute)

        @block.scalar
        def _(act):
            def rows_hi(j, par):
                act.wait_ge(rows_turned, j + 1)
                nc.scalar.copy(x_hi[par][:, :, :], turned[:, :].rearrange("p (k n) -> p k n", k=KD)).then_inc(x_hi_done, 1)

            def store(j, par):
                act.wait_ge(y_done, (j + 1) * ST)
                act.dma_start(d.results[bass.ds(j * SLOTS, SLOTS), :].rearrange("(t p) n -> p t n", p=P), y[par][:, :, :]) \
                    .then_inc(y_stored[par], 16)

            def compute(j, par, more):
                act.wait_ge(b1_chosen, j + 1)
                for f in range(KF):
                    q, i = divmod(f, FQ)
                    if i == 0:
                        act.wait_ge(up_done, j * QUARTERS + q + 1)
                    nc.scalar.activation(hidden[:, f, :], up[q][:, i * SLOTS:(i + 1) * SLOTS], ACT.Gelu,
                                         bias=b1[par][:, f:f + 1]).then_inc(gelu_done, 1)
                if more:
                    rows_hi(j + 1, 1 - par)
                if not isinstance(j, int) or j > 0:
                    store(j - 1, 1 - par)

            rows_hi(0, 0)
            each_block(act, compute)
            store(BLOCKS - 1, (BLOCKS - 1) % 2)
            for par in range(2):
                act.wait_ge(y_stored[par], 16 * ((BLOCKS + 1 - par) // 2))

        @block.tensor
        def _(pe):
            def turn(j, par):
                pe.wait_ge(rows_loaded[par], (j - par) * 8 + 16)
                at_least(pe, x_split, j)
                for k in range(KD):
                    for t in range(ST):
                        last = nc.tensor.transpose(turned[:, (k * ST + t) * P:(k * ST + t + 1) * P],
                                                   rows[par][:, t, k * P:(k + 1) * P], s.ident[:, :])
                last.then_inc(rows_turned, 1)

            def compute(j, par, more):
                pe.wait_ge(w1_split, j + 1)
                pe.wait_ge(x_split, j + 1)
                for f in range(KF):
                    q, i = divmod(f, FQ)
                    if i == 0:
                        at_least(pe, gelu_done, (j - 1) * KF + (q + 1) * FQ)
                    cols = slice(f * P, (f + 1) * P)
                    parts = [(w, x, k) for k in range(KD)
                             for w, x in ((w1_hi, x_hi), (w1_hi, x_lo), (w1_lo, x_hi))]
                    for n, (w, x, k) in enumerate(parts):
                        last = nc.tensor.matmul(up[q][:, i * SLOTS:(i + 1) * SLOTS], w[par][:, k, cols], x[par][:, k, :],
                                                start=(n == 0), stop=(n == len(parts) - 1))
                    if i == FQ - 1:
                        last.then_inc(up_done, 1)
                if more:
                    turn(j + 1, 1 - par)
                pe.wait_ge(w2_split, j + 1)
                at_least(pe, y_done, j * ST)
                for f in range(KF):
                    q, i = divmod(f, FQ)
                    if i == 0:
                        pe.wait_ge(h_split, j * QUARTERS + q + 1)
                    for t in range(ST):
                        for n, (h, w) in enumerate(((h_hi, w2_hi), (h_hi, w2_lo), (h_lo, w2_hi))):
                            last = nc.tensor.matmul(down[t][:, 0:DIM], h[:, f, t * P:(t + 1) * P], w[par][:, f, :],
                                                    start=(f == 0 and n == 0), stop=(f == KF - 1 and n == 2))
                        if f == KF - 1:
                            last.then_inc(down_done, 1)

            turn(0, 0)
            each_block(pe, compute)


def combine(nc, d, s):
    with ExitStack() as ctx:
        RING = 8
        fetched = [ctx.enter_context(nc.sbuf_tensor(f"fetched{i}", [P, DIM], F32)) for i in range(RING)]
        fetched_sem = [ctx.enter_context(nc.semaphore(f"fetched_sem{i}")) for i in range(RING)]
        added = ctx.enter_context(nc.semaphore("c_added"))
        stored = ctx.enter_context(nc.semaphore("stored"))
        block = ctx.enter_context(nc.Block())

        @block.gpsimd
        def _(pool):
            for n in range(2 * TT):
                t, i = divmod(n, 2)
                at_least(pool, added, n - RING + 1)
                nc.gpsimd.indirect_dma_start(fetched[n % RING][:, :], None, d.results,
                                             bass.IndirectOffsetOnAxis(s.row[:, i, t:t + 1], 0)) \
                    .then_inc(fetched_sem[n % RING], 16)

        @block.vector
        def _(dve):
            for n in range(2 * TT):
                t, i = divmod(n, 2)
                dve.wait_ge(fetched_sem[n % RING], 16 * (n // RING + 1))
                at_least(dve, added, n)
                nc.vector.scalar_tensor_tensor(s.x_tok[:, t, :], fetched[n % RING][:, :], s.weight[:, i, t:t + 1],
                                               s.x_tok[:, t, :], ALU.mult, ALU.add).then_inc(added, 1)

        @block.sync
        def _(sp):
            for t in range(0, TT, 4):
                sp.wait_ge(added, 2 * (t + 4))
                sp.dma_start(d.out[t * P:(t + 4) * P, :].rearrange("(t p) n -> p t n", p=P), s.x_tok[:, t:t + 4, :]) \
                    .then_inc(stored, 16)
            sp.wait_ge(stored, 16 * (TT // 4))


def perceiver(nc, d):
    with ExitStack() as ctx:
        x_tok = ctx.enter_context(nc.sbuf_tensor("x_tok", [P, TT, DIM], F32))
        ident = ctx.enter_context(nc.sbuf_tensor("ident", [P, P], F32))
        with ExitStack() as inner:
            s = attention_memory(nc, inner)
            s.x_tok, s.ident = x_tok, ident
            load_constants(nc, d, s)
            with ExitStack() as first:
                xn_T = first.enter_context(nc.sbuf_tensor("xn_T1", [P, KD, TOK], F32))
                xn = first.enter_context(nc.sbuf_tensor("xn1", [P, TT, DIM], F32))
                normalize_and_transpose(nc, "ln1", x_tok, xn, xn_T, ident)
                project_queries(nc, d, s, xn_T)
            attention(nc, d, s)
        s = Names()
        s.x_tok, s.ident = x_tok, ident
        attention_output(nc, d, s)
        with ExitStack() as inner:
            def sb(name, shape):
                return inner.enter_context(nc.sbuf_tensor(name, shape, F32))

            s.a, s.dp = sb("a", [P, KI, STATE]), sb("dp", [P, KI])
            s.xs, s.delta, s.dtx = sb("xs", [P, KI, TOK]), sb("delta", [P, KI, TOK]), sb("dtx", [P, KI, TOK])
            with ExitStack() as first:
                xn_T = first.enter_context(nc.sbuf_tensor("xn_T2", [P, KD, TOK], F32))
                with ExitStack() as norm:
                    xn = norm.enter_context(nc.sbuf_tensor("xn2", [P, TT, DIM], F32))
                    normalize_and_transpose(nc, "ln2", x_tok, xn, xn_T, ident)
                ssm_projections(nc, d, s, xn_T)
            s.y = s.xs
            ssm_scan(nc, d, s)
            add_projection(nc, "wout", s, s.y, d.Wout, d.bout, KI)
        with ExitStack() as inner:
            s.row = inner.enter_context(nc.sbuf_tensor("row", [P, 2, TT], U32))
            s.weight = inner.enter_context(nc.sbuf_tensor("weight", [P, 2, TT], F32))
            s.block_expert = inner.enter_context(nc.sbuf_tensor("block_expert", [P, BLOCKS], U32))
            with ExitStack() as first:
                xn = first.enter_context(nc.sbuf_tensor("xn3", [P, TT, DIM], F32))
                xn_T = first.enter_context(nc.sbuf_tensor("xn_T3", [P, KD, TOK], F32))
                normalize_and_transpose(nc, "ln3", x_tok, xn, xn_T, ident)
                route(nc, d, s, xn, xn_T)
            experts(nc, d, s)
            combine(nc, d, s)


def laid_out(inputs):
    import numpy as np
    names = dict(W_Q="xattn_W_Q", b_Q="xattn_b_Q", W_K="xattn_W_K", b_K="xattn_b_K", W_V="xattn_W_V",
                 b_V="xattn_b_V", W_O="xattn_W_O", b_O="xattn_b_O", Win="attn_Win", bin="attn_bin", Wx="attn_Wx",
                 bx="attn_bx", Wdt="attn_Wdt", bdt="attn_bdt", A_log="attn_A_log", Dp="attn_Dp",
                 Wout="attn_Wout", bout="attn_bout", router_b="ffn_router_b", b2="ffn_b2")
    arrays = {k: np.asarray(inputs["L0_" + v]) for k, v in names.items()}
    arrays["x"] = np.asarray(inputs["x"]).reshape(TOK, DIM)
    arrays["ctx_T"] = np.asarray(inputs["ctx_1024"]).transpose(0, 2, 1)
    arrays["router_w_T"] = np.asarray(inputs["L0_ffn_router_w"]).T
    arrays["w1_T"] = np.asarray(inputs["L0_ffn_w1"]).transpose(0, 2, 1)
    arrays["w2_T"] = np.asarray(inputs["L0_ffn_w2"]).transpose(0, 2, 1)
    arrays["b1_T"] = np.asarray(inputs["L0_ffn_b1"]).reshape(EXPERTS, KF, P).transpose(0, 2, 1)
    return {k: np.ascontiguousarray(v) for k, v in arrays.items()}


def build(nc, shapes):
    def array(name):
        return nc.dram_tensor(f"in_{name}", shapes[name], F32, kind="ExternalInput").ap()

    d = Names()
    d.x, d.ctx_T = array("x"), array("ctx_T")
    d.W_Q, d.b_Q, d.W_K, d.b_K = array("W_Q"), array("b_Q"), array("W_K"), array("b_K")
    d.W_V, d.b_V, d.W_O, d.b_O = array("W_V"), array("b_V"), array("W_O"), array("b_O")
    d.Win, d.bin, d.Wx, d.bx = array("Win"), array("bin"), array("Wx"), array("bx")
    d.Wdt, d.bdt, d.A_log, d.Dp = array("Wdt"), array("bdt"), array("A_log"), array("Dp")
    d.Wout, d.bout = array("Wout"), array("bout")
    d.router_w_T, d.router_b = array("router_w_T"), array("router_b")
    d.w1_T, d.b1_T, d.w2_T, d.b2 = array("w1_T"), array("b1_T"), array("w2_T"), array("b2")
    d.mixed = nc.dram_tensor("scratch_mixed", (BATCH, P, DIM), F32).ap()
    d.z = nc.dram_tensor("scratch_z", (KI, P, TOK), F32).ap()
    d.bc = nc.dram_tensor("scratch_bc", (2, STATE, TOK), F32).ap()
    d.rows = nc.dram_tensor("scratch_rows", (BLOCKS * SLOTS, DIM), F32).ap()
    d.results = nc.dram_tensor("scratch_results", (BLOCKS * SLOTS, DIM), F32).ap()
    d.out = nc.dram_tensor("out", (TOK, DIM), F32, kind="ExternalOutput").ap()
    perceiver(nc, d)


def kernel(**inputs):
    import concourse.bacc as bacc
    from concourse.bass_utils import run_bass_kernel_spmd

    nc = bacc.Bacc("TRN2", target_bir_lowering=False, num_devices=1)
    arrays = laid_out(inputs)
    build(nc, {k: a.shape for k, a in arrays.items()})
    r = run_bass_kernel_spmd(nc, [{f"in_{k}": a for k, a in arrays.items()}], core_ids=[0])
    return r.results[0]["out"].reshape(BATCH, LATENTS, DIM)
```

```python
import concourse.bass as bass
from concourse import mybir
from contextlib import ExitStack

F32 = mybir.dt.float32
F32R = mybir.dt.float32r
ACT = mybir.ActivationFunctionType
ALU = mybir.AluOpType
AX = mybir.AxisListType.X

P = 128
BATCH, LATENTS, DIM = 32, 64, 256
KEYS = 1601
TOK = BATCH * LATENTS
TT = TOK // P
KD = DIM // P
HEADS, HD = 16, 16
HPM = P // HD
GROUPS, HPG = HEADS // 4, 4
SIDE = HPG * HD
GCOLS = HPG * LATENTS


def lo_side(g):
    return slice((g % 2) * SIDE, (g % 2 + 1) * SIDE)


def hi_side(g):
    return lo_side(g + 1)


BANK = 512
EPS = 1e-5
INNER, STATE, RANK = 512, 16, 16
KI = INNER // P
EXPERTS, FF = 8, 1024
KF = FF // P

CHUNKS = [(0, 512), (512, 512), (1024, 512), (1536, KEYS - 1536)]
TILES = [(s, min(P, KEYS - s)) for s in range(0, KEYS, P)]
NT = len(TILES)
KEYS_EVEN = KEYS + KEYS % 2
VW = HD + 1


class Names:
    pass


def even(n):
    return n + n % 2


def column_tiles(v):
    return v.rearrange("(m p) -> p m", p=P)


LN_GROUPS = TOK // BANK
GT = TT // LN_GROUPS


def nothing(engine, g):
    pass


def normalize_and_transpose(nc, tag, x_tok, xn, xn_T, ident, sp_start=None, pool_start=None,
                            pe_before=nothing, act_before=nothing, dve_before=nothing, pe_after=nothing):
    with ExitStack() as ctx:
        TURNED = 3
        stats = ctx.enter_context(nc.sbuf_tensor(f"{tag}_stats", [P, TT, 6], F32))
        mean_var = ctx.enter_context(nc.sbuf_tensor(f"{tag}_mean_var", [P, TT, 2], F32))
        rstd = ctx.enter_context(nc.sbuf_tensor(f"{tag}_rstd", [P, TT], F32))
        banks = [ctx.enter_context(nc.psum_tensor(f"{tag}_T{i}", [P, BANK], F32)) for i in range(TURNED)]
        stats_ready = ctx.enter_context(nc.semaphore(f"{tag}_stats_ready"))
        var_ready = ctx.enter_context(nc.semaphore(f"{tag}_var_ready"))
        rooted = ctx.enter_context(nc.semaphore(f"{tag}_rooted"))
        inverted = ctx.enter_context(nc.semaphore(f"{tag}_inverted"))
        normed = ctx.enter_context(nc.semaphore(f"{tag}_normed"))
        transposed = ctx.enter_context(nc.semaphore(f"{tag}_transposed"))
        copied = ctx.enter_context(nc.semaphore(f"{tag}_copied"))
        block = ctx.enter_context(nc.Block())

        if sp_start is not None:
            @block.sync
            def _(sp):
                sp_start(sp)

        if pool_start is not None:
            @block.gpsimd
            def _(pool):
                pool_start(pool)

        @block.vector
        def _(dve):
            def statistics(g):
                for t in range(g * GT, (g + 1) * GT):
                    nc.vector.bn_stats(stats[:, t, :], x_tok[:, t, :]).then_inc(stats_ready, 1)
                dve.wait_ge(stats_ready, (2 * g + 1) * GT)
                for t in range(g * GT, (g + 1) * GT):
                    nc.vector.bn_aggr(mean_var[:, t, :], stats[:, t, :]).then_inc(stats_ready, 1)
                dve.wait_ge(stats_ready, (2 * g + 2) * GT)
                nc.vector.tensor_scalar(rstd[:, g * GT:(g + 1) * GT], mean_var[:, g * GT:(g + 1) * GT, 1], EPS, None,
                                        ALU.add).then_inc(var_ready, 1)

            def normalize(g):
                part = rstd[:, g * GT:(g + 1) * GT]
                dve.wait_ge(rooted, g + 1)
                nc.vector.reciprocal(part, part).then_inc(inverted, 1)
                dve.wait_ge(inverted, g + 1)
                for t in range(g * GT, (g + 1) * GT):
                    nc.vector.tensor_scalar(xn[:, t, :], x_tok[:, t, :], mean_var[:, t, 0:1], rstd[:, t:t + 1],
                                            ALU.subtract, ALU.mult).then_inc(normed, 1)

            for g in range(LN_GROUPS):
                dve_before(dve, g)
                statistics(g)
                normalize(g)

        @block.tensor
        def _(pe):
            def turn(g):
                pe.wait_ge(normed, (g + 1) * GT)
                for k in range(KD):
                    n = g * KD + k
                    if n >= TURNED:
                        pe.wait_ge(copied, n + 1 - TURNED)
                    for j in range(GT):
                        last = nc.tensor.transpose(banks[n % TURNED][:, j * P:(j + 1) * P],
                                                   xn[:, g * GT + j, k * P:(k + 1) * P], ident[:, :])
                    last.then_inc(transposed, 1)

            def after(g):
                if pe_after is not nothing:
                    pe.wait_ge(copied, (g + 1) * KD)
                    pe_after(pe, g)

            for g in range(LN_GROUPS + 1):
                if g < LN_GROUPS:
                    pe_before(pe, g)
                if g > 0:
                    turn(g - 1)
                if g > 1:
                    after(g - 2)
            after(LN_GROUPS - 1)

        @block.scalar
        def _(act):
            def root(g):
                act.wait_ge(var_ready, g + 1)
                nc.scalar.sqrt(rstd[:, g * GT:(g + 1) * GT], rstd[:, g * GT:(g + 1) * GT]).then_inc(rooted, 1)

            def copy(g):
                for k in range(KD):
                    n = g * KD + k
                    act.wait_ge(transposed, n + 1)
                    nc.scalar.copy(xn_T[:, k, g * BANK:(g + 1) * BANK], banks[n % TURNED][:, :]).then_inc(copied, 1)

            for g in range(LN_GROUPS):
                act_before(act, g)
                root(g)
                if g >= 1:
                    copy(g - 1)
            copy(LN_GROUPS - 1)


def load_constants(nc, d, s):
    with ExitStack() as ctx:
        loaded = ctx.enter_context(nc.semaphore("constants_loaded"))
        filled = ctx.enter_context(nc.semaphore("constants_filled"))
        block = ctx.enter_context(nc.Block())

        @block.sync
        def _(sp):
            sp.dma_start(s.x_tok[:, :, :], d.x.rearrange("(t p) d -> p t d", p=P)).then_inc(loaded, 16)
            sp.wait_ge(loaded, 16)

        @block.gpsimd
        def _(pool):
            nc.gpsimd.memset(s.ident[:, :], 0.0).then_inc(filled, 1)
            pool.wait_ge(filled, 1)
            nc.gpsimd.affine_select(out=s.ident[:, :], in_=s.ident[:, :], compare_op=ALU.not_equal, fill=1.0,
                                    base=0, pattern=[[-1, P]], channel_multiplier=1).then_inc(filled, 1)


def project_queries(nc, d, s, xn_T):
    with ExitStack() as ctx:
        wq = ctx.enter_context(nc.sbuf_tensor("wq", [P, KD, DIM], F32))
        wk = ctx.enter_context(nc.sbuf_tensor("wk", [P, KD, DIM], F32))
        wv = ctx.enter_context(nc.sbuf_tensor("wv", [P, KD, DIM], F32))
        bq = ctx.enter_context(nc.sbuf_tensor("bq", [P, KD], F32))
        tile_mask = ctx.enter_context(nc.sbuf_tensor("tile_mask", [P, HPM], F32))
        banks = [ctx.enter_context(nc.psum_tensor(f"q_bank{i}", [P, BANK], F32)) for i in range(4)]
        loaded = ctx.enter_context(nc.semaphore("q_loaded"))
        mask_made = ctx.enter_context(nc.semaphore("mask_made"))
        hi_made = ctx.enter_context(nc.semaphore("weights_hi_made"))
        projected = ctx.enter_context(nc.semaphore("q_projected"))
        copied = ctx.enter_context(nc.semaphore("q_copied"))
        block = ctx.enter_context(nc.Block())

        @block.sync
        def _(sp):
            for dst, src in ((wq, d.W_Q), (wk, d.W_K), (wv, d.W_V)):
                sp.dma_start(dst[:, :, :], src.rearrange("(k p) n -> p k n", p=P)).then_inc(loaded, 16)
            sp.dma_start(bq[:, :], column_tiles(d.b_Q), allow_slow_non_contiguous=True).then_inc(loaded, 16)
            sp.dma_start(s.bk[:, :], column_tiles(d.b_K), allow_slow_non_contiguous=True).then_inc(loaded, 16)

        @block.gpsimd
        def _(pool):
            nc.gpsimd.memset(s.one[:, :], 1.0)
            nc.gpsimd.memset(tile_mask[:, :], 1.0).then_inc(mask_made, 1)
            pool.wait_ge(mask_made, 1)
            nc.gpsimd.affine_select(out=tile_mask[:, :], in_=tile_mask[:, :], compare_op=ALU.is_ge,
                                    fill=0.0, base=0, pattern=[[-HD, HPM]], channel_multiplier=1) \
                .then_inc(mask_made, 1)
            pool.wait_ge(mask_made, 2)
            nc.gpsimd.affine_select(out=tile_mask[:, :], in_=tile_mask[:, :], compare_op=ALU.is_ge,
                                    fill=0.0, base=HD - 1, pattern=[[HD, HPM]], channel_multiplier=-1) \
                .then_inc(mask_made, 1)
            pool.wait_ge(mask_made, 3)
            nc.gpsimd.tensor_tensor(s.head_mask[:, :], tile_mask[:, 0:HPG], tile_mask[:, HPG:HPM], ALU.add) \
                .then_inc(mask_made, 1)

        @block.vector
        def _(dve):
            dve.wait_ge(loaded, 80)
            nc.vector.tensor_copy(s.wk_hi[:, :, :], wk[:, :, :]).then_inc(hi_made, 1)
            nc.vector.tensor_copy(s.wv_hi[:, :, :], wv[:, :, :]).then_inc(hi_made, 1)
            dve.wait_ge(hi_made, 2)
            for lo, whole, hi in ((s.wk_lo, wk, s.wk_hi), (s.wv_lo, wv, s.wv_hi)):
                nc.vector.tensor_tensor(lo[:, :, :], whole[:, :, :], hi[:, :, :].bitcast(F32), ALU.subtract) \
                    .then_inc(hi_made, 1)
            for v in s.values:
                nc.vector.memset(v[:, :, :, HD:VW], 1.0)
            n = 0
            for m in range(KD):
                for c in range(TOK // BANK):
                    for g in (2 * m, 2 * m + 1):
                        n += 1
                        dve.wait_ge(copied, n)
                        nc.vector.tensor_copy(s.queries[hi_side(g), g, c * BANK:(c + 1) * BANK],
                                              s.queries[lo_side(g), g, c * BANK:(c + 1) * BANK])

        @block.tensor
        def _(pe):
            pe.wait_ge(loaded, 80)
            n = 0
            for m in range(KD):
                for c in range(TOK // BANK):
                    if n >= 4:
                        pe.wait_ge(copied, 2 * (n - 3))
                    for k in range(KD):
                        last = nc.tensor.matmul(banks[n % 4][:, :], wq[:, k, m * P:(m + 1) * P],
                                                xn_T[:, k, c * BANK:(c + 1) * BANK],
                                                start=(k == 0), stop=(k == KD - 1))
                    last.then_inc(projected, 1)
                    n += 1

        @block.scalar
        def _(act):
            n = 0
            for m in range(KD):
                for c in range(TOK // BANK):
                    act.wait_ge(projected, n + 1)
                    for g in (2 * m, 2 * m + 1):
                        natural = lo_side(g)
                        nc.scalar.activation(s.queries[natural, g, c * BANK:(c + 1) * BANK], banks[n % 4][natural, :],
                                             ACT.Identity, bias=bq[natural, m:m + 1]).then_inc(copied, 1)
                    n += 1


UNITS = []
waiting = []
for c in range(len(CHUNKS)):
    for unit in [("k", m, c) for m in range(KD)] + [("v", j) for j in (2 * c, 2 * c + 1) if 2 * j < NT]:
        UNITS += [unit] + waiting[:2]
        waiting = waiting[2:]
    UNITS += waiting
    waiting = [("max", pair, c) for pair in range(HEADS // 2)]
UNITS += waiting
UNITS += [("row", m) for m in range(KD)]
WORK_BANKS = 3
NU = len(UNITS)
UNITS += [None] * (-NU % WORK_BANKS)
PLACES = 4
SPREAD = NU - KD
BESIDE = [[[u for u in range(SPREAD) if u * PLACES * (NT - 2) // SPREAD == t * PLACES + i] for i in range(PLACES)]
          for t in range(NT)]
BESIDE[-1][-1] = list(range(SPREAD, NU))
LAST_OF_CHUNK = [max(u for u in range(NU) if UNITS[u][0] == "v" and UNITS[u][1] // 2 == c)
                 for c in range(len(CHUNKS))]
K_UNITS = [u for u in range(NU) if UNITS[u][0] == "k"]
KRING = 2
CREDIT = 2
STORE_CREDIT = 16


def attention(nc, d, s, batches=BATCH):
    with ExitStack() as ctx:
        def sb(name, shape, dt=F32):
            return ctx.enter_context(nc.sbuf_tensor(name, shape, dt))

        def sem(name):
            return ctx.enter_context(nc.semaphore(name))

        ctx_hi = [sb(f"ctx_hi{i}", [P, KD, BANK], F32R) for i in range(2)]
        ctx_lo = [sb(f"ctx_lo{i}", [P, KD, BANK], F32R) for i in range(2)]
        keys = [sb(f"keys{i}", [P, GROUPS, KEYS_EVEN], F32R) for i in range(2)]
        k_whole = [sb(f"k_whole{i}", [P, BANK]) for i in range(KRING)]
        k_hi = [sb(f"k_hi{i}", [P, BANK], F32R) for i in range(KRING)]
        q_part = sb("q_part", [P, GROUPS, LATENTS])
        q_part_hi = sb("q_part_hi", [P, GROUPS, LATENTS], F32R)
        q_part_lo = sb("q_part_lo", [P, GROUPS, LATENTS], F32R)
        q_hi = [sb(f"q_hi{i}", [P, GROUPS, GCOLS], F32R) for i in range(2)]
        q_lo = [sb(f"q_lo{i}", [P, GROUPS, GCOLS], F32R) for i in range(2)]
        max_part = [sb(f"max_part{i}", [P, HEADS // 2, len(CHUNKS)]) for i in range(2)]
        neg_max = [sb(f"neg_max{i}", [P, HEADS // 2]) for i in range(2)]
        max_all = [sb(f"max_all{i}", [P, KD, BANK]) for i in range(2)]
        probs = [sb(f"probs{i}", [P, HEADS * LATENTS]) for i in range(2)]
        mixed = [sb(f"mixed{i}", [P, 4 * LATENTS]) for i in range(2)]
        work = [ctx.enter_context(nc.psum_tensor(f"work{i}", [P, BANK], F32)) for i in range(WORK_BANKS)]
        scores = [ctx.enter_context(nc.psum_tensor(f"scores{i}", [P, KD * BANK], F32)) for i in range(2)]
        acc = ctx.enter_context(nc.psum_tensor("acc", [P, BANK], F32))

        ctx_loaded = [sem(f"ctx_loaded{i}") for i in range(2)]
        hi_split = sem("hi_split")
        lo_split = sem("lo_split")
        unit_done = sem("unit_done")
        keys_hi = sem("keys_hi")
        keys_lo = sem("keys_lo")
        unit_evacuated = sem("unit_evacuated")
        unit_copied = sem("unit_copied")
        maxima_done = sem("maxima_done")
        q_parted = sem("q_parted")
        q_split = sem("q_split")
        scores_ready = sem("scores_ready")
        scores_shifted = sem("scores_shifted")
        exp_done = sem("exp_done")
        probs_used = sem("probs_used")
        acc_copied = sem("acc_copied")
        mixed_stored = [sem(f"mixed_stored{i}") for i in range(2)]
        block = ctx.enter_context(nc.Block())

        NC = len(CHUNKS)
        pairs = (batches - 1) // 2

        def wait_evacuated(engine, b, u):
            copied = UNITS[u][0] in ("k", "v")
            of_engine = [i for i in range(NU) if (UNITS[i][0] in ("k", "v")) == copied]
            engine.wait_ge(unit_copied if copied else unit_evacuated, b * len(of_engine) + of_engine.index(u) + 1)

        def wait_keys(engine, b, u):
            engine.wait_ge(keys_hi, b * len(K_UNITS) + K_UNITS.index(u) + 1)
            engine.wait_ge(keys_lo, (b * len(K_UNITS) + K_UNITS.index(u) + 1) * 2)

        @block.sync
        def _(sp):
            def load(b):
                for c, (start, size) in enumerate(CHUNKS):
                    g = b * NC + c
                    if not isinstance(b, int) or g >= 2:
                        sp.wait_ge(lo_split, g - 1)
                    sp.dma_start(s.ctx_whole[c % 2][:, :, 0:size],
                                 d.ctx_T[bass.ds(b, 1), :, start:start + size]
                                 .rearrange("a (k p) s -> p (a k) s", p=P)).then_inc(ctx_loaded[c % 2], 16)

            load(0)
            with sp.Fori(1, batches) as b:
                load(b)

        @block.gpsimd
        def _(pool):
            def mask_queries(b, par, tokens):
                if not isinstance(b, int) or b >= 1:
                    pool.wait_ge(probs_used, (b - 1) * NT + CREDIT)
                    pool.wait_ge(q_split, b * 2)
                one = s.one[:, :].rearrange("p (a b) -> p a b", a=1).to_broadcast([P, GROUPS, LATENTS])
                nc.gpsimd.tensor_tensor(q_part[:, :, :], tokens, one, ALU.mult)
                nc.gpsimd.tensor_tensor(q_part_hi[:, :, :], tokens, one, ALU.mult).then_inc(q_parted, 1)
                pool.wait_ge(q_parted, b * 2 + 1)
                nc.gpsimd.tensor_tensor(q_part_lo[:, :, :], q_part[:, :, :], q_part_hi[:, :, :].bitcast(F32), ALU.subtract) \
                    .then_inc(q_parted, 1)
                pool.wait_ge(q_parted, b * 2 + 2)
                for part, masked in ((q_part_hi, q_hi), (q_part_lo, q_lo)):
                    shape = [P, GROUPS, HPG, LATENTS]
                    nc.gpsimd.tensor_tensor(
                        masked[par][:, :, :].rearrange("p g (h l) -> p g h l", h=HPG),
                        part[:, :, :].bitcast(F32).rearrange("p g (a l) -> p g a l", a=1).to_broadcast(shape),
                        s.head_mask[:, :].rearrange("p (b h a) -> p b h a", b=1, a=1).to_broadcast(shape), ALU.mult) \
                        .then_inc(q_split, 1)

            def split(b, c):
                n = even(CHUNKS[c][1])
                pool.wait_ge(hi_split, b * NC + c + 1)
                nc.gpsimd.tensor_tensor(ctx_lo[c % 2][:, :, 0:n], s.ctx_whole[c % 2][:, :, 0:n],
                                        ctx_hi[c % 2][:, :, 0:n].bitcast(F32), ALU.subtract).then_inc(lo_split, 1)

            def split_keys(b, par, u, before):
                _, m, c = UNITS[u]
                start, n = CHUNKS[c][0], even(CHUNKS[c][1])
                i = K_UNITS.index(u)
                wait_evacuated(pool, b, u)
                for g in (2 * m, 2 * m + 1):
                    side = lo_side(g)
                    pool.wait_ge(*before)
                    nc.gpsimd.tensor_tensor(keys[par][side, g, start:start + n], k_whole[i % KRING][side, 0:n],
                                            k_hi[i % KRING][side, 0:n].bitcast(F32), ALU.subtract) \
                        .then_inc(keys_lo, 1)
                    before = (keys_lo, (b * len(K_UNITS) + i) * 2 + g % 2 + 1)
                return before

            def prepare(b, par, more=True):
                pool.wait_ge(lo_split, b * NC + 2)
                mask_queries(b, par, s.queries[:, :, bass.ds(b * LATENTS, LATENTS)])
                before = (q_split, b * 2 + 2)
                for u in range(NU):
                    if UNITS[u][0] == "k":
                        before = split_keys(b, par, u, before)
                    if u in LAST_OF_CHUNK:
                        c = LAST_OF_CHUNK.index(u) + 2
                        if c < NC or more:
                            pool.wait_ge(*before)
                            split(b + c // NC, c % NC)
                            before = (lo_split, (b + c // NC) * NC + c % NC + 1)

            split(0, 0)
            split(0, 1)
            prepare(0, 0)
            if pairs:
                with pool.Fori(0, pairs) as i:
                    prepare(i * 2 + 1, 1)
                    prepare(i * 2 + 2, 0)
            prepare(batches - 1, 1, more=False)

        @block.vector
        def _(dve):
            def split(b, c):
                g = b * NC + c
                n = even(CHUNKS[c][1])
                dve.wait_ge(ctx_loaded[c % 2], (b * (NC // 2) + c // 2 + 1) * 16)
                if not isinstance(b, int) or g >= 2:
                    before = LAST_OF_CHUNK[c - 2] + (NU if c >= 2 else 0)
                    dve.wait_ge(unit_done, (b - 1) * NU + before + 1)
                nc.vector.tensor_copy(ctx_hi[c % 2][:, :, 0:n], s.ctx_whole[c % 2][:, :, 0:n]) \
                    .then_inc(hi_split, 1)

            def unit(b, par, u):
                kind = UNITS[u][0]
                if kind == "k":
                    wait_evacuated(dve, b, u)
                else:
                    dve.wait_ge(unit_done, b * NU + u + 1)
                bank = work[u % WORK_BANKS]
                if kind == "k":
                    _, m, c = UNITS[u]
                    start, size = CHUNKS[c]
                    n = even(size)
                    i = K_UNITS.index(u)
                    for g in (2 * m, 2 * m + 1):
                        high = nc.vector.tensor_copy(keys[par][hi_side(g), g, start:start + n],
                                                     k_hi[i % KRING][lo_side(g), 0:n].bitcast(F32))
                    high.then_inc(keys_hi, 1)
                elif kind == "max":
                    _, pair, c = UNITS[u]
                    nc.vector.reduce_max(max_part[par][:, pair, c:c + 1], bank[:, 0:CHUNKS[c][1]], AX) \
                        .then_inc(unit_evacuated, 1)
                    if u == SPREAD - 1:
                        wait_evacuated(dve, b, u)
                        nc.vector.tensor_reduce(neg_max[par][:, :], max_part[par][:, :, :], AX, ALU.max, negate=True) \
                            .then_inc(maxima_done, 1)
                else:
                    nc.vector.tensor_copy(max_all[par][:, UNITS[u][1], :], bank[:, :]).then_inc(unit_evacuated, 1)

            def prepare(b, par, units, more):
                for u in units:
                    if UNITS[u][0] != "v":
                        unit(b, par, u)
                    if u in LAST_OF_CHUNK:
                        c = LAST_OF_CHUNK.index(u) + 2
                        if c < NC:
                            split(b, c)
                        elif more:
                            split(b + 1, c - NC)

            def shift(b, par, t):
                n = b * NT + t
                rows = TILES[t][1]
                bank = scores[(par * NT + t) % 2][0:rows, :]
                dve.wait_ge(scores_ready, n + 1)
                nc.vector.tensor_tensor(bank, bank, max_all[par][0:rows, :, :].rearrange("p m n -> p (m n)"),
                                        ALU.add).then_inc(scores_shifted, 1)

            def attend(b, par, ahead, more=True):
                wait_evacuated(dve, b, NU - 1)
                shift(b, par, 0)
                for t in range(NT):
                    for place in range(PLACES):
                        if place == 1 and t + 1 < NT:
                            shift(b, par, t + 1)
                        if ahead:
                            prepare(b + 1, 1 - par, BESIDE[t][place], more)

            nc.vector.memset(acc[:, :], 0.0)
            split(0, 0)
            split(0, 1)
            prepare(0, 0, range(NU), True)
            if pairs:
                with dve.Fori(0, pairs) as i:
                    attend(i * 2, 0, True)
                    attend(i * 2 + 1, 1, True)
            attend(batches - 2, 0, True, more=False)
            attend(batches - 1, 1, False)

        @block.scalar
        def _(act):
            def unit(b, par, u):
                if UNITS[u][0] == "k":
                    _, m, c = UNITS[u]
                    start, size = CHUNKS[c]
                    n = even(size)
                    act.wait_ge(unit_done, b * NU + u + 1)
                    i = K_UNITS.index(u)
                    if not isinstance(b, int) or b > 0 or i >= KRING:
                        act.wait_ge(keys_hi, b * len(K_UNITS) + i + 1 - KRING)
                        act.wait_ge(keys_lo, (b * len(K_UNITS) + i + 1 - KRING) * 2)
                    nc.scalar.activation(k_hi[i % KRING][:, 0:n], work[u % WORK_BANKS][:, 0:n],
                                         ACT.Identity, bias=s.bk[:, m:m + 1])
                    nc.scalar.activation(k_whole[i % KRING][:, 0:n], work[u % WORK_BANKS][:, 0:n],
                                         ACT.Identity, bias=s.bk[:, m:m + 1]).then_inc(unit_copied, 1)
                elif UNITS[u][0] == "v":
                    j = UNITS[u][1]
                    tiles = min(2, NT - 2 * j)
                    rows = TILES[2 * j][1]
                    act.wait_ge(unit_done, b * NU + u + 1)
                    nc.scalar.copy(
                        s.values[par][0:rows, 2 * j:2 * j + tiles, :, 0:HD],
                        work[u % WORK_BANKS][0:rows, 0:tiles * DIM].rearrange("p (t h e) -> p t h e", t=tiles, h=HEADS)) \
                        .then_inc(unit_copied, 1)

            def attend(b, par, ahead):
                for t in range(NT):
                    n = b * NT + t
                    slot = (par * NT + t) % 2
                    rows = TILES[t][1]
                    act.wait_ge(scores_shifted, n + 1)
                    act.wait_ge(probs_used, n + 1)
                    nc.scalar.activation(probs[slot][0:rows, :], scores[slot][0:rows, :], ACT.Exp,
                                         scale=1.0 / HD ** 0.5).then_inc(exp_done, 1)
                    if ahead:
                        for units in BESIDE[t]:
                            for u in units:
                                unit(b + 1, 1 - par, u)
                act.wait_ge(probs_used, b * NT + NT + CREDIT)
                act.wait_ge(mixed_stored[par], (b - par) * 8 + STORE_CREDIT)
                nc.scalar.copy(mixed[par][:, :], acc[:, par * DIM:(par + 1) * DIM]).then_inc(acc_copied, 1)
                act.wait_ge(acc_copied, b + 1 + CREDIT)
                act.dma_start(d.mixed[bass.ds(b, 1), :, :].rearrange("a p n -> p a n"),
                              mixed[par][:, :].rearrange("p (a n) -> p a n", a=1)).then_inc(mixed_stored[par], 16)

            act.sem_inc(exp_done, CREDIT)
            act.sem_inc(acc_copied, CREDIT)
            for par in range(2):
                act.sem_inc(mixed_stored[par], STORE_CREDIT)
            for u in range(NU):
                unit(0, 0, u)
            if pairs:
                with act.Fori(0, pairs) as i:
                    attend(i * 2, 0, True)
                    attend(i * 2 + 1, 1, True)
            attend(batches - 2, 0, True)
            attend(batches - 1, 1, False)
            for par in range(2):
                act.wait_ge(mixed_stored[par], 16 * (batches // 2) + STORE_CREDIT)

        @block.tensor
        def _(pe):
            def unit(b, par, u):
                if UNITS[u] is None:
                    return
                kind = UNITS[u][0]
                bank = work[u % WORK_BANKS]
                if not isinstance(b, int) or b * NU + u - WORK_BANKS >= 0:
                    if u >= WORK_BANKS:
                        wait_evacuated(pe, b, u - WORK_BANKS)
                    else:
                        wait_evacuated(pe, b - 1, min(u + len(UNITS) - WORK_BANKS, NU - 1))
                if kind == "k":
                    _, m, c = UNITS[u]
                    n = even(CHUNKS[c][1])
                    if m == 0:
                        pe.wait_ge(lo_split, b * NC + c + 1)
                    cols = slice(m * P, (m + 1) * P)
                    parts = [(w, x, k) for w, x in ((s.wk_hi, ctx_hi), (s.wk_hi, ctx_lo), (s.wk_lo, ctx_hi))
                             for k in range(KD)]
                    for i, (w, x, k) in enumerate(parts):
                        last = nc.tensor.matmul(bank[:, 0:n], w[:, k, cols], x[c % 2][:, k, 0:n],
                                                start=(i == 0), stop=(i == len(parts) - 1))
                elif kind == "v":
                    j = UNITS[u][1]
                    c = j // 2
                    for i, t in enumerate(range(2 * j, min(2 * j + 2, NT))):
                        start, rows = TILES[t]
                        at = start - CHUNKS[c][0]
                        parts = [(x, w, k) for k in range(KD)
                                 for x, w in ((ctx_hi, s.wv_hi), (ctx_hi, s.wv_lo), (ctx_lo, s.wv_hi))]
                        for n, (x, w, k) in enumerate(parts):
                            last = nc.tensor.matmul(bank[0:rows, i * DIM:(i + 1) * DIM],
                                                    x[c % 2][:, k, at:at + rows], w[:, k, :],
                                                    start=(n == 0), stop=(n == len(parts) - 1))
                elif kind == "max":
                    _, pair, c = UNITS[u]
                    start, size = CHUNKS[c]
                    if pair == 0:
                        pe.wait_ge(q_split, b * 2 + 2)
                        wait_keys(pe, b, UNITS.index(("k", KD - 1, c)))
                    g, at = pair // 2, (pair % 2) * P
                    last = nc.tensor.matmul(bank[:, 0:even(size)], q_hi[par][:, g, at:at + P],
                                            keys[par][:, g, start:start + even(size)], start=True, stop=True)
                else:
                    m = UNITS[u][1]
                    pe.wait_ge(maxima_done, b + 1)
                    for j in range(4):
                        last = nc.tensor.matmul(bank[:, j * P:(j + 1) * P],
                                                neg_max[par][:, 4 * m + j:4 * m + j + 1].to_broadcast([P, P]),
                                                s.ident[:, :], start=True, stop=True)
                last.then_inc(unit_done, 1)

            def score(b, par, t, m):
                start, rows = TILES[t]
                bank = scores[(par * NT + t) % 2]
                if m == 0:
                    pe.wait_ge(exp_done, b * NT + t + 1)
                    if t == 0:
                        wait_keys(pe, b, UNITS.index(("k", KD - 1, NC - 1)))
                for g in (2 * m, 2 * m + 1):
                    for q in (q_hi, q_lo):
                        last = nc.tensor.matmul(bank[0:rows, g * GCOLS:(g + 1) * GCOLS],
                                                keys[par][:, g, start:start + rows], q[par][:, g, :],
                                                start=(q is q_hi), stop=(q is q_lo))
                if m == KD - 1:
                    last.then_inc(scores_ready, 1)

            def mix(b, par, t, half):
                rows = TILES[t][1]
                if half == 0:
                    pe.wait_ge(exp_done, b * NT + t + 1 + CREDIT)
                if half == 0 and t == 0:
                    pe.wait_ge(acc_copied, b + 1)
                    wait_evacuated(pe, b, max(u for u in range(NU) if UNITS[u][0] == "v"))
                p = probs[(par * NT + t) % 2]
                for g in range(2 * half, 2 * half + 2):
                    for j in range(4):
                        h = 4 * g + j
                        last = nc.tensor.matmul(
                            acc[32 * j:32 * j + VW, par * DIM + g * LATENTS:par * DIM + (g + 1) * LATENTS],
                            s.values[par][0:rows, t, h, :], p[0:rows, h * LATENTS:(h + 1) * LATENTS],
                            start=(t == 0 and g == 0), stop=(t == NT - 1), skip_group_check=True)
                if half == 1:
                    last.then_inc(probs_used, 1)

            def attend(b, par, ahead):
                for t in range(NT):
                    for place in range(PLACES):
                        if place < 2:
                            if t + 1 < NT:
                                score(b, par, t + 1, place)
                            elif ahead:
                                score(b + 1, 1 - par, 0, place)
                        else:
                            mix(b, par, t, place - 2)
                        if ahead:
                            for u in BESIDE[t][place]:
                                unit(b + 1, 1 - par, u)

            pe.sem_inc(probs_used, CREDIT)
            for u in range(NU):
                unit(0, 0, u)
            score(0, 0, 0, 0)
            score(0, 0, 0, 1)
            if pairs:
                with pe.Fori(0, pairs) as i:
                    attend(i * 2, 0, True)
                    attend(i * 2 + 1, 1, True)
            attend(batches - 2, 0, True)
            attend(batches - 1, 1, False)


def attention_memory(nc, ctx):
    def sb(name, shape, dt=F32):
        return ctx.enter_context(nc.sbuf_tensor(name, shape, dt))
    s = Names()
    s.queries, s.head_mask, s.bk = sb("queries", [P, GROUPS, TOK]), sb("head_mask", [P, HPG]), sb("bk", [P, KD])
    s.one = sb("one", [P, 1])
    s.wk_hi, s.wk_lo = sb("wk_hi", [P, KD, DIM], F32R), sb("wk_lo", [P, KD, DIM], F32R)
    s.wv_hi, s.wv_lo = sb("wv_hi", [P, KD, DIM], F32R), sb("wv_lo", [P, KD, DIM], F32R)
    s.ctx_whole = [sb(f"ctx_whole{i}", [P, KD, BANK]) for i in range(2)]
    s.values = [sb(f"values{i}", [P, NT, HEADS, VW]) for i in range(2)]
    return s


def attention_output(nc, d, s, xn, xn_T):
    with ExitStack() as ctx:
        def sb(name, shape, dt=F32):
            return ctx.enter_context(nc.sbuf_tensor(name, shape, dt))

        def sem(name):
            return ctx.enter_context(nc.semaphore(name))

        G = HEADS // 4
        SPREAD_RING, OUTS_RING = 2, 3
        PAIR = P // LATENTS
        CB = BANK // LATENTS
        CT = BANK // P
        mixed = sb("mixed_b", [P, BATCH, G, LATENTS])
        mixed_T = sb("mixed_T", [P, G, TOK])
        row_of = sb("row_of", [P, P, 32])
        inverse = sb("inverse", [P, G * LATENTS])
        wo = sb("wo", [P, G, DIM])
        bv = sb("bv", [P, G])
        bo = sb("bo", [P, DIM])
        spread = [ctx.enter_context(nc.psum_tensor(f"o_spread{i}", [P, PAIR, G * LATENTS], F32)) for i in range(SPREAD_RING)]
        outs = [ctx.enter_context(nc.psum_tensor(f"o_outs{i}", [P, BANK], F32)) for i in range(OUTS_RING)]
        loaded, cleared, sums_loaded = sem("o_loaded"), sem("o_cleared"), sem("o_sums_loaded")
        mixed_loaded = [sem(f"mixed_loaded{c}") for c in range(TOK // BANK)]
        row_of_made = sem("row_of_made")
        inverted, spread_done, divided, biased = (
            sem("o_inverted"), sem("o_spread_done"), sem("o_divided"), sem("o_biased"))
        projected, added, bias_added = sem("o_projected"), sem("o_added"), sem("o_bias_added")
        NCH = TOK // BANK

        def sp_start(sp):
            sp.dma_start(inverse[:, :], d.mixed.rearrange("b (j i) n -> b j i n", i=32)[:, :, HD, :]
                         .rearrange("b j n -> (b j) n")).then_inc(sums_loaded, 16)
            for c in range(NCH):
                batches = slice(c * CB, (c + 1) * CB)
                sp.dma_start(mixed[:, batches, :, :].rearrange("p b g l -> p b (g l)"),
                             d.mixed.rearrange("b p n -> p b n")[:, batches, :]).then_inc(mixed_loaded[c], 16)
            load_ssm_weights(sp, d, s)

        def add_values_bias(act, c):
            act.wait_ge(divided, CT * (c + 1))
            for g in range(G):
                part = mixed_T[:, g, c * BANK:(c + 1) * BANK]
                nc.scalar.activation(part, part, ACT.Identity, bias=bv[:, g:g + 1]).then_inc(biased, 1)

        def act_start(act):
            act.dma_start(bo[:, :], d.b_O.rearrange("(a n) -> a n", a=1).to_broadcast([P, DIM])).then_inc(loaded, 16)
            act.wait_ge(cleared, 2)
            for j in range(4):
                rows = slice(32 * j, 32 * j + HD)
                act.dma_start(wo[rows, :, :], d.W_O.rearrange("(g c e) n -> c e g n", c=4, e=HD)[j]) \
                    .then_inc(loaded, 16)
                act.dma_start(bv[rows, :], d.b_V.rearrange("(g c e) -> c e g", c=4, e=HD)[j],
                              allow_slow_non_contiguous=True).then_inc(loaded, 16)
            act.wait_ge(loaded, 16 * 9)
            add_values_bias(act, 0)

        def act_before(act, c):
            if c == 0:
                act_start(act)
            if c + 1 < NCH:
                add_values_bias(act, c + 1)

        def pool_start(pool):
            clear_ssm_weights(nc, s)
            nc.gpsimd.memset(wo[:, :, :], 0.0).then_inc(cleared, 1)
            nc.gpsimd.memset(bv[:, :], 0.0).then_inc(cleared, 1)
            nc.gpsimd.memset(row_of[:, :, :], 0.0).then_inc(row_of_made, 1)
            pool.wait_ge(row_of_made, 1)
            nc.gpsimd.affine_select(out=row_of[:, :, :], in_=row_of[:, :, :], compare_op=ALU.not_equal, fill=1.0,
                                    base=0, pattern=[[-1, P], [0, 32]], channel_multiplier=1) \
                .then_inc(row_of_made, 1)
            pool.wait_ge(loaded, 16 * 9)
            nc.gpsimd.tensor_tensor(s.x_tok[:, :, :], s.x_tok[:, :, :],
                                    bo[:, :].rearrange("p (a n) -> p a n", a=1).to_broadcast([P, TT, DIM]), ALU.add) \
                .then_inc(bias_added, 1)

        def spread_inverses(pe, c):
            for t in range(CT * c, CT * (c + 1)):
                if t >= SPREAD_RING:
                    pe.wait_ge(divided, t + 1 - SPREAD_RING)
                for i in range(PAIR):
                    b = PAIR * t + i
                    last = nc.tensor.matmul(spread[t % SPREAD_RING][:, i, :],
                                            row_of[:, 4 * b:4 * b + 4, :].rearrange("p j i -> p (j i)"), inverse[:, :],
                                            start=True, stop=True)
                last.then_inc(spread_done, 1)

        def project(pe, c):
            pe.wait_ge(biased, G * (c + 1))
            for t in range(CT * c, CT * (c + 1)):
                if t >= OUTS_RING:
                    pe.wait_ge(added, t + 1 - OUTS_RING)
                for g in range(G):
                    last = nc.tensor.matmul(outs[t % OUTS_RING][:, 0:DIM], mixed_T[:, g, t * P:(t + 1) * P], wo[:, g, :],
                                            start=(g == 0), stop=(g == G - 1))
                last.then_inc(projected, 1)

        def pe_before(pe, c):
            if c == 0:
                pe.wait_ge(row_of_made, 2)
                pe.wait_ge(inverted, 1)
                spread_inverses(pe, 0)
                pe.wait_ge(loaded, 16 * 9)
            if c + 1 < NCH:
                spread_inverses(pe, c + 1)
            project(pe, c)

        def divide(dve, c):
            dve.wait_ge(mixed_loaded[c], 16)
            for t in range(CT * c, CT * (c + 1)):
                dve.wait_ge(spread_done, t + 1)
                nc.vector.tensor_tensor(
                    mixed_T[:, :, t * P:(t + 1) * P].rearrange("p g (b l) -> p b g l", l=LATENTS),
                    mixed[:, PAIR * t:PAIR * (t + 1), :, :],
                    spread[t % SPREAD_RING][:, :, :].rearrange("p b (g l) -> p b g l", l=LATENTS), ALU.mult) \
                    .then_inc(divided, 1)

        def dve_before(dve, c):
            if c == 0:
                dve.wait_ge(sums_loaded, 16)
                nc.vector.reciprocal(inverse[:, :], inverse[:, :]).then_inc(inverted, 1)
                divide(dve, 0)
            if c + 1 < NCH:
                divide(dve, c + 1)
            dve.wait_ge(bias_added, 1)
            for t in range(CT * c, CT * (c + 1)):
                dve.wait_ge(projected, t + 1)
                nc.vector.tensor_tensor(s.x_tok[:, t, :], s.x_tok[:, t, :], outs[t % OUTS_RING][:, 0:DIM], ALU.add) \
                    .then_inc(added, 1)
            dve.wait_ge(added, CT * (c + 1))

        normalize_and_transpose(nc, "ln2", s.x_tok, xn, xn_T, s.ident, sp_start=sp_start, pool_start=pool_start,
                                pe_before=pe_before, act_before=act_before, dve_before=dve_before)


HALF = 1024
BC_COLS = 96
NCH = TOK // BANK


def ssm_weights(nc, ctx, s):
    def sb(name, shape):
        return ctx.enter_context(nc.sbuf_tensor(name, shape, F32))

    s.win, s.bin = sb("win", [P, KD, 2 * INNER]), sb("bin", [P, 2 * KI])
    s.wx, s.bx = sb("wx", [P, KI, BC_COLS]), sb("bx", [BC_COLS, 1])
    s.wdt, s.bdt = sb("wdt", [RANK, INNER]), sb("bdt", [P, KI])
    s.ssm_loaded = ctx.enter_context(nc.semaphore("ssm_loaded"))
    s.ssm_cleared = ctx.enter_context(nc.semaphore("ssm_cleared"))


def clear_ssm_weights(nc, s):
    nc.gpsimd.memset(s.wx[:, :, :], 0.0).then_inc(s.ssm_cleared, 1)
    nc.gpsimd.memset(s.bx[:, :], 0.0).then_inc(s.ssm_cleared, 1)


def load_ssm_weights(sp, d, s):
    sp.dma_start(s.win[:, :, :], d.Win.rearrange("(k p) n -> p k n", p=P)).then_inc(s.ssm_loaded, 16)
    sp.dma_start(s.bin[:, :], column_tiles(d.bin), allow_slow_non_contiguous=True).then_inc(s.ssm_loaded, 16)
    sp.dma_start(s.wdt[:, :], d.Wdt).then_inc(s.ssm_loaded, 16)
    sp.dma_start(s.bdt[:, :], column_tiles(d.bdt), allow_slow_non_contiguous=True).then_inc(s.ssm_loaded, 16)
    sp.dma_start(s.dp[:, :], column_tiles(d.Dp), allow_slow_non_contiguous=True).then_inc(s.ssm_loaded, 16)
    sp.dma_start(s.a[:, :, :], d.A_log.rearrange("(k p) n -> p k n", p=P)).then_inc(s.ssm_loaded, 16)
    sp.wait_ge(s.ssm_cleared, 2)
    wx_v = d.Wx.rearrange("(k p) n -> p k n", p=P)
    bx_v = d.bx.rearrange("(p a) -> p a", a=1)
    for i in range(3):
        sp.dma_start(s.wx[:, :, 32 * i:32 * i + STATE], wx_v[:, :, STATE * i:STATE * (i + 1)]) \
            .then_inc(s.ssm_loaded, 16)
        sp.dma_start(s.bx[32 * i:32 * i + STATE, :], bx_v[STATE * i:STATE * (i + 1), :]).then_inc(s.ssm_loaded, 16)
    sp.wait_ge(s.ssm_loaded, 16 * 12)


def ssm_projections(nc, d, s, xn_T):
    with ExitStack() as ctx:
        def sb(name, shape, dt=F32):
            return ctx.enter_context(nc.sbuf_tensor(name, shape, dt))

        def sem(name):
            return ctx.enter_context(nc.semaphore(name))

        BANKS, RING, ZRING = 8, 6, 4
        PIECES = KI * NCH
        XP, DT, Z = PIECES, PIECES + NCH, 2 * PIECES + NCH
        xp = sb("xp", [BC_COLS, TOK])
        z = [sb(f"z{i}", [P, BANK]) for i in range(ZRING)]
        log = [sb(f"log{i}", [P, BANK]) for i in range(RING)]
        lost = [sb(f"lost{i}", [P, BANK]) for i in range(RING)]
        banks = [ctx.enter_context(nc.psum_tensor(f"s_bank{i}", [P, BANK], F32)) for i in range(BANKS)]
        filled = sem("s_filled")
        xs_done, xp_done, z_done = sem("xs_done"), sem("xp_done"), sem("z_done")
        z_stored = [sem(f"z_stored{i}") for i in range(ZRING)]
        bc_stored = sem("bc_stored")
        dt_raw, dt_abs, dt_exp, dt_log = sem("dt_raw"), sem("dt_abs"), sem("dt_exp"), sem("dt_log")
        rounded, lost_ready = sem("dt_rounded"), sem("dt_lost_ready")
        clamped, dt_done = sem("dt_clamped"), sem("dt_done")
        block = ctx.enter_context(nc.Block())

        def piece(n):
            m, c = divmod(n, NCH)
            return m, slice(c * BANK, (c + 1) * BANK)

        @block.sync
        def _(sp):
            sp.wait_ge(xp_done, NCH)
            for i in range(2):
                sp.dma_start(d.bc[i, :, :], xp[32 * (i + 1):32 * (i + 1) + STATE, :]).then_inc(bc_stored, 16)
            for n in range(PIECES):
                m, cols = piece(n)
                sp.wait_ge(z_done, n + 1)
                sp.dma_start(d.z[m, :, cols], z[n % ZRING][:, :]).then_inc(z_stored[n % ZRING], 16)
            for i in range(ZRING):
                sp.wait_ge(z_stored[i], 16 * PIECES // ZRING)
            sp.wait_ge(bc_stored, 32)

        @block.gpsimd
        def _(pool):
            def lose(n):
                m, cols = piece(n)
                pool.wait_ge(rounded, n + 1)
                nc.gpsimd.tensor_tensor(lost[n % RING][:, :], s.delta[:, m, cols], lost[n % RING][:, :],
                                        ALU.subtract).then_inc(lost_ready, 1)

            for n in range(RING):
                lose(n)
            for n in range(PIECES):
                m, cols = piece(n)
                pool.wait_ge(dt_done, n + 1)
                nc.gpsimd.tensor_tensor(s.dtx[:, m, cols], s.delta[:, m, cols], s.xs[:, m, cols], ALU.mult)
                if n + RING < PIECES:
                    lose(n + RING)

        @block.tensor
        def _(pe):
            def bank(n):
                former = n - BANKS
                if former >= Z:
                    pe.wait_ge(z_done, former - Z + 1)
                elif former >= DT:
                    pe.wait_ge(dt_raw, former - DT + 1)
                elif former >= XP:
                    pe.wait_ge(xp_done, former - XP + 1)
                elif former >= 0:
                    pe.wait_ge(xs_done, former + 1)
                return banks[n % BANKS]

            def from_tokens(n, m, cols):
                out = bank(n)
                for k in range(KD):
                    last = nc.tensor.matmul(out[:, :], s.win[:, k, m * P:(m + 1) * P], xn_T[:, k, cols],
                                            start=(k == 0), stop=(k == KD - 1))
                last.then_inc(filled, 1)

            for n in range(PIECES):
                from_tokens(n, *piece(n))
            for c in range(NCH):
                cols = slice(c * BANK, (c + 1) * BANK)
                out = bank(XP + c)
                pe.wait_ge(xs_done, (KI - 1) * NCH + c + 1)
                for k in range(KI):
                    last = nc.tensor.matmul(out[0:BC_COLS, :], s.wx[:, k, :], s.xs[:, k, cols],
                                            start=(k == 0), stop=(k == KI - 1))
                last.then_inc(filled, 1)
            for n in range(PIECES):
                m, cols = piece(n)
                out = bank(DT + n)
                pe.wait_ge(xp_done, n % NCH + 1)
                nc.tensor.matmul(out[:, :], s.wdt[:, m * P:(m + 1) * P], xp[0:RANK, cols],
                                 start=True, stop=True).then_inc(filled, 1)
            for n in range(PIECES):
                m, cols = piece(n)
                from_tokens(Z + n, KI + m, cols)

        @block.scalar
        def _(act):
            for n in range(PIECES):
                m, cols = piece(n)
                act.wait_ge(filled, n + 1)
                nc.scalar.activation(s.xs[:, m, cols], banks[n % BANKS][:, :], ACT.Silu, bias=s.bin[:, m:m + 1]) \
                    .then_inc(xs_done, 1)
            for c in range(NCH):
                act.wait_ge(filled, XP + c + 1)
                nc.scalar.activation(xp[:, c * BANK:(c + 1) * BANK], banks[(XP + c) % BANKS][0:BC_COLS, :],
                                     ACT.Identity, bias=s.bx[:, 0:1]).then_inc(xp_done, 1)
            nc.scalar.activation(s.a[:, :, :], s.a[:, :, :], ACT.Exp)
            def raw(n):
                m, cols = piece(n)
                act.wait_ge(filled, DT + n + 1)
                nc.scalar.activation(s.dtx[:, m, cols], banks[(DT + n) % BANKS][:, :], ACT.Identity,
                                     bias=s.bdt[:, m:m + 1]).then_inc(dt_raw, 1)

            raw(0)
            for n in range(PIECES):
                m, cols = piece(n)
                if n + 1 < PIECES:
                    raw(n + 1)
                e = s.delta[:, m, cols]
                act.wait_ge(dt_abs, n + 1)
                nc.scalar.activation(e, e, ACT.Exp).then_inc(dt_exp, 1)
            for n in range(PIECES):
                m, cols = piece(n)
                act.wait_ge(dt_exp, n + 1)
                if n >= RING:
                    act.wait_ge(dt_done, n - RING + 1)
                nc.scalar.activation(log[n % RING][:, :], s.delta[:, m, cols], ACT.Ln, bias=1.0).then_inc(dt_log, 1)
            for n in range(PIECES):
                m, cols = piece(n)
                act.wait_ge(filled, Z + n + 1)
                if n >= ZRING:
                    act.wait_ge(z_stored[n % ZRING], 16 * (n // ZRING))
                nc.scalar.activation(z[n % ZRING][:, :], banks[(Z + n) % BANKS][:, :], ACT.Silu,
                                     bias=s.bin[:, KI + m:KI + m + 1]).then_inc(z_done, 1)

        @block.vector
        def _(dve):
            def round_off(n):
                m, cols = piece(n)
                dve.wait_ge(dt_exp, n + 1)
                nc.vector.tensor_scalar(lost[n % RING][:, :], s.delta[:, m, cols], 1.0, -1.0, ALU.add, ALU.add) \
                    .then_inc(rounded, 1)

            for n in range(PIECES):
                m, cols = piece(n)
                v = s.dtx[:, m, cols]
                dve.wait_ge(dt_raw, n + 1)
                nc.vector.scalar_tensor_tensor(s.delta[:, m, cols], v, -1.0, v, ALU.mult, ALU.min) \
                    .then_inc(dt_abs, 1)
                if n > 0 and n - 1 < RING:
                    round_off(n - 1)
            for n in range(PIECES):
                m, cols = piece(n)
                l, v, delta = log[n % RING][:, :], s.dtx[:, m, cols], s.delta[:, m, cols]
                dve.wait_ge(dt_log, n + 1)
                nc.vector.scalar_tensor_tensor(l, v, 0.0, l, ALU.max, ALU.add).then_inc(clamped, 1)
                if n >= 2 and n - 2 + RING < PIECES:
                    dve.wait_ge(dt_done, n - 1)
                    round_off(n - 2 + RING)
                dve.wait_ge(clamped, n + 1)
                dve.wait_ge(lost_ready, n + 1)
                nc.vector.tensor_tensor(delta, l, lost[n % RING][:, :], ALU.add).then_inc(dt_done, 1)


def ssm_scan(nc, d, s):
    with ExitStack() as ctx:
        def sb(name, shape, dt=F32):
            return ctx.enter_context(nc.sbuf_tensor(name, shape, dt))

        def sem(name):
            return ctx.enter_context(nc.semaphore(name))

        b_all = [sb(f"b_all{i}", [P, HALF]) for i in range(2)]
        c_all = [sb(f"c_all{i}", [P, HALF]) for i in range(2)]
        da, dbx = s.da, s.dbx
        h = [sb(f"h{i}", [P, HALF]) for i in range(KI)]
        hc = [sb(f"hc{i}", [P, HALF]) for i in range(2)]
        z = [sb(f"zg{i}", [P, HALF]) for i in range(2)]
        y = [ctx.enter_context(nc.psum_tensor(f"y{k}", [P, HALF], F32)) for k in range(KI)]
        b_loaded = [sem(f"b_loaded{i}") for i in range(2)]
        c_loaded = [sem(f"c_loaded{i}") for i in range(2)]
        da_cut, da_done, dbx_done, h_done, hc_done, summed = (
            sem("da_cut"), sem("da_done"), sem("dbx_done"), sem("h_done"), sem("hc_done"), sem("y_summed"))
        z_loaded = [sem(f"z_loaded{i}") for i in range(2)]
        skip = sb("skip", [P, KI, P])
        skip_made, y_done = sem("skip_made"), sem("y_done")
        a_signed, wout_loaded = sem("a_signed"), sem("wout_loaded")
        block = ctx.enter_context(nc.Block())
        HALVES = TOK // HALF
        STEPS = STATE * KI

        def each_state(engine, half, body):
            first = half * STEPS
            body(0, 0, first)
            body(1, 1, first + KI)
            with engine.Fori(0, (STATE - 4) // 2) as i:
                body(i * 2 + 2, 0, i * (2 * KI) + first + 2 * KI)
                body(i * 2 + 3, 1, i * (2 * KI) + first + 3 * KI)
            body(STATE - 2, 0, first + (STATE - 2) * KI)
            body(STATE - 1, 1, first + (STATE - 1) * KI)

        @block.sync
        def _(sp):
            sp.dma_start(s.wout[:, :, :], d.Wout.rearrange("(k p) n -> p k n", p=P)).then_inc(wout_loaded, 16)
            sp.dma_start(s.bout[:, :], d.bout.rearrange("(a n) -> a n", a=1).to_broadcast([P, DIM])) \
                .then_inc(wout_loaded, 16)
            for half in range(HALVES):
                cols = slice(half * HALF, (half + 1) * HALF)

                def load(n, par, r):
                    for i, (dst, used, loaded) in enumerate(((b_all, dbx_done, b_loaded), (c_all, hc_done, c_loaded))):
                        at_least(sp, used, r - KI)
                        sp.dma_start(dst[par][:, :], d.bc[i, bass.ds(n, 1), cols].to_broadcast([P, HALF])) \
                            .then_inc(loaded[par], 16)

                each_state(sp, half, load)
                for k in range(KI):
                    zi = half * KI + k
                    if zi >= 2:
                        sp.wait_ge(y_done, zi - 1)
                    sp.dma_start(z[zi % 2][:, :], d.z[k, :, cols]).then_inc(z_loaded[zi % 2], 16)
            sp.wait_ge(wout_loaded, 32)

        @block.scalar
        def _(act):
            act.wait_ge(a_signed, 1)
            act.wait_ge(da_cut, KI)
            for half in range(HALVES):
                def decay(n, par, r):
                    for k in range(KI):
                        at_least(act, h_done, r + k + 1 - KI)
                        nc.scalar.activation(by_batch(da[k])[:, :, 1:],
                                             by_batch(s.delta[:, k, half * HALF:(half + 1) * HALF])[:, :, 1:],
                                             ACT.Exp, scale=s.a[:, k, bass.ds(n, 1)]).then_inc(da_done, 1)

                each_state(act, half, decay)

        @block.gpsimd
        def _(pool):
            for i in range(KI):
                nc.gpsimd.memset(by_batch(da[i])[:, :, 0:1], 0.0).then_inc(da_cut, 1)
            for half in range(HALVES):
                def terms(n, par, r):
                    pool.wait_ge(b_loaded[par], loads(half, n, par))
                    for k in range(KI):
                        at_least(pool, h_done, r + k + 1 - KI)
                        nc.gpsimd.tensor_tensor(dbx[k], s.dtx[:, k, half * HALF:(half + 1) * HALF],
                                                b_all[par][:, :], ALU.mult).then_inc(dbx_done, 1)

                each_state(pool, half, terms)

        @block.vector
        def _(dve):
            def scan(r, k):
                dve.wait_ge(da_done, r + k + 1)
                dve.wait_ge(dbx_done, r + k + 1)
                at_least(dve, hc_done, r + k + 1 - KI)
                nc.vector.tensor_tensor_scan(h[k][:, :], da[k], dbx[k], 0.0,
                                             ALU.mult, ALU.add).then_inc(h_done, 1)

            def times_c(half, n, par, r, k):
                if k == 0:
                    dve.wait_ge(c_loaded[par], loads(half, n, par))
                dve.wait_ge(h_done, r + k + 1)
                at_least(dve, summed, r + k - 1)
                nc.vector.tensor_tensor(hc[k % 2][:, :], h[k][:, :], c_all[par][:, :], ALU.mult) \
                    .then_inc(hc_done, 1)

            nc.vector.tensor_scalar(s.a[:, :, :], s.a[:, :, :], -1.0, None, ALU.mult).then_inc(a_signed, 1)
            for k in range(KI):
                nc.vector.tensor_scalar(skip[:, k, :], s.ident[:, :], s.dp[:, k:k + 1], None, ALU.mult) \
                    .then_inc(skip_made, 1)
            dve.wait_ge(da_cut, KI)
            for half in range(HALVES):
                def states(n, par, r):
                    for k in range(KI):
                        scan(r, k)
                        if k > 0:
                            times_c(half, n, par, r, k - 1)
                        elif not isinstance(n, int) or n > 0:
                            times_c(half, n - 1, 1 - par, r - KI, KI - 1)

                each_state(dve, half, states)
                times_c(half, STATE - 1, 1, half * STEPS + STEPS - KI, KI - 1)
                for k in range(KI):
                    out = half * KI + k
                    cols = slice(half * HALF, (half + 1) * HALF)
                    dve.wait_ge(summed, (half + 1) * STEPS - KI + k + 1)
                    dve.wait_ge(z_loaded[out % 2], 16 * (out // 2 + 1))
                    nc.vector.tensor_tensor(s.y[:, k, cols], y[k][:, :], z[out % 2][:, :], ALU.mult).then_inc(y_done, 1)

        @block.tensor
        def _(pe):
            pe.wait_ge(skip_made, KI)
            for half in range(HALVES):
                def start_sums():
                    for k in range(KI):
                        if half > 0:
                            pe.wait_ge(y_done, (half - 1) * KI + k + 1)
                        for c in range(HALF // BANK):
                            at = half * HALF + c * BANK
                            nc.tensor.matmul(y[k][:, c * BANK:(c + 1) * BANK], skip[:, k, :], s.xs[:, k, at:at + BANK],
                                             start=True, stop=False)

                def add_up(n, par, r):
                    for k in range(KI):
                        pe.wait_ge(hc_done, r + k + 1)
                        for c in range(HALF // BANK):
                            cols = slice(c * BANK, (c + 1) * BANK)
                            last = nc.tensor.matmul(y[k][:, cols], s.ident[:, :], hc[k % 2][:, cols], start=False,
                                                    stop=(isinstance(n, int) and n == STATE - 1))
                        last.then_inc(summed, 1)

                start_sums()
                each_state(pe, half, add_up)


def by_batch(a):
    return a.rearrange("p (b l) -> p b l", l=LATENTS)


def loads(half, n, par):
    return (n - par) * 8 + 16 + half * STATE * 8


def at_least(engine, semaphore, value):
    if not isinstance(value, int) or value > 0:
        engine.wait_ge(semaphore, value)


def ssm_output(nc, d, s, xn, xn_T, logits_bank):
    with ExitStack() as ctx:
        RING = 3
        banks = [ctx.enter_context(nc.psum_tensor(f"out_bank{i}", [P, BANK], F32)) for i in range(RING)]
        rw = ctx.enter_context(nc.sbuf_tensor("rw", [P, KD, EXPERTS], F32))
        rw_loaded = ctx.enter_context(nc.semaphore("rw_loaded"))
        projected = ctx.enter_context(nc.semaphore("out_projected"))
        added = ctx.enter_context(nc.semaphore("out_added"))
        bias_added = ctx.enter_context(nc.semaphore("out_bias_added"))

        def sp_start(sp):
            sp.dma_start(rw[:, :, :], d.router_w_T.rearrange("(k p) e -> p k e", p=P)).then_inc(rw_loaded, 16)

        def pool_start(pool):
            for t in range(TT):
                nc.gpsimd.tensor_tensor(s.x_tok[:, t, :], s.x_tok[:, t, :], s.bout[:, :], ALU.add) \
                    .then_inc(bias_added, 1)

        def pe_before(pe, g):
            for t in range(g * GT, (g + 1) * GT):
                if t >= RING:
                    pe.wait_ge(added, t + 1 - RING)
                for k in range(KI):
                    last = nc.tensor.matmul(banks[t % RING][:, 0:DIM], s.y[:, k, t * P:(t + 1) * P], s.wout[:, k, :],
                                            start=(k == 0), stop=(k == KI - 1))
                last.then_inc(projected, 1)

        def pe_after(pe, g):
            pe.wait_ge(rw_loaded, 16)
            for t in range(g * GT, (g + 1) * GT):
                for k in range(KD):
                    nc.tensor.matmul(logits_bank[:, t * EXPERTS:(t + 1) * EXPERTS], xn_T[:, k, t * P:(t + 1) * P],
                                     rw[:, k, :], start=(k == 0), stop=(k == KD - 1))

        def dve_before(dve, g):
            for t in range(g * GT, (g + 1) * GT):
                dve.wait_ge(bias_added, t + 1)
                dve.wait_ge(projected, t + 1)
                nc.vector.tensor_tensor(s.x_tok[:, t, :], s.x_tok[:, t, :], banks[t % RING][:, 0:DIM], ALU.add) \
                    .then_inc(added, 1)
            dve.wait_ge(added, (g + 1) * GT)

        normalize_and_transpose(nc, "ln3", s.x_tok, xn, xn_T, s.ident, sp_start=sp_start, pool_start=pool_start,
                                pe_before=pe_before, dve_before=dve_before, pe_after=pe_after)


SLOTS = 256
BLOCKS = (2 * TOK + EXPERTS * (SLOTS - 1)) // SLOTS
ST = SLOTS // P
SLOT_TILES = BLOCKS * ST
MAX_NB = TOK // SLOTS
U32 = mybir.dt.uint32


def route(nc, d, s, xn, logits_bank):
    with ExitStack() as ctx:
        def sb(name, shape, dt=F32):
            return ctx.enter_context(nc.sbuf_tensor(name, shape, dt))

        def sem(name):
            return ctx.enter_context(nc.semaphore(name))

        E = EXPERTS
        zeros = sb("zeros", [P, DIM])
        rb = sb("rb", [P, E])
        earlier = sb("earlier", [P, P])
        ones = sb("ones", [P, P])
        lower = sb("lower", [P, E, E])
        fill_levels = sb("fill_levels", [P, MAX_NB])
        block_index = sb("block_index", [P, BLOCKS])
        logits = sb("logits", [P, TT, E])
        top = sb("top", [P, TT])
        coef = sb("coef", [P, TT, E])
        before = sb("before", [P, TT, E, E])
        same = sb("same", [P, TT, E, E])
        chosen = sb("chosen", [P, TT, E])
        total = sb("total", [P, TT])
        counts = sb("counts", [P, TT + 1, E])
        filled = sb("filled", [P, E, MAX_NB])
        n_blocks = sb("n_blocks", [P, E])
        starts = sb("starts", [P, E, E])
        start = sb("start", [P, E])
        ends = sb("ends", [P, E])
        passed = sb("passed", [P, BLOCKS, E])
        block_f = sb("block_f", [P, BLOCKS])
        place = sb("place", [P, TT, E])
        masked = sb("masked", [P, TT, E])
        hit = sb("hit", [P, TT, E])
        slot = sb("slot", [P, TT, 2])
        tile_starts = sb("tile_starts", [P, SLOT_TILES + 1])
        reached = sb("reached", [P, 2 * TT, SLOT_TILES + 1])
        in_tile = sb("in_tile", [P, 2 * TT, SLOT_TILES])
        at_tile = sb("at_tile", [P, 2 * TT, 2, SLOT_TILES], F32R)
        tile_count = sb("tile_count", [P, 2 * TT])
        in_row = sb("in_row", [P, 2 * TT, P], F32R)
        row_index = sb("row_index", [P, P])
        tile_number = sb("tile_number", [P, 2 * TT])
        partition = sb("partition", [P, 1])
        empty_row = sb("empty_row", [P, 1])
        empty = sb("empty", [P, SLOT_TILES])
        read = sb("read", [P, SLOT_TILES])
        slots_bank = ctx.enter_context(nc.psum_tensor("slots_bank", [P, 2, SLOT_TILES], F32))
        prefix_bank = ctx.enter_context(nc.psum_tensor("r_prefix", [P, TT * E], F32))
        total_bank = ctx.enter_context(nc.psum_tensor("r_total", [P, TT * E], F32))
        loaded = sem("r_loaded")
        made = sem("r_made")
        zeros_made = sem("r_zeros_made")
        rows_stored, blocks_known = sem("rows_stored"), sem("blocks_known")
        in_tile_ready, in_row_ready, slots_found = sem("in_tile_ready"), sem("in_row_ready"), sem("slots_found")
        step = sem("r_step")
        shifted = sem("r_shifted")
        exped = sem("r_exp")
        chosen_ready = sem("chosen_ready")
        counted = sem("r_counted")
        block = ctx.enter_context(nc.Block())

        @block.sync
        def _(sp):
            sp.dma_start(rb[:, :], d.router_b.rearrange("(a e) -> a e", a=1).to_broadcast([P, E])).then_inc(loaded, 16)
            for i in range(2):
                sp.dma_start(d.rows[0:2 * TOK, :].rearrange("(t i p) n -> p t i n", p=P, i=2)[:, :, i, :], xn[:, :, :]) \
                    .then_inc(rows_stored, 16)
            sp.wait_ge(zeros_made, 1)
            sp.dma_start(d.rows[2 * TOK:2 * TOK + P, :], zeros[:, :]).then_inc(rows_stored, 16)
            sp.dma_start(s.b1_all[:, :, :], d.b1_T.rearrange("e p k -> p e k")).then_inc(s.biases_loaded, 16)
            sp.dma_start(s.b2_all[:, :, :], d.b2.rearrange("(a e) n -> a e n", a=1).to_broadcast([P, EXPERTS, DIM])) \
                .then_inc(s.biases_loaded, 16)
            sp.wait_ge(blocks_known, 1)
            load_weights(sp, d, s, 0, 0)
            sp.wait_ge(rows_stored, 48)

        @block.gpsimd
        def _(pool):
            nc.gpsimd.memset(zeros[:, :], 0.0).then_inc(zeros_made, 1)
            nc.gpsimd.memset(earlier[:, :], 1.0).then_inc(made, 1)
            nc.gpsimd.memset(lower[:, :, :], 1.0).then_inc(made, 1)
            nc.gpsimd.memset(ones[:, :], 1.0).then_inc(made, 1)
            pool.wait_ge(made, 3)
            nc.gpsimd.affine_select(out=earlier[:, :], in_=earlier[:, :], compare_op=ALU.is_gt, fill=0.0,
                                    base=0, pattern=[[1, P]], channel_multiplier=-1).then_inc(made, 1)
            nc.gpsimd.affine_select(out=lower[:, :, :], in_=lower[:, :, :], compare_op=ALU.is_gt, fill=0.0,
                                    base=0, pattern=[[1, E], [-1, E]], channel_multiplier=0).then_inc(made, 1)
            nc.gpsimd.iota(fill_levels[:, :], pattern=[[SLOTS, MAX_NB]], base=0, channel_multiplier=0,
                           allow_small_or_imprecise_dtypes=True).then_inc(made, 1)
            nc.gpsimd.iota(block_index[:, :], pattern=[[1, BLOCKS]], base=0, channel_multiplier=0,
                           allow_small_or_imprecise_dtypes=True).then_inc(made, 1)
            nc.gpsimd.iota(tile_starts[:, :], pattern=[[P, SLOT_TILES + 1]], base=0, channel_multiplier=0,
                           allow_small_or_imprecise_dtypes=True).then_inc(made, 1)
            nc.gpsimd.iota(row_index[:, :], pattern=[[1, P]], base=0, channel_multiplier=0,
                           allow_small_or_imprecise_dtypes=True).then_inc(made, 1)
            nc.gpsimd.iota(tile_number[:, :], pattern=[[1, 2 * TT]], base=1, channel_multiplier=0,
                           allow_small_or_imprecise_dtypes=True).then_inc(made, 1)
            nc.gpsimd.iota(partition[:, :], pattern=[[0, 1]], base=0, channel_multiplier=1,
                           allow_small_or_imprecise_dtypes=True).then_inc(made, 1)
            nc.gpsimd.iota(empty_row[:, :], pattern=[[0, 1]], base=2 * TOK + P, channel_multiplier=1,
                           allow_small_or_imprecise_dtypes=True).then_inc(made, 1)

        @block.tensor
        def _(pe):
            pe.wait_ge(made, 12)
            pe.wait_ge(chosen_ready, 1)
            flat = chosen[:, :, :].rearrange("p t e -> p (t e)")
            nc.tensor.matmul(prefix_bank[:, :], earlier[:, :], flat, start=True, stop=True)
            nc.tensor.matmul(total_bank[:, :], ones[:, :], flat, start=True, stop=True).then_inc(counted, 1)
            pe.wait_ge(in_tile_ready, 1)
            for a in range(2 * TT):
                if a % 8 == 0:
                    pe.wait_ge(in_row_ready, a // 8 + 1)
                last = nc.tensor.matmul(slots_bank[:, :, :], in_row[:, a, :], at_tile[:, a, :, :],
                                        start=(a == 0), stop=(a == 2 * TT - 1))
            last.then_inc(slots_found, 1)

        @block.scalar
        def _(act):
            act.wait_ge(shifted, 1)
            nc.scalar.activation(coef[:, :, :], coef[:, :, :], ACT.Exp).then_inc(exped, 1)

        @block.vector
        def _(dve):
            done = [0]

            def then(instruction):
                done[0] += 1
                instruction.then_inc(step, 1)
                dve.wait_ge(step, done[0])

            def over(a, shape):
                axes = "p t e" if len(a.shape) == 3 else "p t"
                return a.rearrange(f"{axes[:-1]}({axes[-1]} a) -> {axes} a", a=1).to_broadcast(shape)

            def across(a, shape):
                if len(a.shape) == 3:
                    return a.rearrange("p t (a e) -> p t a e", a=1).to_broadcast(shape)
                return a.rearrange("p (a e) -> p a e", a=1).to_broadcast(shape)

            tee, te = [P, TT, E, E], [P, TT, E]
            dve.wait_ge(loaded, 16)
            dve.wait_ge(made, 12)
            L = logits[:, :, :]
            then(nc.vector.tensor_tensor(L, logits_bank[:, :].rearrange("p (t e) -> p t e", e=E),
                                         across(rb[:, :], te), ALU.add))
            then(nc.vector.tensor_reduce(top[:, :], L, AX, ALU.max))
            nc.vector.tensor_tensor(coef[:, :, :], L, over(top[:, :], te), ALU.subtract).then_inc(shifted, 1)
            nc.vector.tensor_tensor(before[:, :, :, :], across(L, tee), over(L, tee), ALU.is_gt)
            then(nc.vector.tensor_tensor(same[:, :, :, :], across(L, tee), over(L, tee), ALU.is_equal))
            then(nc.vector.tensor_tensor(same[:, :, :, :], same[:, :, :, :],
                                         lower[:, :, :].rearrange("p (a i) j -> p a i j", a=1).to_broadcast(tee), ALU.mult))
            then(nc.vector.tensor_tensor(before[:, :, :, :], before[:, :, :, :], same[:, :, :, :], ALU.add))
            then(nc.vector.tensor_reduce(place[:, :, :], before[:, :, :, :], AX, ALU.add))
            nc.vector.tensor_scalar(chosen[:, :, :], place[:, :, :], 1.5, None, ALU.is_lt).then_inc(chosen_ready, 1)
            dve.wait_ge(chosen_ready, 1)
            dve.wait_ge(exped, 1)
            then(nc.vector.tensor_tensor(coef[:, :, :], coef[:, :, :], chosen[:, :, :], ALU.mult))
            then(nc.vector.tensor_reduce(total[:, :], coef[:, :, :], AX, ALU.add))
            then(nc.vector.reciprocal(total[:, :], total[:, :]))
            then(nc.vector.tensor_tensor(coef[:, :, :], coef[:, :, :], over(total[:, :], te), ALU.mult))

            dve.wait_ge(counted, 1)
            then(nc.vector.memset(counts[:, 0, :], 0.0))
            for t in range(TT):
                then(nc.vector.tensor_tensor(counts[:, t + 1, :], counts[:, t, :], total_bank[:, t * E:(t + 1) * E],
                                             ALU.add))
            ee = [P, E, MAX_NB]
            then(nc.vector.tensor_tensor(filled[:, :, :], over(counts[:, TT, :], ee), across(fill_levels[:, :], ee),
                                         ALU.is_gt))
            then(nc.vector.tensor_reduce(n_blocks[:, :], filled[:, :, :], AX, ALU.add))
            then(nc.vector.tensor_tensor(starts[:, :, :], lower[:, :, :], across(n_blocks[:, :], [P, E, E]), ALU.mult))
            then(nc.vector.tensor_reduce(start[:, :], starts[:, :, :], AX, ALU.add))
            then(nc.vector.tensor_tensor(ends[:, :], start[:, :], n_blocks[:, :], ALU.add))
            be = [P, BLOCKS, E]
            then(nc.vector.tensor_tensor(passed[:, :, :], over(block_index[:, :], be), across(ends[:, :], be), ALU.is_ge))
            then(nc.vector.tensor_reduce(block_f[:, :], passed[:, :, :], AX, ALU.add))
            nc.vector.tensor_scalar(s.block_expert[:, :], block_f[:, :], float(E - 1), None, ALU.min).then_inc(blocks_known, 1)

            then(nc.vector.tensor_scalar(start[:, :], start[:, :], float(SLOTS), None, ALU.mult))
            then(nc.vector.tensor_tensor(place[:, :, :], counts[:, 0:TT, :], across(start[:, :], te), ALU.add))
            then(nc.vector.tensor_tensor(place[:, :, :], place[:, :, :],
                                         prefix_bank[:, :].rearrange("p (t e) -> p t e", e=E), ALU.add))
            FAR = float(BLOCKS * SLOTS)
            for i, (away, pick) in enumerate(((FAR, ALU.min), (-FAR, ALU.max))):
                then(nc.vector.tensor_scalar(masked[:, :, :], chosen[:, :, :], -away, away, ALU.mult, ALU.add))
                then(nc.vector.tensor_tensor(masked[:, :, :], masked[:, :, :], place[:, :, :], ALU.add))
                slot_i = slot[:, :, i]
                then(nc.vector.tensor_reduce(slot_i, masked[:, :, :], AX, pick))
                then(nc.vector.tensor_tensor(hit[:, :, :], masked[:, :, :], over(slot_i, te), ALU.is_equal))
                then(nc.vector.tensor_tensor(hit[:, :, :], hit[:, :, :], coef[:, :, :], ALU.mult))
                nc.vector.tensor_reduce(s.weight[:, i, :], hit[:, :, :], AX, ALU.add)

            at = [P, 2 * TT, SLOT_TILES + 1]
            slots = slot[:, :, :].rearrange("p t i -> p (t i)")
            then(nc.vector.tensor_tensor(reached[:, :, :], over(slots, at), across(tile_starts[:, :], at), ALU.is_ge))
            nc.vector.tensor_reduce(tile_count[:, :], reached[:, :, :], AX, ALU.add)
            then(nc.vector.tensor_tensor(in_tile[:, :, :], reached[:, :, 0:SLOT_TILES], reached[:, :, 1:SLOT_TILES + 1],
                                         ALU.subtract))
            nc.vector.tensor_scalar(at_tile[:, :, 1, :], in_tile[:, :, :], partition[:, 0:1], None, ALU.mult)
            then(nc.vector.scalar_tensor_tensor(slots, tile_count[:, :], -float(P), slots, ALU.mult, ALU.add))
            nc.vector.tensor_scalar(slots, slots, float(P), None, ALU.add).then_inc(step, 1)
            done[0] += 1
            nc.vector.tensor_tensor(at_tile[:, :, 0, :], in_tile[:, :, :],
                                    over(tile_number[:, :], [P, 2 * TT, SLOT_TILES]), ALU.mult).then_inc(in_tile_ready, 1)
            dve.wait_ge(step, done[0])
            for a in range(0, 2 * TT, 8):
                nc.vector.tensor_tensor(in_row[:, a:a + 8, :], over(slots[:, a:a + 8], [P, 8, P]),
                                        across(row_index[:, :], [P, 8, P]), ALU.is_equal).then_inc(in_row_ready, 1)
            dve.wait_ge(slots_found, 1)
            then(nc.vector.tensor_scalar(empty[:, :], slots_bank[:, 0, :], 0.0, None, ALU.is_equal))
            then(nc.vector.tensor_scalar(read[:, :], slots_bank[:, 0, :], float(P), None, ALU.mult))
            then(nc.vector.tensor_tensor(read[:, :], read[:, :], slots_bank[:, 1, :], ALU.add))
            then(nc.vector.scalar_tensor_tensor(read[:, :], empty[:, :], empty_row[:, 0:1], read[:, :],
                                                ALU.mult, ALU.add))
            nc.vector.tensor_scalar(s.row_in[:, :], read[:, :], -float(P), None, ALU.add)
            then(nc.vector.tensor_tensor(empty[:, :], empty[:, :], tile_starts[:, 0:SLOT_TILES], ALU.mult))
            nc.vector.scalar_tensor_tensor(s.row_out[:, :], read[:, :], -float(P), empty[:, :], ALU.add, ALU.add)


def load_weights(sp, d, s, j, par):
    e = sp.value_load(s.block_expert[0:1, bass.ds(j, 1)], min_val=0, max_val=EXPERTS - 1)
    sp.dma_start(s.w1[par], d.w1_T[bass.ds(e, 1), :, :].rearrange("a (k p) f -> p (a k) f", p=P)) \
        .then_inc(s.w_loaded[par], 16)
    sp.dma_start(s.w2[par], d.w2_T[bass.ds(e, 1), :, :].rearrange("a (k p) n -> p (a k) n", p=P)) \
        .then_inc(s.w_loaded[par], 16)


def experts(nc, d, s):
    with ExitStack() as ctx:
        def sb(name, shape, dt=F32):
            return ctx.enter_context(nc.sbuf_tensor(name, shape, dt))

        def sem(name):
            return ctx.enter_context(nc.semaphore(name))

        QUARTERS = 4
        FQ = KF // QUARTERS
        b1_all, b2_all, w1, w2, hidden = s.b1_all, s.b2_all, s.w1, s.w2, s.hidden
        w1_hi = [sb(f"w1_hi{i}", [P, KD, FF], F32R) for i in range(2)]
        w1_lo = [sb(f"w1_lo{i}", [P, KD, FF], F32R) for i in range(2)]
        w2_hi = [sb(f"w2_hi{i}", [P, KF, DIM], F32R) for i in range(2)]
        w2_lo = [sb(f"w2_lo{i}", [P, KF, DIM], F32R) for i in range(2)]
        b1 = [sb(f"b1_{i}", [P, KF]) for i in range(2)]
        rows = [sb(f"rows{i}", [P, ST, DIM]) for i in range(2)]
        x_hi = [sb(f"x_hi{i}", [P, KD, SLOTS], F32R) for i in range(2)]
        x_lo = [sb(f"x_lo{i}", [P, KD, SLOTS], F32R) for i in range(2)]
        h_hi = sb("h_hi", [P, KF, SLOTS], F32R)
        h_lo = sb("h_lo", [P, KF, SLOTS], F32R)
        y = [sb(f"y_out{i}", [P, ST, DIM]) for i in range(2)]
        up = [ctx.enter_context(nc.psum_tensor(f"up{i}", [P, BANK], F32)) for i in range(QUARTERS)]
        turned = ctx.enter_context(nc.psum_tensor("turned", [P, BANK], F32))
        down = [ctx.enter_context(nc.psum_tensor(f"down{i}", [P, BANK], F32)) for i in range(ST)]
        rows_in = [sb(f"rows_in{i}", [P, ST], U32) for i in range(2)]
        rows_out = [sb(f"rows_out{i}", [P, ST], U32) for i in range(2)]
        rows_in_chosen = sem("rows_in_chosen")
        biases_loaded, w_loaded = s.biases_loaded, s.w_loaded
        rows_loaded = [sem(f"rows_loaded{i}") for i in range(2)]
        y_stored = [sem(f"y_stored{i}") for i in range(2)]
        w1_hi_done, w1_split, w2_hi_done, w2_split = (
            sem("w1_hi_done"), sem("w1_split"), sem("w2_hi_done"), sem("w2_split"))
        b1_chosen = sem("b1_chosen")
        rows_turned, x_hi_done, x_split = sem("rows_turned"), sem("x_hi_done"), sem("x_split")
        up_done, gelu_done, h_hi_done, h_split = sem("up_done"), sem("gelu_done"), sem("h_hi_done"), sem("h_split")
        down_done, y_done = sem("down_done"), sem("y_done2")
        block = ctx.enter_context(nc.Block())

        def each_block(engine, body):
            pairs = (BLOCKS - 5) // 2
            body(0, 0, True)
            body(1, 1, True)
            with engine.Fori(0, pairs) as i:
                body(i * 2 + 2, 0, True)
                body(i * 2 + 3, 1, True)
            for j in range(2 * pairs + 2, BLOCKS):
                body(j, j % 2, j + 1 < BLOCKS)

        @block.sync
        def _(sp):
            def load(j, par, more):
                if isinstance(j, int) and j == 0:
                    return
                at_least(sp, w1_split, j - 1)
                at_least(sp, w2_split, j - 1)
                load_weights(sp, d, s, j, par)

            each_block(sp, load)

        def is_block(j):
            return not isinstance(j, int) or j < BLOCKS

        @block.gpsimd
        def _(pool):
            def gather(j, par):
                for t in range(ST):
                    nc.gpsimd.indirect_dma_start(rows[par][:, t, :], None, d.rows,
                                                 bass.IndirectOffsetOnAxis(rows_in[par][:, t:t + 1], 0)) \
                        .then_inc(rows_loaded[par], 16)

            def store(j, par):
                for t in range(ST):
                    nc.gpsimd.indirect_dma_start(d.results, bass.IndirectOffsetOnAxis(rows_out[par][:, t:t + 1], 0),
                                                 y[par][:, t, :], None).then_inc(y_stored[par], 16)

            def split(j, par):
                pool.wait_ge(w1_hi_done, j + 1)
                nc.gpsimd.tensor_tensor(w1_lo[par][:, :, :], w1[par], w1_hi[par][:, :, :].bitcast(F32),
                                        ALU.subtract).then_inc(w1_split, 1)

            def beside(j, par, more):
                if is_block(j + 2):
                    pool.wait_ge(rows_in_chosen, j + 3)
                    pool.wait_ge(rows_turned, j + 1)
                at_least(pool, y_done, j * ST)
                if more:
                    split(j + 1, 1 - par)
                if is_block(j + 2):
                    gather(j + 2, par)
                if not isinstance(j, int) or j > 0:
                    store(j - 1, 1 - par)

            pool.wait_ge(rows_in_chosen, 2)
            gather(0, 0)
            gather(1, 1)
            split(0, 0)
            each_block(pool, beside)
            pool.wait_ge(y_done, BLOCKS * ST)
            store(BLOCKS - 1, (BLOCKS - 1) % 2)
            for par in range(2):
                pool.wait_ge(y_stored[par], 16 * ST * ((BLOCKS + 1 - par) // 2))

        @block.vector
        def _(dve):
            def prepare(j, par, part):
                if part == 0:
                    dve.wait_ge(w_loaded[par], (j - par) * 16 + 32)
                    at_least(dve, down_done, (j - 1) * ST)
                    nc.vector.tensor_copy(w1_hi[par][:, :, :], w1[par]).then_inc(w1_hi_done, 1)
                elif part == 1:
                    nc.vector.tensor_copy(w2_hi[par][:, :, :], w2[par]).then_inc(w2_hi_done, 1)
                    e = dve.value_load(s.block_expert[0:1, bass.ds(j, 1)], min_val=0, max_val=EXPERTS - 1)
                    nc.vector.tensor_copy(b1[par][:, :], b1_all[:, bass.ds(e, 1), :].rearrange("p a k -> p (a k)")) \
                        .then_inc(b1_chosen, 1)
                elif part == 2:
                    dve.wait_ge(w2_hi_done, j + 1)
                    nc.vector.tensor_tensor(w2_lo[par][:, :, :], w2[par], w2_hi[par][:, :, :].bitcast(F32),
                                            ALU.subtract).then_inc(w2_split, 1)
                else:
                    dve.wait_ge(x_hi_done, j + 1)
                    nc.vector.tensor_tensor(x_lo[par][:, :, :], turned[:, :].rearrange("p (k n) -> p k n", k=KD),
                                            x_hi[par][:, :, :].bitcast(F32), ALU.subtract).then_inc(x_split, 1)

            def choose_rows_in(j, par):
                nc.vector.tensor_copy(rows_in[par][:, :], s.row_in[:, bass.ds(j * ST, ST)]).then_inc(rows_in_chosen, 1)

            def compute(j, par, more):
                if is_block(j + 2):
                    choose_rows_in(j + 2, par)
                for q in range(QUARTERS):
                    dve.wait_ge(gelu_done, (j * QUARTERS + q + 1) * FQ)
                    part = slice(q * FQ, (q + 1) * FQ)
                    nc.vector.tensor_copy(h_hi[:, part, :], hidden[:, part, :]).then_inc(h_hi_done, 1)
                    dve.wait_ge(h_hi_done, j * QUARTERS + q + 1)
                    nc.vector.tensor_tensor(h_lo[:, part, :], hidden[:, part, :], h_hi[:, part, :].bitcast(F32),
                                            ALU.subtract).then_inc(h_split, 1)
                    if more:
                        prepare(j + 1, 1 - par, q)
                e = dve.value_load(s.block_expert[0:1, bass.ds(j, 1)], min_val=0, max_val=EXPERTS - 1)
                at_least(dve, y_stored[par], (j - par) // 2 * 16 * ST if isinstance(j, int) else (j - par) * (8 * ST))
                nc.vector.tensor_copy(rows_out[par][:, :], s.row_out[:, bass.ds(j * ST, ST)])
                for t in range(ST):
                    dve.wait_ge(down_done, j * ST + t + 1)
                    nc.vector.tensor_tensor(y[par][:, t:t + 1, :], down[t][:, 0:DIM].rearrange("p (a n) -> p a n", a=1),
                                            b2_all[:, bass.ds(e, 1), :], ALU.add).then_inc(y_done, 1)

            choose_rows_in(0, 0)
            choose_rows_in(1, 1)
            dve.wait_ge(biases_loaded, 32)
            for part in range(4):
                prepare(0, 0, part)
            each_block(dve, compute)

        @block.scalar
        def _(act):
            def rows_hi(j, par):
                act.wait_ge(rows_turned, j + 1)
                nc.scalar.copy(x_hi[par][:, :, :], turned[:, :].rearrange("p (k n) -> p k n", k=KD)).then_inc(x_hi_done, 1)

            def compute(j, par, more):
                act.wait_ge(b1_chosen, j + 1)
                for f in range(KF):
                    q, i = divmod(f, FQ)
                    if i == 0:
                        act.wait_ge(up_done, j * QUARTERS + q + 1)
                    nc.scalar.activation(hidden[:, f, :], up[q][:, i * SLOTS:(i + 1) * SLOTS], ACT.Gelu,
                                         bias=b1[par][:, f:f + 1]).then_inc(gelu_done, 1)
                if more:
                    rows_hi(j + 1, 1 - par)

            rows_hi(0, 0)
            each_block(act, compute)

        @block.tensor
        def _(pe):
            def turn(j, par):
                pe.wait_ge(rows_loaded[par], (j - par) * (8 * ST) + 16 * ST)
                at_least(pe, x_split, j)
                for k in range(KD):
                    for t in range(ST):
                        last = nc.tensor.transpose(turned[:, (k * ST + t) * P:(k * ST + t + 1) * P],
                                                   rows[par][:, t, k * P:(k + 1) * P], s.ident[:, :])
                last.then_inc(rows_turned, 1)

            def compute(j, par, more):
                pe.wait_ge(w1_split, j + 1)
                pe.wait_ge(x_split, j + 1)
                for f in range(KF):
                    q, i = divmod(f, FQ)
                    if i == 0:
                        at_least(pe, gelu_done, (j - 1) * KF + (q + 1) * FQ)
                    cols = slice(f * P, (f + 1) * P)
                    parts = [(w, x, k) for k in range(KD)
                             for w, x in ((w1_hi, x_hi), (w1_hi, x_lo), (w1_lo, x_hi))]
                    for n, (w, x, k) in enumerate(parts):
                        last = nc.tensor.matmul(up[q][:, i * SLOTS:(i + 1) * SLOTS], w[par][:, k, cols], x[par][:, k, :],
                                                start=(n == 0), stop=(n == len(parts) - 1))
                    if i == FQ - 1:
                        last.then_inc(up_done, 1)
                if more:
                    turn(j + 1, 1 - par)
                pe.wait_ge(w2_split, j + 1)
                at_least(pe, y_done, j * ST)
                for f in range(KF):
                    q, i = divmod(f, FQ)
                    if i == 0:
                        pe.wait_ge(h_split, j * QUARTERS + q + 1)
                    for t in range(ST):
                        for n, (h, w) in enumerate(((h_hi, w2_hi), (h_hi, w2_lo), (h_lo, w2_hi))):
                            last = nc.tensor.matmul(down[t][:, 0:DIM], h[:, f, t * P:(t + 1) * P], w[par][:, f, :],
                                                    start=(f == 0 and n == 0), stop=(f == KF - 1 and n == 2))
                        if f == KF - 1:
                            last.then_inc(down_done, 1)

            turn(0, 0)
            each_block(pe, compute)


def combine(nc, d, s):
    with ExitStack() as ctx:
        fetched = [ctx.enter_context(nc.sbuf_tensor(f"fetched{g}", [P, GT, 2, DIM], F32)) for g in range(LN_GROUPS)]
        fetched_sem = [ctx.enter_context(nc.semaphore(f"fetched_sem{g}")) for g in range(LN_GROUPS)]
        added = ctx.enter_context(nc.semaphore("c_added"))
        stored = ctx.enter_context(nc.semaphore("stored"))
        block = ctx.enter_context(nc.Block())
        results = d.results[0:2 * TOK, :].rearrange("(t p) n -> p t n", p=P)

        @block.sync
        def _(sp):
            for g in range(LN_GROUPS):
                sp.dma_start(fetched[g][:, :, :, :].rearrange("p t i n -> p (t i) n"),
                             results[:, 2 * g * GT:2 * (g + 1) * GT, :]) \
                    .then_inc(fetched_sem[g], 16)
            for g in range(LN_GROUPS):
                sp.wait_ge(added, 2 * GT * (g + 1))
                sp.dma_start(d.out[g * BANK:(g + 1) * BANK, :].rearrange("(t p) n -> p t n", p=P),
                             s.x_tok[:, g * GT:(g + 1) * GT, :]).then_inc(stored, 16)
            sp.wait_ge(stored, 16 * LN_GROUPS)

        @block.vector
        def _(dve):
            for g in range(LN_GROUPS):
                dve.wait_ge(fetched_sem[g], 16)
                for i in range(2):
                    if i > 0:
                        dve.wait_ge(added, 2 * GT * g + GT)
                    for t in range(GT):
                        x = s.x_tok[:, g * GT + t, :]
                        nc.vector.scalar_tensor_tensor(x, fetched[g][:, t, i, :],
                                                       s.weight[:, i, g * GT + t:g * GT + t + 1], x,
                                                       ALU.mult, ALU.add).then_inc(added, 1)


def perceiver(nc, d):
    with ExitStack() as ctx:
        def sb(name, shape, dt=F32):
            return ctx.enter_context(nc.sbuf_tensor(name, shape, dt))

        x_tok, ident = sb("x_tok", [P, TT, DIM]), sb("ident", [P, P])
        with ExitStack() as inner:
            s = attention_memory(nc, inner)
            s.x_tok, s.ident = x_tok, ident
            load_constants(nc, d, s)
            with ExitStack() as first:
                xn_T = first.enter_context(nc.sbuf_tensor("xn_T1", [P, KD, TOK], F32))
                xn = first.enter_context(nc.sbuf_tensor("xn1", [P, TT, DIM], F32))
                normalize_and_transpose(nc, "ln1", x_tok, xn, xn_T, ident)
                project_queries(nc, d, s, xn_T)
            attention(nc, d, s)
        s = Names()
        s.x_tok, s.ident = x_tok, ident
        xn = sb("xn", [P, TT, DIM])
        s.weight = sb("weight", [P, 2, TT])
        s.row_in, s.row_out = sb("row_in", [P, SLOT_TILES], U32), sb("row_out", [P, SLOT_TILES], U32)
        s.block_expert = sb("block_expert", [P, BLOCKS], U32)
        with ExitStack() as inner:
            s.a, s.dp = inner.enter_context(nc.sbuf_tensor("a", [P, KI, STATE], F32)), \
                inner.enter_context(nc.sbuf_tensor("dp", [P, KI], F32))
            ssm_weights(nc, inner, s)
            xn_T = inner.enter_context(nc.sbuf_tensor("xn_T", [P, KD, TOK], F32))
            attention_output(nc, d, s, xn, xn_T)
            s.xs = inner.enter_context(nc.sbuf_tensor("xs", [P, KI, TOK], F32))
            with ExitStack() as scanned:
                s.delta = scanned.enter_context(nc.sbuf_tensor("delta", [P, KI, TOK], F32))
                s.dtx = scanned.enter_context(nc.sbuf_tensor("dtx", [P, KI, TOK], F32))
                ssm_projections(nc, d, s, xn_T)
                s.y = s.xs
                s.da = [xn_T[:, k // 2, (k % 2) * HALF:(k % 2 + 1) * HALF] for k in range(KI)]
                s.dbx = [xn[:, 4 * k:4 * k + 4, :].rearrange("p t n -> p (t n)") for k in range(KI)]
                s.wout = s.win[:, 0, :].rearrange("p (k n) -> p k n", k=KI)
                s.bout = s.win[:, 1, 0:DIM]
                ssm_scan(nc, d, s)
            logits_bank = inner.enter_context(nc.psum_tensor("logits_bank", [P, TT * EXPERTS], F32))
            ssm_output(nc, d, s, xn, xn_T, logits_bank)
            s.w1 = [s.xs[:, i, :].rearrange("p (k f) -> p k f", k=KD) for i in range(2)]
            s.w2 = [s.xs[:, 2 + i, :].rearrange("p (k n) -> p k n", k=KF) for i in range(2)]
            s.hidden = xn_T[:, 0, :].rearrange("p (f n) -> p f n", f=KF)
            s.b1_all = inner.enter_context(nc.sbuf_tensor("b1_all", [P, EXPERTS, KF], F32))
            s.b2_all = inner.enter_context(nc.sbuf_tensor("b2_all", [P, EXPERTS, DIM], F32))
            s.biases_loaded = inner.enter_context(nc.semaphore("biases_loaded"))
            s.w_loaded = [inner.enter_context(nc.semaphore(f"w_loaded{i}")) for i in range(2)]
            route(nc, d, s, xn, logits_bank)
            experts(nc, d, s)
        combine(nc, d, s)


def laid_out(inputs):
    import numpy as np
    names = dict(W_Q="xattn_W_Q", b_Q="xattn_b_Q", W_K="xattn_W_K", b_K="xattn_b_K", W_V="xattn_W_V",
                 b_V="xattn_b_V", W_O="xattn_W_O", b_O="xattn_b_O", Win="attn_Win", bin="attn_bin", Wx="attn_Wx",
                 bx="attn_bx", Wdt="attn_Wdt", bdt="attn_bdt", A_log="attn_A_log", Dp="attn_Dp",
                 Wout="attn_Wout", bout="attn_bout", router_b="ffn_router_b", b2="ffn_b2")
    arrays = {k: np.asarray(inputs["L0_" + v]) for k, v in names.items()}
    arrays["x"] = np.asarray(inputs["x"]).reshape(TOK, DIM)
    arrays["ctx_T"] = np.asarray(inputs["ctx_1024"]).transpose(0, 2, 1)
    arrays["router_w_T"] = np.asarray(inputs["L0_ffn_router_w"]).T
    arrays["w1_T"] = np.asarray(inputs["L0_ffn_w1"]).transpose(0, 2, 1)
    arrays["w2_T"] = np.asarray(inputs["L0_ffn_w2"]).transpose(0, 2, 1)
    arrays["b1_T"] = np.asarray(inputs["L0_ffn_b1"]).reshape(EXPERTS, KF, P).transpose(0, 2, 1)
    return {k: np.ascontiguousarray(v) for k, v in arrays.items()}


def build(nc, shapes):
    def array(name):
        return nc.dram_tensor(f"in_{name}", shapes[name], F32, kind="ExternalInput").ap()

    d = Names()
    d.x, d.ctx_T = array("x"), array("ctx_T")
    d.W_Q, d.b_Q, d.W_K, d.b_K = array("W_Q"), array("b_Q"), array("W_K"), array("b_K")
    d.W_V, d.b_V, d.W_O, d.b_O = array("W_V"), array("b_V"), array("W_O"), array("b_O")
    d.Win, d.bin, d.Wx, d.bx = array("Win"), array("bin"), array("Wx"), array("bx")
    d.Wdt, d.bdt, d.A_log, d.Dp = array("Wdt"), array("bdt"), array("A_log"), array("Dp")
    d.Wout, d.bout = array("Wout"), array("bout")
    d.router_w_T, d.router_b = array("router_w_T"), array("router_b")
    d.w1_T, d.b1_T, d.w2_T, d.b2 = array("w1_T"), array("b1_T"), array("w2_T"), array("b2")
    d.mixed = nc.dram_tensor("scratch_mixed", (BATCH, P, DIM), F32).ap()
    d.z = nc.dram_tensor("scratch_z", (KI, P, TOK), F32).ap()
    d.bc = nc.dram_tensor("scratch_bc", (2, STATE, TOK), F32).ap()
    d.rows = nc.dram_tensor("scratch_rows", (2 * TOK + P, DIM), F32).ap()
    d.results = nc.dram_tensor("scratch_results", (2 * TOK + BLOCKS * SLOTS, DIM), F32).ap()
    d.out = nc.dram_tensor("out", (TOK, DIM), F32, kind="ExternalOutput").ap()
    perceiver(nc, d)


def kernel(**inputs):
    import concourse.bacc as bacc
    from concourse.bass_utils import run_bass_kernel_spmd

    nc = bacc.Bacc("TRN2", target_bir_lowering=False, num_devices=1)
    arrays = laid_out(inputs)
    build(nc, {k: a.shape for k, a in arrays.items()})
    r = run_bass_kernel_spmd(nc, [{f"in_{k}": a for k, a in arrays.items()}], core_ids=[0])
    return r.results[0]["out"].reshape(BATCH, LATENTS, DIM)
```
